# Optimizing a Trainium2 kernel written in Bass

```python
import numpy as np
import jax
import jax.numpy as jnp

def _softmax(x, axis=-1):
    return jax.nn.softmax(x, axis=axis)
def _gelu(x):
    return jax.nn.gelu(x, approximate=True)
def _silu(x):
    return jax.nn.silu(x)
def _sigmoid(x):
    return jax.nn.sigmoid(x)
def _layernorm(x, axis=-1, eps=1e-5):
    m = jnp.mean(x, axis=axis, keepdims=True)
    v = jnp.var(x, axis=axis, keepdims=True)
    return (x - m) / jnp.sqrt(v + eps)
def _scatter_add(tgt, idx, src, axis=0):
    return tgt.at[idx].add(src)
def _segment_sum(src, seg, n):
    return jax.ops.segment_sum(src, seg, n)

kernel_name = 'mk_conv_preact_d4_conv_nchw64_c6dc6f'

def setup_inputs(seed: int = 0):
    np.random.seed(seed)
    _w = jnp.asarray
    def _rec_inputs():
        import jax
        import jax.numpy as jnp
        _gk = jax.random.key(seed)
        x = 7.22e-05 + 1 * jax.random.normal(jax.random.fold_in(_gk, 1), (8, 64, 128, 128), jnp.float32)
        return x
    x = _rec_inputs()
    def _L0_conv_setup():
        import jax, jax.numpy as jnp
        import numpy as np
        MAX_ANGLES = 6
        SCALES = 2
        BN_EPS = 1e-05

        def _gauss(k):
            xs = np.arange(k, dtype=np.float32) - k // 2
            w = np.exp(-xs ** 2 / (2.0 * (k / 4.0) ** 2)).astype(np.float32)
            return jnp.asarray((w / w.sum()).reshape(1, 1, k))

        def _grid_sample(img, grid):
            N, C, H, W = img.shape
            ix = (grid[..., 0] + 1.0) * 0.5 * (W - 1)
            iy = (grid[..., 1] + 1.0) * 0.5 * (H - 1)
            x0 = jnp.floor(ix)
            y0 = jnp.floor(iy)
            wx = ix - x0
            wy = iy - y0

            def gather(xi, yi):
                valid = (xi >= 0) & (xi <= W - 1) & (yi >= 0) & (yi <= H - 1)
                xc = jnp.clip(xi, 0, W - 1).astype(jnp.int32)
                yc = jnp.clip(yi, 0, H - 1).astype(jnp.int32)
                v = jax.vmap(lambda im, yy, xx: im[:, yy, xx])(img, yc, xc)
                return v * valid[:, None, :, :].astype(img.dtype)
            v00 = gather(x0, y0)
            v01 = gather(x0 + 1, y0)
            v10 = gather(x0, y0 + 1)
            v11 = gather(x0 + 1, y0 + 1)
            return v00 * ((1 - wx) * (1 - wy))[:, None] + v01 * (wx * (1 - wy))[:, None] + v10 * ((1 - wx) * wy)[:, None] + v11 * (wx * wy)[:, None]

        def _interp1d(x, Lout):
            Lin = x.shape[-1]
            real = jnp.clip((jnp.arange(Lout, dtype=jnp.float32) + 0.5) * (Lin / Lout) - 0.5, 0.0, Lin - 1.0)
            i0 = jnp.floor(real).astype(jnp.int32)
            i1 = jnp.minimum(i0 + 1, Lin - 1)
            w = real - i0
            return x[..., i0] * (1.0 - w) + x[..., i1] * w

        def _interp_last_ac(x, Lout):
            Lin = x.shape[-1]
            if Lin == Lout:
                return x
            pos = jnp.arange(Lout, dtype=jnp.float32) * ((Lin - 1) / (Lout - 1))
            i0 = jnp.floor(pos).astype(jnp.int32)
            i1 = jnp.minimum(i0 + 1, Lin - 1)
            w = pos - i0
            return x[..., i0] * (1.0 - w) + x[..., i1] * w

        def _avgpool1(x):
            L = x.shape[-1]
            return x[..., :L // 2 * 2].reshape(x.shape[:-1] + (L // 2, 2)).mean(-1)

        def _conv1(sig, w):
            k = w.shape[-1]
            return jax.lax.conv_general_dilated(sig, w, (1,), [(k // 2, k // 2)], dimension_numbers=('NCH', 'OIH', 'NCH'))
        key = jax.random.key(seed)
        ks = jax.random.split(key, 8)
        B, C, H, W = (8, 64, 128, 128)
        return {'x': jax.random.normal(ks[0], (B, C, H, W), jnp.float32), 'lin1_w': jax.random.normal(ks[1], (32, C * 16), jnp.float32) * 0.02, 'lin1_b': jnp.zeros((32,), jnp.float32), 'lin2_w': jax.random.normal(ks[2], (MAX_ANGLES, 32), jnp.float32) * 0.02, 'lin2_b': jnp.zeros((MAX_ANGLES,), jnp.float32), 'wf0': _gauss(3), 'wf1': _gauss(5), 'fuse_w': jax.random.normal(ks[3], (C, C * SCALES), jnp.float32) * 0.05, 'fuse_b': jax.random.normal(ks[4], (C,), jnp.float32) * 0.05, 'bn_gamma': jnp.ones((C,), jnp.float32), 'bn_beta': jnp.zeros((C,), jnp.float32), 'bn_mean': jnp.zeros((C,), jnp.float32), 'bn_var': jnp.ones((C,), jnp.float32)}
    _L0_conv_all = _L0_conv_setup()
    _L0_conv_in = {k: v for k, v in _L0_conv_all.items() if k in ('lin1_w', 'lin1_b', 'lin2_w', 'lin2_b', 'wf0', 'wf1', 'fuse_w', 'fuse_b', 'bn_gamma', 'bn_beta', 'bn_mean', 'bn_var', )}
    del _L0_conv_all

    def _L1_conv_setup():
        import jax, jax.numpy as jnp
        import numpy as np
        C = 64
        K = 3
        B, H, W = (8, 128, 128)

        def conv2d(x, w, b, pad, groups=1):
            y = jax.lax.conv_general_dilated(x, w, window_strides=(1, 1), padding=[(pad, pad), (pad, pad)], feature_group_count=groups, dimension_numbers=('NCHW', 'OIHW', 'NCHW'))
            return y + b[None, :, None, None]
        key = jax.random.key(seed)
        ks = jax.random.split(key, 11)
        s3 = 1.0 / np.sqrt(C * 9)
        inp = {'x': jax.random.normal(ks[0], (B, C, H, W), jnp.float32), 'w0': jax.random.normal(ks[1], (C, C, 3, 3), jnp.float32) * s3, 'b0': jax.random.normal(ks[2], (C,), jnp.float32) * 0.01, 'w1': jax.random.normal(ks[3], (C, 1, 3, 3), jnp.float32) * (1.0 / 3.0), 'b1': jax.random.normal(ks[4], (C,), jnp.float32) * 0.01, 'w2': jax.random.normal(ks[5], (1, 1, K), jnp.float32) * (1.0 / np.sqrt(K)), 'b2': jax.random.normal(ks[6], (1,), jnp.float32) * 0.01, 'w3': jax.random.normal(ks[7], (C * K * K, C, 1, 1), jnp.float32) * (1.0 / np.sqrt(C)), 'b3': jax.random.normal(ks[8], (C * K * K,), jnp.float32) * 0.01, 'wf': jax.random.normal(ks[9], (C, C, 3, 3), jnp.float32) * s3, 'bf': jax.random.normal(ks[10], (C,), jnp.float32) * 0.01}
        return inp
    _L1_conv_all = _L1_conv_setup()
    _L1_conv_in = {k: v for k, v in _L1_conv_all.items() if k in ('w0', 'b0', 'w1', 'b1', 'w2', 'b2', 'w3', 'b3', 'wf', 'bf', )}
    del _L1_conv_all

    def _L2_conv_setup():
        import jax, jax.numpy as jnp
        from jax import lax
        import numpy as np
        C = 64
        K = 3
        N = 2
        H = 256
        W = 256
        DOWN = 4

        def _conv(x, w, b):
            y = lax.conv_general_dilated(x, w, (1, 1), 'SAME', dimension_numbers=('NCHW', 'OIHW', 'NCHW'))
            return y + b[None, :, None, None]

        def _resblock(x, w1, b1, w2, b2):
            out = jax.nn.leaky_relu(_conv(x, w1, b1), 0.1)
            return _conv(out, w2, b2) + x

        def _block(x, ws1, bs1, ws2, bs2):
            for i in range(ws1.shape[0]):
                x = _resblock(x, ws1[i], bs1[i], ws2[i], bs2[i])
            return x

        def _avgpool(x, k):
            n, c, h, w = x.shape
            return x.reshape(n, c, h // k, k, w // k, k).mean(axis=(3, 5))

        def _maxpool(x, k):
            n, c, h, w = x.shape
            return x.reshape(n, c, h // k, k, w // k, k).max(axis=(3, 5))

        def _dyn_conv(x, wt, k):
            n, c, h, w = x.shape
            pad = (k - 1) // 2
            xp = jnp.pad(x, ((0, 0), (0, 0), (pad, pad), (pad, pad)), mode='edge')
            wr = wt.reshape(n, c, k * k, h, w)
            out = jnp.zeros_like(x)
            for dh in range(k):
                for dw in range(k):
                    out = out + xp[:, :, dh:dh + h, dw:dw + w] * wr[:, :, dh * k + dw]
            return out
        key = jax.random.key(seed)
        ks = jax.random.split(key, 11)
        s = 0.05
        return {'x': jax.random.normal(ks[0], (N, C, H, W), jnp.float32), 'blk1_w1': jax.random.normal(ks[1], (3, C, C, K, K), jnp.float32) * s, 'blk1_b1': jnp.zeros((3, C), jnp.float32), 'blk1_w2': jax.random.normal(ks[2], (3, C, C, K, K), jnp.float32) * s, 'blk1_b2': jnp.zeros((3, C), jnp.float32), 'blk2_w1': jax.random.normal(ks[3], (3, C, C, K, K), jnp.float32) * s, 'blk2_b1': jnp.zeros((3, C), jnp.float32), 'blk2_w2': jax.random.normal(ks[4], (3, C, C, K, K), jnp.float32) * s, 'blk2_b2': jnp.zeros((3, C), jnp.float32), 'tok_w': jax.random.normal(ks[5], (K * K * C, C, 1, 1), jnp.float32) * s, 'tok_b': jnp.zeros((K * K * C,), jnp.float32)}
    _L2_conv_all = _L2_conv_setup()
    _L2_conv_in = {k: v for k, v in _L2_conv_all.items() if k in ('blk1_w1', 'blk1_b1', 'blk1_w2', 'blk1_b2', 'blk2_w1', 'blk2_b1', 'blk2_w2', 'blk2_b2', 'tok_w', 'tok_b', )}
    del _L2_conv_all

    def _L3_conv_setup():
        import jax, jax.numpy as jnp
        import numpy as np
        B, CIN, COUT, S1, S2, M1, M2 = (16, 64, 64, 128, 128, 16, 16)

        def _cas(L, dtype):
            k = jnp.arange(L, dtype=dtype)
            ang = 2.0 * jnp.pi / L * (k[:, None] * k[None, :])
            return jnp.cos(ang) + jnp.sin(ang)

        def dht2(x):
            M, N = (x.shape[-2], x.shape[-1])
            cas_row = _cas(M, x.dtype)
            cas_col = _cas(N, x.dtype)
            y = jnp.einsum('bimn,gn->bimg', x, cas_col)
            return jnp.einsum('mf,bimn->bifn', cas_row, y)

        def idht2(x):
            return dht2(x) / (x.shape[-2] * x.shape[-1])

        def _neg_freq(a):
            return jnp.roll(jnp.flip(a, axis=(-2, -1)), shift=(1, 1), axis=(-2, -1))

        def compl_mul2d(x1, x2):
            x1n = _neg_freq(x1)
            x2n = _neg_freq(x2)
            e = lambda a, b: jnp.einsum('bixy,ioxy->boxy', a, b)
            return 0.5 * (e(x1, x2) - e(x1n, x2n) + e(x1, x2n) + e(x1n, x2))
        key = jax.random.key(seed)
        k1, k2, k3 = jax.random.split(key, 3)
        scale = 1.0 / (CIN * COUT)
        x = jax.random.normal(k1, (B, CIN, S1, S2), dtype=jnp.float32)
        weights1 = scale * jax.random.uniform(k2, (CIN, COUT, M1, M2), dtype=jnp.float32)
        weights2 = scale * jax.random.uniform(k3, (CIN, COUT, M1, M2), dtype=jnp.float32)
        return {'x': x, 'weights1': weights1, 'weights2': weights2}
    _L3_conv_all = _L3_conv_setup()
    _L3_conv_in = {k: v for k, v in _L3_conv_all.items() if k in ('weights1', 'weights2', )}
    del _L3_conv_all

    return {
        "x": x,
        "L0_conv_lin1_w": _L0_conv_in["lin1_w"],
        "L0_conv_lin1_b": _L0_conv_in["lin1_b"],
        "L0_conv_lin2_w": _L0_conv_in["lin2_w"],
        "L0_conv_lin2_b": _L0_conv_in["lin2_b"],
        "L0_conv_wf0": _L0_conv_in["wf0"],
        "L0_conv_wf1": _L0_conv_in["wf1"],
        "L0_conv_fuse_w": _L0_conv_in["fuse_w"],
        "L0_conv_fuse_b": _L0_conv_in["fuse_b"],
        "L0_conv_bn_gamma": _L0_conv_in["bn_gamma"],
        "L0_conv_bn_beta": _L0_conv_in["bn_beta"],
        "L0_conv_bn_mean": _L0_conv_in["bn_mean"],
        "L0_conv_bn_var": _L0_conv_in["bn_var"],
        "L1_conv_w0": _L1_conv_in["w0"],
        "L1_conv_b0": _L1_conv_in["b0"],
        "L1_conv_w1": _L1_conv_in["w1"],
        "L1_conv_b1": _L1_conv_in["b1"],
        "L1_conv_w2": _L1_conv_in["w2"],
        "L1_conv_b2": _L1_conv_in["b2"],
        "L1_conv_w3": _L1_conv_in["w3"],
        "L1_conv_b3": _L1_conv_in["b3"],
        "L1_conv_wf": _L1_conv_in["wf"],
        "L1_conv_bf": _L1_conv_in["bf"],
        "L2_conv_blk1_w1": _L2_conv_in["blk1_w1"],
        "L2_conv_blk1_b1": _L2_conv_in["blk1_b1"],
        "L2_conv_blk1_w2": _L2_conv_in["blk1_w2"],
        "L2_conv_blk1_b2": _L2_conv_in["blk1_b2"],
        "L2_conv_blk2_w1": _L2_conv_in["blk2_w1"],
        "L2_conv_blk2_b1": _L2_conv_in["blk2_b1"],
        "L2_conv_blk2_w2": _L2_conv_in["blk2_w2"],
        "L2_conv_blk2_b2": _L2_conv_in["blk2_b2"],
        "L2_conv_tok_w": _L2_conv_in["tok_w"],
        "L2_conv_tok_b": _L2_conv_in["tok_b"],
        "L3_conv_weights1": _L3_conv_in["weights1"],
        "L3_conv_weights2": _L3_conv_in["weights2"],
    }

def reference(x, L0_conv_lin1_w, L0_conv_lin1_b, L0_conv_lin2_w, L0_conv_lin2_b, L0_conv_wf0, L0_conv_wf1, L0_conv_fuse_w, L0_conv_fuse_b, L0_conv_bn_gamma, L0_conv_bn_beta, L0_conv_bn_mean, L0_conv_bn_var, L1_conv_w0, L1_conv_b0, L1_conv_w1, L1_conv_b1, L1_conv_w2, L1_conv_b2, L1_conv_w3, L1_conv_b3, L1_conv_wf, L1_conv_bf, L2_conv_blk1_w1, L2_conv_blk1_b1, L2_conv_blk1_w2, L2_conv_blk1_b2, L2_conv_blk2_w1, L2_conv_blk2_b1, L2_conv_blk2_w2, L2_conv_blk2_b2, L2_conv_tok_w, L2_conv_tok_b, L3_conv_weights1, L3_conv_weights2):
    import jax
    import jax.numpy as jnp
    def _L0_conv_ref(x, lin1_w, lin1_b, lin2_w, lin2_b, wf0, wf1, fuse_w, fuse_b, bn_gamma, bn_beta, bn_mean, bn_var):
        import jax, jax.numpy as jnp
        import numpy as np
        MAX_ANGLES = 6
        SCALES = 2
        BN_EPS = 1e-05

        def _gauss(k):
            xs = np.arange(k, dtype=np.float32) - k // 2
            w = np.exp(-xs ** 2 / (2.0 * (k / 4.0) ** 2)).astype(np.float32)
            return jnp.asarray((w / w.sum()).reshape(1, 1, k))

        def _grid_sample(img, grid):
            N, C, H, W = img.shape
            ix = (grid[..., 0] + 1.0) * 0.5 * (W - 1)
            iy = (grid[..., 1] + 1.0) * 0.5 * (H - 1)
            x0 = jnp.floor(ix)
            y0 = jnp.floor(iy)
            wx = ix - x0
            wy = iy - y0

            def gather(xi, yi):
                valid = (xi >= 0) & (xi <= W - 1) & (yi >= 0) & (yi <= H - 1)
                xc = jnp.clip(xi, 0, W - 1).astype(jnp.int32)
                yc = jnp.clip(yi, 0, H - 1).astype(jnp.int32)
                v = jax.vmap(lambda im, yy, xx: im[:, yy, xx])(img, yc, xc)
                return v * valid[:, None, :, :].astype(img.dtype)
            v00 = gather(x0, y0)
            v01 = gather(x0 + 1, y0)
            v10 = gather(x0, y0 + 1)
            v11 = gather(x0 + 1, y0 + 1)
            return v00 * ((1 - wx) * (1 - wy))[:, None] + v01 * (wx * (1 - wy))[:, None] + v10 * ((1 - wx) * wy)[:, None] + v11 * (wx * wy)[:, None]

        def _interp1d(x, Lout):
            Lin = x.shape[-1]
            real = jnp.clip((jnp.arange(Lout, dtype=jnp.float32) + 0.5) * (Lin / Lout) - 0.5, 0.0, Lin - 1.0)
            i0 = jnp.floor(real).astype(jnp.int32)
            i1 = jnp.minimum(i0 + 1, Lin - 1)
            w = real - i0
            return x[..., i0] * (1.0 - w) + x[..., i1] * w

        def _interp_last_ac(x, Lout):
            Lin = x.shape[-1]
            if Lin == Lout:
                return x
            pos = jnp.arange(Lout, dtype=jnp.float32) * ((Lin - 1) / (Lout - 1))
            i0 = jnp.floor(pos).astype(jnp.int32)
            i1 = jnp.minimum(i0 + 1, Lin - 1)
            w = pos - i0
            return x[..., i0] * (1.0 - w) + x[..., i1] * w

        def _avgpool1(x):
            L = x.shape[-1]
            return x[..., :L // 2 * 2].reshape(x.shape[:-1] + (L // 2, 2)).mean(-1)

        def _conv1(sig, w):
            k = w.shape[-1]
            return jax.lax.conv_general_dilated(sig, w, (1,), [(k // 2, k // 2)], dimension_numbers=('NCH', 'OIH', 'NCH'))
        B, C, H, W = x.shape
        K = MAX_ANGLES
        pooled = x.reshape(B, C, 4, H // 4, 4, W // 4).mean(axis=(3, 5))
        feat = pooled.reshape(B, C * 16)
        h = jax.nn.relu(feat @ lin1_w.T + lin1_b)
        off = (h @ lin2_w.T + lin2_b) * 30.0
        base = jnp.linspace(0.0, 180.0, K)
        angles = jnp.sort(jnp.clip(base[None, :] + off, 0.0, 180.0), axis=1)
        xs = jnp.linspace(-1.0, 1.0, W)
        ys = jnp.linspace(-1.0, 1.0, H)
        yc, xc = jnp.meshgrid(ys, xs, indexing='ij')
        th = angles * (jnp.pi / 180.0)
        co = jnp.cos(th)[:, :, None, None]
        si = jnp.sin(th)[:, :, None, None]
        gx = xc[None, None] * co + yc[None, None] * si
        gy = -xc[None, None] * si + yc[None, None] * co
        grid = jnp.stack([gx, gy], axis=-1).reshape(B * K, H, W, 2)
        xexp = jnp.broadcast_to(x[:, None], (B, K, C, H, W)).reshape(B * K, C, H, W)
        rotated = _grid_sample(xexp, grid)
        sig = rotated.sum(axis=3)
        N = B * K
        c0 = _conv1(sig.reshape(N * C, 1, H), wf0).reshape(N, C, H)
        cur = _avgpool1(sig)
        L2 = H // 2
        f1 = _conv1(cur.reshape(N * C, 1, L2), wf1)
        u1 = _interp1d(_avgpool1(f1), L2).reshape(N, C, L2)
        c1 = _interp1d(u1, H)
        coeffs = jnp.stack([c0, c1], axis=2)
        wav = coeffs.reshape(B, K, C, SCALES, H).transpose(0, 2, 4, 3, 1)
        combined = wav.reshape(B, C * SCALES, H, K)
        combined = _interp_last_ac(combined, W)
        combined = _interp_last_ac(combined.swapaxes(-1, -2), H).swapaxes(-1, -2)
        out = jnp.einsum('oc,bchw->bohw', fuse_w, combined) + fuse_b[None, :, None, None]
        scale = (bn_gamma / jnp.sqrt(bn_var + BN_EPS))[None, :, None, None]
        out = (out - bn_mean[None, :, None, None]) * scale + bn_beta[None, :, None, None]
        return jax.nn.relu(out)

    def _L1_conv_ref(x, w0, b0, w1, b1, w2, b2, w3, b3, wf, bf):
        import jax, jax.numpy as jnp
        import numpy as np
        C = 64
        K = 3
        B, H, W = (8, 128, 128)

        def conv2d(x, w, b, pad, groups=1):
            y = jax.lax.conv_general_dilated(x, w, window_strides=(1, 1), padding=[(pad, pad), (pad, pad)], feature_group_count=groups, dimension_numbers=('NCHW', 'OIHW', 'NCHW'))
            return y + b[None, :, None, None]
        b, c, h, w = x.shape
        pre = x
        x0 = conv2d(x, w0, b0, pad=1)
        x1 = conv2d(x0, w1, b1, pad=1, groups=c)
        m = jnp.mean(x0, axis=(2, 3))
        x2 = jax.lax.conv_general_dilated(m[:, None, :], w2, window_strides=(1,), padding=[(K // 2, K // 2)], dimension_numbers=('NCH', 'OIH', 'NCH')) + b2[None, :, None]
        out = x1 + x2[:, 0, :, None, None]
        fil = jnp.einsum('oc,bchw->bohw', w3[:, :, 0, 0], out) + b3[None, :, None, None]
        filter_x = fil.reshape(b, c, K * K, h, w)
        xp = jnp.pad(x0, ((0, 0), (0, 0), (1, 1), (1, 1)))
        unfold_x = jnp.stack([xp[:, :, i:i + h, j:j + w] for i in range(3) for j in range(3)], axis=2)
        out = jnp.sum(unfold_x * filter_x, axis=2)
        out = jnp.where(out >= 0, out, 0.2 * out)
        out = conv2d(out, wf, bf, pad=1) + pre
        return out

    def _L2_conv_ref(x, blk1_w1, blk1_b1, blk1_w2, blk1_b2, blk2_w1, blk2_b1, blk2_w2, blk2_b2, tok_w, tok_b):
        import jax, jax.numpy as jnp
        from jax import lax
        import numpy as np
        C = 64
        K = 3
        N = 2
        H = 256
        W = 256
        DOWN = 4

        def _conv(x, w, b):
            y = lax.conv_general_dilated(x, w, (1, 1), 'SAME', dimension_numbers=('NCHW', 'OIHW', 'NCHW'))
            return y + b[None, :, None, None]

        def _resblock(x, w1, b1, w2, b2):
            out = jax.nn.leaky_relu(_conv(x, w1, b1), 0.1)
            return _conv(out, w2, b2) + x

        def _block(x, ws1, bs1, ws2, bs2):
            for i in range(ws1.shape[0]):
                x = _resblock(x, ws1[i], bs1[i], ws2[i], bs2[i])
            return x

        def _avgpool(x, k):
            n, c, h, w = x.shape
            return x.reshape(n, c, h // k, k, w // k, k).mean(axis=(3, 5))

        def _maxpool(x, k):
            n, c, h, w = x.shape
            return x.reshape(n, c, h // k, k, w // k, k).max(axis=(3, 5))

        def _dyn_conv(x, wt, k):
            n, c, h, w = x.shape
            pad = (k - 1) // 2
            xp = jnp.pad(x, ((0, 0), (0, 0), (pad, pad), (pad, pad)), mode='edge')
            wr = wt.reshape(n, c, k * k, h, w)
            out = jnp.zeros_like(x)
            for dh in range(k):
                for dw in range(k):
                    out = out + xp[:, :, dh:dh + h, dw:dw + w] * wr[:, :, dh * k + dw]
            return out
        y = _avgpool(x, DOWN)
        y = _block(y, blk1_w1, blk1_b1, blk1_w2, blk1_b2)
        y = _maxpool(y, 2)
        y = _block(y, blk2_w1, blk2_b1, blk2_w2, blk2_b2)
        wt = _conv(y, tok_w, tok_b)
        n, ck2, hs, ws = wt.shape
        wt = jax.image.resize(wt, (n, ck2, hs * 2 * DOWN, ws * 2 * DOWN), method='bilinear')
        return _dyn_conv(x, wt, K)

    def _L3_conv_ref(x, weights1, weights2):
        import jax, jax.numpy as jnp
        import numpy as np
        B, CIN, COUT, S1, S2, M1, M2 = (16, 64, 64, 128, 128, 16, 16)

        def _cas(L, dtype):
            k = jnp.arange(L, dtype=dtype)
            ang = 2.0 * jnp.pi / L * (k[:, None] * k[None, :])
            return jnp.cos(ang) + jnp.sin(ang)

        def dht2(x):
            M, N = (x.shape[-2], x.shape[-1])
            cas_row = _cas(M, x.dtype)
            cas_col = _cas(N, x.dtype)
            y = jnp.einsum('bimn,gn->bimg', x, cas_col)
            return jnp.einsum('mf,bimn->bifn', cas_row, y)

        def idht2(x):
            return dht2(x) / (x.shape[-2] * x.shape[-1])

        def _neg_freq(a):
            return jnp.roll(jnp.flip(a, axis=(-2, -1)), shift=(1, 1), axis=(-2, -1))

        def compl_mul2d(x1, x2):
            x1n = _neg_freq(x1)
            x2n = _neg_freq(x2)
            e = lambda a, b: jnp.einsum('bixy,ioxy->boxy', a, b)
            return 0.5 * (e(x1, x2) - e(x1n, x2n) + e(x1, x2n) + e(x1n, x2))
        m1, m2 = (weights1.shape[2], weights1.shape[3])
        b, cout = (x.shape[0], weights1.shape[1])
        s1, s2 = (x.shape[-2], x.shape[-1])
        cos_part = dht2(x)
        sin_part = dht2(jnp.flip(x, axis=(-2, -1)))
        phase = jnp.arctan2(sin_part, cos_part)
        out_dht = jnp.zeros((b, cout, s1, s2), dtype=x.dtype)
        out_dht = out_dht.at[:, :, :m1, :m2].set(compl_mul2d(cos_part[:, :, :m1, :m2], weights1))
        out_dht = out_dht.at[:, :, -m1:, :m2].set(compl_mul2d(cos_part[:, :, -m1:, :m2], weights2))
        y = idht2(out_dht)
        return y * jnp.cos(phase)

    def _gn(v, G=32, eps=1e-5):
        B_, C_, H_, W_ = v.shape
        g = v.reshape(B_, G, C_ // G, H_, W_)
        m = jnp.mean(g, axis=(2, 3, 4), keepdims=True)
        s = jnp.var(g, axis=(2, 3, 4), keepdims=True)
        return ((g - m) / jnp.sqrt(s + eps)).reshape(v.shape)

    def _ln_c(v, eps=1e-6):
        m = jnp.mean(v, axis=1, keepdims=True)
        s = jnp.var(v, axis=1, keepdims=True)
        return (v - m) / jnp.sqrt(s + eps)

    def _ln_t(v, eps=1e-5):
        m = jnp.mean(v, axis=-1, keepdims=True)
        s = jnp.var(v, axis=-1, keepdims=True)
        return (v - m) / jnp.sqrt(s + eps)

    def _to_tokens(v):
        B_, C_, H_, W_ = v.shape
        return v.reshape(B_, C_, H_ * W_).transpose(0, 2, 1)
    def _from_tokens(t, like):
        B_, C_, H_, W_ = like.shape
        return t.transpose(0, 2, 1).reshape(B_, C_, H_, W_)

    x = x + _L0_conv_ref(_gn(x), L0_conv_lin1_w, L0_conv_lin1_b, L0_conv_lin2_w, L0_conv_lin2_b, L0_conv_wf0, L0_conv_wf1, L0_conv_fuse_w, L0_conv_fuse_b, L0_conv_bn_gamma, L0_conv_bn_beta, L0_conv_bn_mean, L0_conv_bn_var)
    x = x + _L1_conv_ref(_gn(x), L1_conv_w0, L1_conv_b0, L1_conv_w1, L1_conv_b1, L1_conv_w2, L1_conv_b2, L1_conv_w3, L1_conv_b3, L1_conv_wf, L1_conv_bf)
    x = x + _L2_conv_ref(_gn(x), L2_conv_blk1_w1, L2_conv_blk1_b1, L2_conv_blk1_w2, L2_conv_blk1_b2, L2_conv_blk2_w1, L2_conv_blk2_b1, L2_conv_blk2_w2, L2_conv_blk2_b2, L2_conv_tok_w, L2_conv_tok_b)
    x = x + _L3_conv_ref(_gn(x), L3_conv_weights1, L3_conv_weights2)
    return x


_drawn_inputs = setup_inputs


def setup_inputs(seed=0):
    import zlib

    import numpy as np

    out = dict(_drawn_inputs(seed))
    spreads = {'L0_conv_lin1_b': (0.0, 0.1),
     'L0_conv_lin2_b': (0.0, 0.1),
     'L0_conv_bn_gamma': (1.0, 0.2),
     'L0_conv_bn_beta': (0.0, 0.1),
     'L0_conv_bn_mean': (0.0, 0.1),
     'L0_conv_bn_var': (1.0, 0.2),
     'L2_conv_blk1_b1': (0.0, 0.1),
     'L2_conv_blk1_b2': (0.0, 0.1),
     'L2_conv_blk2_b1': (0.0, 0.279),
     'L2_conv_blk2_b2': (0.0, 0.1),
     'L2_conv_tok_b': (0.0, 0.1)}
    factors = {'L1_conv_b0': 5.604,
     'L1_conv_b1': 8.0,
     'L1_conv_b3': 7.45,
     'L1_conv_bf': 8.0,
     'L3_conv_weights1': 8.0,
     'L3_conv_weights2': 8.0}
    for name, (base, spread) in spreads.items():
        noise = np.random.default_rng([zlib.crc32(name.encode()), seed]).standard_normal(out[name].shape)
        drawn = base * np.exp(spread * noise) if base else spread * noise
        out[name] = jnp.asarray(drawn.astype(out[name].dtype))
    for name, factor in factors.items():
        out[name] = (out[name] * factor).astype(out[name].dtype)
    return out
```

```python
import numpy as np
from contextlib import ExitStack, contextmanager

import concourse.bass as bass
from concourse import mybir

F32 = mybir.dt.float32
ALU = mybir.AluOpType
ACT = mybir.ActivationFunctionType
AX_X = mybir.AxisListType.X

C = 64
W = 128
HR = W // 2
NPX = HR * W
NA = 6
GN_EPS = 1e-5
BN_EPS = 1e-5


class Chain:

    def __init__(self, eng, sem, base, per):
        self.eng, self.sem, self.base, self.per, self.n = eng, sem, base, per, 0

    def __call__(self, ins):
        self.n += 1
        ins.then_inc(self.sem, 1)
        self.eng.wait_ge(self.sem, self.base + self.n)

    def done(self):
        assert self.n == self.per, self.n


def gate(eng, sem, value, passed):
    eng.wait_ge(sem, value)
    eng.sem_inc(passed, 1)


@contextmanager
def phase(nc):
    held = []

    def named(name):
        held.append(nc.alloc_semaphore(name=name))
        return held[-1]

    yield named
    for s in held:
        nc.gpsimd.sem_clear(s)
        nc.release_semaphore(s)
    nc.all_engine_barrier()


def bc(ap, shape):
    return ap.broadcast_to(shape)


def layer0(nc, B, x, x1, k):
    PAIRS = NA // 2
    GR = 4
    GPP = 2 * HR // GR
    CPER = 66
    with phase(nc) as named, ExitStack() as ctx:
        def sb(name, shape, dt=F32):
            return ctx.enter_context(nc.sbuf_tensor("a_" + name, shape, dt))

        def sem(name):
            return named("a_" + name)

        X = sb("X", [128, NPX])
        R = sb("R", [128, 128, 128])
        Rf = R[:, :, :].rearrange("p a b -> p (a b)")
        V = Rf[:, 0:NPX]
        GN = Rf[:, NPX:2 * NPX]
        XT = sb("XT", [128, 128, 2, C])
        D = sb("D", [128, 2, 2, GR, 128])
        T = sb("T", [128, 2, 2, GR, 128])
        COORD = sb("COORD", [128, 2, PAIRS * 128])
        iota = sb("iota", [128, 128])
        ident = sb("ident", [128, 128])
        anti = sb("anti", [128, 128])
        gsum = sb("gsum", [128, 128])
        lin1 = sb("lin1", [128, 8, 32])
        lin2 = sb("lin2", [32, NA])
        lin1b = sb("lin1b", [32, 1])
        lin2b = sb("lin2b", [128, NA])
        base = sb("base", [128, NA])
        jc = sb("jc", [128, 2])
        ic = sb("ic", [128, HR])
        ftab = sb("ftab", [128, W])
        wf0 = sb("wf0", [C, 3])
        wf1 = sb("wf1", [C, 5])
        fuse = sb("fuse", [C, 2, C])
        bn = sb("bn", [128, 5])
        st = sb("st", [128, 16])
        bnp = sb("bnp", [128, 4])
        PB1 = sb("PB1", [128, HR, 4])
        PB = sb("PB", [128, 8])
        PBn = sb("PBn", [128, 8])
        h1 = sb("h1", [32, 1])
        h1b = sb("h1b", [32, 128])
        ones32 = sb("ones32", [32, 128])
        ang = sb("ang", [128, 8, NA])
        trig = sb("trig", [128, 2, NA])
        jt = sb("jt", [128, 2, NA])
        SIG = sb("SIG", [128, PAIRS * 128])
        SP = sb("SP", [C, NA, W + 2])
        CUR = sb("CUR", [C, NA, HR + 4])
        F1 = sb("F1", [C, NA, HR])
        F2 = sb("F2", [C, NA, HR // 2 + 2])
        U1 = sb("U1", [C, NA, HR + 2])
        QT = sb("QT", [C, NA, HR + 2])
        CC = sb("CC", [C, NA, W, 2])
        Z = sb("Z", [128, NA, HR])
        DZ = sb("DZ", [128, NA - 1, HR])
        P = ctx.enter_context(nc.psum_tensor("a_P", [128, 8, 512], F32))

        const_loaded = sem("const_loaded")
        x_loaded = sem("x_loaded")
        x_used = sem("x_used")
        x1_stored = sem("x1_stored")
        init_done = sem("init_done")
        chain_dve = sem("chain_dve")
        chain_act = sem("chain_act")
        sum_ready = sem("sum_ready")
        mean_ready = sem("mean_ready")
        negmean_ready = sem("negmean_ready")
        sq_ready = sem("sq_ready")
        var_ready = sem("var_ready")
        vare_ready = sem("vare_ready")
        std_ready = sem("std_ready")
        gnp_ready = sem("gnp_ready")
        gn_ready = sem("gn_ready")
        pooled_ready = sem("pooled_ready")
        lin1_done = sem("lin1_done")
        h1_ready = sem("h1_ready")
        h1b_ready = sem("h1b_ready")
        lin2_done = sem("lin2_done")
        theta_ready = sem("theta_ready")
        trig_ready = sem("trig_ready")
        coord_ready = sem("coord_ready")
        tr_done = sem("tr_done")
        tr_ev = sem("tr_ev")
        rot_done = sem("rot_done")
        rot_ev = sem("rot_ev")
        diff_ready = sem("diff_ready")
        abs_ready = sem("abs_ready")
        tents_ready = sem("tents_ready")
        rows_done = sem("rows_done")
        rows_evicted = sem("rows_evicted")
        sig_ready = sem("sig_ready")
        sig_evicted = sem("sig_evicted")
        coef_ready = sem("coef_ready")
        fuse_done = sem("fuse_done")
        blend_ready = sem("blend_ready")
        relu_ready = sem("relu_ready")
        out_ready = sem("out_ready")
        tr_ev0 = sem("tr_ev0")
        rot_ev0 = sem("rot_ev0")
        bn_std = sem("bn_std")
        passed = sem("passed")
        consts = [(iota, "iota"), (ident, "ident"), (anti, "anti"), (gsum, "gsum"), (lin1, "lin1"),
                  (lin2, "lin2"), (lin1b, "lin1b"), (lin2b, "lin2b"), (base, "base"), (jc, "jc"),
                  (ic, "ic"), (ftab, "ftab"), (wf0, "wf0"), (wf1, "wf1"), (fuse, "fuse"), (bn, "bn")]
        CONST = 16 * len(consts)
        block = ctx.enter_context(nc.Block())

        def pair_no(b, p):
            return b * PAIRS + p

        @block.sync
        def _(sp):
            for t, name in consts:
                sp.dma_start(t[:], k[name]).then_inc(const_loaded, 16)
            with sp.Fori(0, B) as b:
                sp.wait_ge(x_used, b + 1)
                for h in range(2):
                    sp.dma_start(X[64 * h:64 * h + 64, :], x[b, :, HR * h:HR * h + HR, :].rearrange("c r w -> c (r w)")
                                 ).then_inc(x_loaded, 16)
                sp.wait_ge(out_ready, b + 1)
                for h in range(2):
                    sp.dma_start(x1[b, :, HR * h:HR * h + HR, :].rearrange("c r w -> c (r w)"), V[64 * h:64 * h + 64, :]
                                 ).then_inc(x1_stored, 16)
            sp.wait_ge(x1_stored, 32 * B + 1)

        @block.scalar
        def _(act):
            act.wait_ge(init_done, 4)
            nc.scalar.activation(bnp[:, 1:2], bnp[:, 0:1], ACT.Sqrt).then_inc(bn_std, 1)
            act.sem_inc(abs_ready, 2)
            act.sem_inc(rows_evicted, 2)
            with act.Fori(0, B) as b:
                ch = Chain(act, chain_act, b * 2, 2)
                act.wait_ge(negmean_ready, b + 1)
                nc.scalar.activation(GN, X[:, :], ACT.Square, bias=st[:, 1:2], accum_out=st[:, 2:3]
                                     ).then_inc(sq_ready, 1)
                act.wait_ge(vare_ready, b + 1)
                nc.scalar.activation(st[:, 4:5], st[:, 3:4], ACT.Sqrt).then_inc(std_ready, 1)
                act.wait_ge(gnp_ready, b + 1)
                nc.scalar.activation(GN, X[:, :], ACT.Identity, bias=st[:, 6:7], scale=st[:, 5:6]
                                     ).then_inc(gn_ready, 1)
                act.wait_ge(lin1_done, b + 1)
                nc.scalar.activation(h1[:, :], P[0:32, 2, 0:1], ACT.Relu, bias=lin1b[:, 0:1]).then_inc(h1_ready, 1)
                for n in range(1, 16, 2):
                    act.wait_ge(tr_done, b * 16 + n + 1)
                    for h in range(2):
                        ins = nc.scalar.activation(XT[:, HR * h + 4 * n:HR * h + 4 * n + 4, 0, :],
                                                   P[:, 4 + n % 4, :].rearrange("p (r h c) -> p h r c", r=4, h=2)[:, h],
                                                   ACT.Copy)
                    ins.then_inc(tr_ev, 1)
                act.wait_ge(theta_ready, b + 1)
                nc.scalar.activation(trig[:, 0, :], ang[:, 2, :], ACT.Sin).then_inc(chain_act, 1)
                nc.scalar.activation(trig[:, 1, :], ang[:, 3, :], ACT.Sin).then_inc(trig_ready, 1)
                for n in range(1, 16, 2):
                    act.wait_ge(rot_done, b * 16 + n + 1)
                    nc.scalar.activation(XT[:, 127 - 8 * n:(119 - 8 * n) if n < 15 else None:-1, 1, :],
                                         P[:, 4 + n % 4, :].rearrange("p (r c) -> p r c", r=8), ACT.Copy
                                         ).then_inc(rot_ev, 1)

                def absolute(p, q, u):
                    g = (b * PAIRS + p) * GPP + q * 2 + u
                    act.wait_ge(diff_ready, g + 1)
                    act.wait_ge(rows_done, g + 1)
                    nc.scalar.activation(T[:, u].rearrange("p a r w -> p (a r w)"),
                                         D[:, u].rearrange("p a r w -> p (a r w)"), ACT.Abs
                                         ).then_inc(abs_ready, 1)

                def evict(p, q, u):
                    g = (b * PAIRS + p) * GPP + q * 2 + u
                    act.wait_ge(rows_done, g + 3)
                    nc.scalar.activation(R[:, bass.ds(q * 2 * GR + u * GR, GR), :],
                                         P[:, u, :].rearrange("p (r w) -> p r w", r=GR), ACT.Copy
                                         ).then_inc(rows_evicted, 1)

                with act.Fori(0, PAIRS) as p:
                    absolute(p, 0, 0)
                    absolute(p, 0, 1)
                    act.wait_ge(sig_ready, b * PAIRS + p + 1)
                    act.wait_ge(x1_stored, b * 32 + 1)
                    with act.Fori(1, GPP // 2) as q:
                        absolute(p, q, 0)
                        evict(p, q - 1, 0)
                        absolute(p, q, 1)
                        evict(p, q - 1, 1)
                    evict(p, GPP // 2 - 1, 0)
                    evict(p, GPP // 2 - 1, 1)
                act.wait_ge(blend_ready, b + 1)
                nc.scalar.activation(V, V, ACT.Relu, bias=bnp[:, 3:4], scale=bnp[:, 2:3]).then_inc(relu_ready, 1)

        @block.tensor
        def _(pe):
            pe.sem_inc(rows_done, 2)
            pe.sem_inc(sig_ready, 1)
            pe.wait_ge(const_loaded, CONST)
            with pe.Fori(0, B) as b:
                pe.wait_ge(sum_ready, b + 1)
                nc.tensor.matmul(P[:, 2, 0:1], gsum[:, :], st[:, 0:1], start=True, stop=True).then_inc(mean_ready, 1)
                pe.wait_ge(sq_ready, b + 1)
                pe.wait_ge(negmean_ready, b + 1)
                nc.tensor.matmul(P[:, 2, 0:1], gsum[:, :], st[:, 2:3], start=True, stop=True).then_inc(var_ready, 1)
                pe.wait_ge(pooled_ready, b + 1)
                for n in range(8):
                    mm = nc.tensor.matmul(P[0:32, 2, 0:1], lin1[:, n, :], PBn[:, n:n + 1], start=n == 0, stop=n == 7)
                mm.then_inc(lin1_done, 1)
                pe.wait_ge(h1b_ready, b + 1)
                nc.tensor.matmul(P[:, 2, 0:NA], h1b[:, :], lin2[:, :], start=True, stop=True).then_inc(lin2_done, 1)
                pe.wait_ge(gn_ready, b + 1)
                for n in range(16):
                    if n >= 4:
                        pe.wait_ge(tr_ev if n % 2 else tr_ev0, b * 8 + (n - 4) // 2 + 1)
                    for r in range(4):
                        mm = nc.tensor.transpose(P[:, 4 + n % 4, 128 * r:128 * r + 128],
                                                 GN[:, (4 * n + r) * W:(4 * n + r + 1) * W], ident[:, :])
                    mm.then_inc(tr_done, 1)
                for n in range(16):
                    pe.wait_ge(tr_ev, b * 8 + 8)
                    pe.wait_ge(tr_ev0, b * 8 + 8)
                    if n >= 4:
                        pe.wait_ge(rot_ev if n % 2 else rot_ev0, b * 8 + (n - 4) // 2 + 1)
                    nc.tensor.matmul(P[:, 4 + n % 4, :], anti[:, :], XT[:, 8 * n:8 * n + 8, 0, :],
                                     start=True, stop=True).then_inc(rot_done, 1)
                gate(pe, rot_ev, b * 8 + 8, passed)
                gate(pe, rot_ev0, b * 8 + 8, passed)
                with pe.Fori(0, PAIRS) as p:
                    with pe.Fori(0, GPP // 2) as q:
                        for u in range(2):
                            g = (b * PAIRS + p) * GPP + q * 2 + u
                            pe.wait_ge(tents_ready, g + 1)
                            pe.wait_ge(rows_evicted, g + 1)
                            for r in range(GR):
                                mm = nc.tensor.matmul(P[:, u, 128 * r:128 * r + 128], T[:, u, 0, r, :], T[:, u, 1, r, :],
                                                      start=True, stop=True)
                            mm.then_inc(rows_done, 1)
                    pe.wait_ge(rows_evicted, (b * PAIRS + p) * GPP + GPP + 2)
                    pe.wait_ge(sig_evicted, b * PAIRS + p + 1)
                    for y in range(W):
                        mm = nc.tensor.matmul(P[:, 3, 0:128], XT[:, y].rearrange("p v c -> p (v c)"), R[:, :, y],
                                              start=y == 0, stop=y == W - 1)
                    mm.then_inc(sig_ready, 1)
                gate(pe, coef_ready, b + 1, passed)
                for h in range(2):
                    for s in range(2):
                        mm = nc.tensor.matmul(P[64 * h:64 * h + 64, 2, 0:NA * HR], fuse[:, s, :],
                                              CC[:, :, HR * s + HR // 2 * h:HR * s + HR // 2 * (h + 1), :], start=s == 0, stop=s == 1)
                mm.then_inc(fuse_done, 1)

        @block.vector
        def _(dve):
            v = nc.vector
            dve.wait_ge(const_loaded, CONST)
            v.memset(ones32[:, :], 1.0).then_inc(init_done, 1)
            v.memset(SP[:, :, :], 0.0).then_inc(init_done, 1)
            v.memset(CUR[:, :, :], 0.0).then_inc(init_done, 1)
            v.tensor_scalar(bnp[:, 0:1], bn[:, 3:4], BN_EPS, None, ALU.add).then_inc(init_done, 1)
            dve.wait_ge(bn_std, 1)
            v.reciprocal(bnp[:, 1:2], bnp[:, 1:2]).then_inc(init_done, 1)
            dve.wait_ge(init_done, 5)
            v.tensor_tensor(bnp[:, 2:3], bnp[:, 1:2], bn[:, 0:1], ALU.mult).then_inc(init_done, 1)
            v.tensor_tensor(bnp[:, 3:4], bn[:, 4:5], bn[:, 2:3], ALU.subtract).then_inc(init_done, 1)
            dve.wait_ge(init_done, 7)
            v.scalar_tensor_tensor(bnp[:, 3:4], bnp[:, 3:4], bnp[:, 2:3], bn[:, 1:2], ALU.mult, ALU.add
                                   ).then_inc(init_done, 1)
            dve.wait_ge(init_done, 8)
            dve.sem_inc(x1_stored, 1)
            dve.sem_inc(x_used, 1)
            dve.sem_inc(sig_evicted, 1)
            with dve.Fori(0, B) as b:
                ch = Chain(dve, chain_dve, b * CPER, CPER)
                dve.wait_ge(x_loaded, b * 32 + 32)
                ch(v.tensor_reduce(PB1[:, :, :], X[:, :].rearrange("p (r q w) -> p r q w", r=HR, q=4), AX_X, ALU.add))
                ch(v.tensor_reduce(PB[:, :].rearrange("p (a q) -> p a q", a=2),
                                   PB1[:, :, :].rearrange("p (a r) q -> p a q r", a=2), AX_X, ALU.add))
                v.tensor_reduce(st[:, 0:1], PB[:, :], AX_X, ALU.add).then_inc(sum_ready, 1)
                dve.wait_ge(mean_ready, b + 1)
                v.tensor_scalar(st[:, 1:2], P[:, 2, 0:1], -1.0, None, ALU.mult).then_inc(negmean_ready, 1)
                dve.wait_ge(var_ready, b + 1)
                v.tensor_scalar(st[:, 3:4], P[:, 2, 0:1], GN_EPS, None, ALU.add).then_inc(vare_ready, 1)
                dve.wait_ge(std_ready, b + 1)
                ch(v.reciprocal(st[:, 5:6], st[:, 4:5]))
                v.tensor_scalar(st[:, 6:7], st[:, 1:2], st[:, 5:6], None, ALU.mult).then_inc(gnp_ready, 1)
                dve.wait_ge(gnp_ready, b + 1)
                ch(v.tensor_scalar(PBn[:, :], PB[:, :], 1.0 / 1024, None, ALU.mult))
                v.tensor_scalar(PBn[:, :], PBn[:, :], st[:, 5:6], st[:, 6:7], ALU.mult, ALU.add
                                ).then_inc(pooled_ready, 1)
                dve.wait_ge(h1_ready, b + 1)
                v.tensor_scalar(h1b[:, :], ones32[:, :], h1[:, 0:1], None, ALU.mult).then_inc(h1b_ready, 1)
                dve.wait_ge(lin2_done, b + 1)
                ch(v.tensor_tensor(ang[:, 0, :], P[:, 2, 0:NA], lin2b[:, :], ALU.add))
                ch(v.scalar_tensor_tensor(ang[:, 0, :], ang[:, 0, :], 30.0, base[:, :], ALU.mult, ALU.add))
                ch(v.tensor_scalar(ang[:, 0, :], ang[:, 0, :], 0.0, 180.0, ALU.max, ALU.min))
                a, o = 0, 1
                for n in range(NA):
                    if n % 2 == 0:
                        lo, hi = slice(0, NA, 2), slice(1, NA, 2)
                    else:
                        lo, hi = slice(1, NA - 1, 2), slice(2, NA - 1, 2)
                        ch(v.tensor_copy(ang[:, o, 0:NA:NA - 1], ang[:, a, 0:NA:NA - 1]))
                    ch(v.tensor_tensor(ang[:, o, lo], ang[:, a, lo], ang[:, a, hi], ALU.min))
                    ch(v.tensor_tensor(ang[:, o, hi], ang[:, a, lo], ang[:, a, hi], ALU.max))
                    a, o = o, a
                ch(v.tensor_scalar(ang[:, 2, :], ang[:, a, :], float(np.float32(np.pi / 180)), None, ALU.mult))
                v.tensor_scalar(ang[:, 3, :], ang[:, 2, :], -1.0, float(np.pi / 2), ALU.mult, ALU.add
                                ).then_inc(theta_ready, 1)
                for n in range(0, 16, 2):
                    dve.wait_ge(tr_done, b * 16 + n + 1)
                    for h in range(2):
                        ins = v.tensor_copy(XT[:, HR * h + 4 * n:HR * h + 4 * n + 4, 0, :],
                                            P[:, 4 + n % 4, :].rearrange("p (r h c) -> p h r c", r=4, h=2)[:, h])
                    ins.then_inc(tr_ev0, 1)
                for n in range(0, 16, 2):
                    dve.wait_ge(rot_done, b * 16 + n + 1)
                    v.tensor_copy(XT[:, 127 - 8 * n:119 - 8 * n:-1, 1, :],
                                  P[:, 4 + n % 4, :].rearrange("p (r c) -> p r c", r=8)).then_inc(rot_ev0, 1)
                dve.wait_ge(trig_ready, b + 1)
                dve.wait_ge(chain_act, b + 1)
                ch(v.tensor_scalar(jt[:, 0, :], trig[:, 1, :], jc[:, 0:1], 63.5, ALU.mult, ALU.add))
                ch(v.tensor_scalar(jt[:, 1, :], trig[:, 0, :], jc[:, 1:2], 63.5, ALU.mult, ALU.add))
                icb = bc(ic[:, :].unsqueeze(1), [128, NA, HR])
                for m in range(2):
                    cm = COORD[:, m, :].rearrange("p (k i) -> p k i", k=NA)
                    ch(v.tensor_tensor(cm, icb, bc(trig[:, m, :].unsqueeze(2), [128, NA, HR]), ALU.mult))
                    ch(v.tensor_tensor(cm, cm, bc(jt[:, m, :].unsqueeze(2), [128, NA, HR]), ALU.add))

                dve.sem_inc(passed, 1)

                def diff(p, q, u):
                    g = (b * PAIRS + p) * GPP + q * 2 + u
                    dve.wait_ge(abs_ready, g + 1)
                    c = COORD[:, :, bass.ds(p * 128 + q * (2 * GR) + u * GR, GR)]
                    v.tensor_tensor(D[:, u], bc(iota[:, :].unsqueeze(1).unsqueeze(1), [128, 2, GR, 128]),
                                    bc(c.unsqueeze(3), [128, 2, GR, 128]), ALU.subtract).then_inc(diff_ready, 1)

                def tent(p, q, u):
                    g = (b * PAIRS + p) * GPP + q * 2 + u
                    dve.wait_ge(abs_ready, g + 3)
                    t = T[:, u].rearrange("p a r w -> p (a r w)")
                    v.tensor_scalar(t, t, 1.0, 1.0, ALU.min, ALU.subtract).then_inc(tents_ready, 1)

                with dve.Fori(0, PAIRS) as p:
                    diff(p, 0, 0)
                    diff(p, 0, 1)
                    with dve.Fori(1, GPP // 2) as q:
                        tent(p, q - 1, 0)
                        diff(p, q, 0)
                        tent(p, q - 1, 1)
                        diff(p, q, 1)
                    tent(p, GPP // 2 - 1, 0)
                    tent(p, GPP // 2 - 1, 1)
                    dve.wait_ge(sig_ready, b * PAIRS + p + 2)
                    v.tensor_copy(SIG[:, bass.ds(p * 128, 128)], P[:, 3, 0:128]).then_inc(sig_evicted, 1)
                dve.wait_ge(sig_evicted, b * PAIRS + PAIRS + 1)
                sig = SIG[:, :].rearrange("p (k i) -> p k i", k=NA)
                ch(v.tensor_copy(SP[:, :, 1:1 + HR], sig[0:64]))
                ch(v.tensor_copy(SP[:, :, W:HR:-1], sig[64:128]))
                ch(v.tensor_scalar(CC[:, :, :, 0], SP[:, :, 0:W], wf0[:, 0:1], None, ALU.mult))
                for t in (1, 2):
                    ch(v.scalar_tensor_tensor(CC[:, :, :, 0], SP[:, :, t:t + W], wf0[:, t:t + 1], CC[:, :, :, 0], ALU.mult, ALU.add))
                cur = CUR[:, :, 2:2 + HR]
                ch(v.tensor_tensor(cur, SP[:, :, 1:W:2], SP[:, :, 2:W + 1:2], ALU.add))
                ch(v.tensor_scalar(cur, cur, 0.5, None, ALU.mult))
                ch(v.tensor_scalar(F1[:, :, :], CUR[:, :, 0:HR], wf1[:, 0:1], None, ALU.mult))
                for t in range(1, 5):
                    ch(v.scalar_tensor_tensor(F1[:, :, :], CUR[:, :, t:t + HR], wf1[:, t:t + 1], F1[:, :, :], ALU.mult, ALU.add))
                L = HR // 2
                ch(v.tensor_tensor(F2[:, :, 1:1 + L], F1[:, :, 0:HR:2], F1[:, :, 1:HR:2], ALU.add))
                ch(v.tensor_scalar(F2[:, :, 1:1 + L], F2[:, :, 1:1 + L], 0.5, None, ALU.mult))
                for src, dst, n in ((F2, U1[:, :, 1:1 + HR], L), (U1, CC[:, :, :, 1], HR)):
                    ch(v.tensor_copy(src[:, :, 0:1], src[:, :, 1:2]))
                    ch(v.tensor_copy(src[:, :, n + 1:n + 2], src[:, :, n:n + 1]))
                    ch(v.tensor_scalar(QT[:, :, 0:n + 2], src[:, :, 0:n + 2], 0.25, None, ALU.mult))
                    ch(v.scalar_tensor_tensor(dst[:, :, 0:2 * n:2], src[:, :, 1:n + 1], 0.75, QT[:, :, 0:n], ALU.mult, ALU.add))
                    ch(v.scalar_tensor_tensor(dst[:, :, 1:2 * n:2], src[:, :, 1:n + 1], 0.75, QT[:, :, 2:n + 2], ALU.mult, ALU.add))
                dve.sem_inc(coef_ready, 1)
                dve.wait_ge(fuse_done, b + 1)
                ch(v.tensor_copy(Z[:, :, :], P[:, 2, 0:NA * HR].rearrange("p (k i) -> p k i", k=NA)))
                ch(v.tensor_tensor(DZ[:, :, :], Z[:, 1:NA, :], Z[:, 0:NA - 1, :], ALU.subtract))
                Vw = V.rearrange("p (r w) -> p r w", r=HR)
                for m, (w0, w1) in enumerate(segments()):
                    n = w1 - w0
                    ch(v.tensor_tensor(Vw[:, :, w0:w1], bc(DZ[:, m, :].unsqueeze(2), [128, HR, n]),
                                       bc(ftab[:, w0:w1].unsqueeze(1), [128, HR, n]), ALU.mult))
                for m, (w0, w1) in enumerate(segments()):
                    n = w1 - w0
                    ch(v.tensor_tensor(Vw[:, :, w0:w1], Vw[:, :, w0:w1], bc(Z[:, m, :].unsqueeze(2), [128, HR, n]), ALU.add))
                dve.sem_inc(blend_ready, 1)
                dve.wait_ge(relu_ready, b + 1)
                ch(v.tensor_tensor(V, V, X[:, :], ALU.add))
                dve.sem_inc(x_used, 1)
                dve.sem_inc(out_ready, 1)
                ch.done()


def segments():
    pos = np.arange(W, dtype=np.float32) * np.float32((NA - 1) / (W - 1))
    i0 = np.minimum(np.floor(pos).astype(int), NA - 2)
    return [(int(np.argmax(i0 == m)), int(W - np.argmax(i0[::-1] == m))) for m in range(NA - 1)]



TAPS = 9
TR = 4
NT = HR // TR
PR, PW = HR + 2, W + 2


def layer1(nc, B, x1, x2, k):
    UN = 4
    CPER = 5
    with phase(nc) as named, ExitStack() as ctx:
        def sb(name, shape, dt=F32):
            return ctx.enter_context(nc.sbuf_tensor("b_" + name, shape, dt))

        def sem(name):
            return named("b_" + name)

        X = sb("X", [128, HR, W])
        G = sb("G", [128, PR, PW])
        Y = sb("Y", [128, PR, PW])
        T = sb("T", [128, HR, W])
        W0 = sb("W0", [128, TAPS, 128])
        W3 = sb("W3", [128, TAPS, 128])
        WF = sb("WF", [128, TAPS, 128])
        DW = sb("DW", [128, TAPS, 128])
        ident = sb("ident", [128, 128])
        gsum = sb("gsum", [128, 128])
        shift = sb("shift", [128, 3, 128])
        w1 = sb("w1", [128, TAPS])
        b3 = sb("b3", [128, TAPS])
        w2 = sb("w2", [128, 3])
        bias = sb("bias", [128, 4])
        st = sb("st", [128, 16])
        ms = sb("ms", [128, NT])
        m3 = sb("m3", [128, 4])
        PROD = sb("PROD", [128, 4, TR, W])
        RL = sb("RL", [128, 2, TR, W])
        P = ctx.enter_context(nc.psum_tensor("b_P", [128, 8, 512], F32))
        const_loaded = sem("const_loaded")
        cleared = sem("cleared")
        weights_loaded = sem("weights_loaded")
        diag_ready = sem("diag_ready")
        x_loaded = sem("x_loaded")
        x_used = sem("x_used")
        x2_stored = sem("x2_stored")
        out_ready = sem("out_ready")
        passed = sem("passed")
        prod_used = sem("prod_used")
        chain0 = sem("chain0")
        chain_dve = sem("chain_dve")
        sum_ready = sem("sum_ready")
        mean_ready = sem("mean_ready")
        negmean_ready = sem("negmean_ready")
        sq_ready = sem("sq_ready")
        var_ready = sem("var_ready")
        vare_ready = sem("vare_ready")
        std_ready = sem("std_ready")
        gnp_ready = sem("gnp_ready")
        gn_ready = sem("gn_ready")
        gn_halo = sem("gn_halo")
        conv0_done = sem("conv0_done")
        conv0_ev = sem("conv0_ev")
        y_halo = sem("y_halo")
        ysum_ready = sem("ysum_ready")
        m3_done = sem("m3_done")
        dbias_ready = sem("dbias_ready")
        depth_done = sem("depth_done")
        depth_ev = sem("depth_ev")
        fil_done = sem("fil_done")
        prod_ready = sem("prod_ready")
        acc_done = sem("acc_done")
        relu_ready = sem("relu_ready")
        filtered = sem("filtered")
        f_halo = sem("f_halo")
        convf_done = sem("convf_done")
        mix_ready = sem("mix_ready")
        consts = [(ident, "ident"), (gsum, "gsum"), (shift, "shift"), (w1, "w1"), (b3, "b3"), (w2, "w2"), (bias, "bias1")]
        block = ctx.enter_context(nc.Block())
        t9 = [(t // 3, t % 3) for t in range(TAPS)]

        @block.sync
        def _(sp):
            for t, name in consts:
                sp.dma_start(t[:], k[name]).then_inc(const_loaded, 16)
            sp.wait_ge(cleared, 3)
            for t, name in ((W0, "w0"), (W3, "w3"), (WF, "wf")):
                for h in range(2):
                    sp.dma_start(t[64 * h:64 * h + 64, :, 64 * h:64 * h + 64], k[name]).then_inc(weights_loaded, 16)
            with sp.Fori(0, B) as b:
                sp.wait_ge(x_used, b + 1)
                for h in range(2):
                    sp.dma_start(X[64 * h:64 * h + 64], x1[b, :, HR * h:HR * h + HR, :]).then_inc(x_loaded, 16)
                sp.wait_ge(out_ready, b + 1)
                for h in range(2):
                    sp.dma_start(x2[b, :, HR * h:HR * h + HR, :], T[64 * h:64 * h + 64]).then_inc(x2_stored, 16)
            sp.wait_ge(x2_stored, 32 * B + 1)

        def inner(t):
            return t[:, 1:1 + HR, 1:1 + W]

        def halo(copy, t):
            copy(t[0:64, PR - 1, :], t[64:128, 1, :])
            return copy(t[64:128, 0, :], t[0:64, HR, :])

        @block.scalar
        def _(act):
            act.sem_inc(conv0_ev, 4)
            act.sem_inc(relu_ready, 2)
            with act.Fori(0, B) as b:
                gate(act, negmean_ready, b + 1, passed)
                nc.scalar.activation(inner(Y), X[:, :, :], ACT.Square, bias=st[:, 1:2], accum_out=st[:, 2:3]
                                     ).then_inc(sq_ready, 1)
                act.wait_ge(vare_ready, b + 1)
                nc.scalar.activation(st[:, 4:5], st[:, 3:4], ACT.Sqrt).then_inc(std_ready, 1)
                act.wait_ge(gnp_ready, b + 1)
                nc.scalar.activation(inner(G), X[:, :, :], ACT.Identity, bias=st[:, 6:7], scale=st[:, 5:6]
                                     ).then_inc(gn_ready, 1)
                for n in range(NT):
                    act.wait_ge(conv0_done, b * NT + n + 1)
                    nc.scalar.activation(Y[:, 1 + TR * n:1 + TR * n + TR, 1:1 + W], P[:, n % 4, :].rearrange("p (r w) -> p r w", r=TR),
                                         ACT.Identity, bias=bias[:, 0:1], accum_out=ms[:, n:n + 1]).then_inc(conv0_ev, 1)
                gate(act, dbias_ready, b + 1, passed)
                gate(act, x2_stored, b * 32 + 1, passed)
                for n in range(NT):
                    act.wait_ge(depth_done, b * NT + n + 1)
                    nc.scalar.activation(T[:, TR * n:TR * n + TR, :], P[:, n % 4, :].rearrange("p (r w) -> p r w", r=TR),
                                         ACT.Identity, bias=m3[:, 3:4]).then_inc(depth_ev, 1)
                for n in range(NT):
                    act.wait_ge(acc_done, b * NT + n + 1)
                    if n >= 2:
                        act.wait_ge(filtered, b * NT + n - 1)
                    nc.scalar.activation(RL[:, n % 2], P[:, 4 + n % 2, :].rearrange("p (r w) -> p r w", r=TR),
                                         ACT.Relu, scale=0.8).then_inc(relu_ready, 1)
                for n in range(NT):
                    act.wait_ge(mix_ready, b * NT + n + 1)
                    ins = nc.scalar.activation(T[:, TR * n:TR * n + TR, :], T[:, TR * n:TR * n + TR, :],
                                               ACT.Identity, bias=st[:, 8:9])
                ins.then_inc(out_ready, 1)

        def conv(pe, b, src, wts, done, ready, free, bank0=0):
            for n in range(NT):
                free(n)
                for t, (dy, dx) in enumerate(t9):
                    mm = nc.tensor.matmul(P[:, bank0 + n % 4, :], wts[:, t, :],
                                          src[:, TR * n + dy:TR * n + dy + TR, dx:dx + W], start=t == 0, stop=t == TAPS - 1)
                mm.then_inc(done, 1)

        @block.tensor
        def _(pe):
            pe.wait_ge(const_loaded, 16 * len(consts))
            pe.wait_ge(diag_ready, TAPS)
            pe.wait_ge(weights_loaded, 96)
            with pe.Fori(0, B) as b:
                pe.wait_ge(sum_ready, b + 1)
                nc.tensor.matmul(P[:, 7, 0:1], gsum[:, :], st[:, 0:1], start=True, stop=True).then_inc(mean_ready, 1)
                gate(pe, sq_ready, b + 1, passed)
                pe.wait_ge(negmean_ready, b + 1)
                nc.tensor.matmul(P[:, 7, 0:1], gsum[:, :], st[:, 2:3], start=True, stop=True).then_inc(var_ready, 1)
                gate(pe, gn_ready, b + 1, passed)
                gate(pe, gn_halo, b + 1, passed)
                conv(pe, b, G, W0, conv0_done, None, lambda n: pe.wait_ge(conv0_ev, b * NT + n + 1))
                gate(pe, ysum_ready, b + 1, passed)
                for m in range(3):
                    mm = nc.tensor.matmul(P[:, 7, m:m + 1], shift[:, m, :], st[:, 7:8], start=True, stop=True)
                mm.then_inc(m3_done, 1)
                gate(pe, y_halo, b + 1, passed)
                gate(pe, conv0_ev, b * NT + NT + 4, passed)
                conv(pe, b, Y, DW, depth_done, None, lambda n: pe.wait_ge(depth_ev, b * NT + n - 3) if n >= 4 else None)
                gate(pe, depth_ev, b * NT + NT, passed)
                steps = [(n, t) for n in range(NT) for t in range(TAPS)]
                LAG = 3
                for s in range(len(steps) + LAG):
                    if s < len(steps):
                        n, t = steps[s]
                        if s >= 4:
                            pe.wait_ge(prod_ready, b * NT * TAPS + s - 3)
                        nc.tensor.matmul(P[:, s % 4, :], W3[:, t, :], T[:, TR * n:TR * n + TR, :],
                                         start=True, stop=True).then_inc(fil_done, 1)
                    if s >= LAG:
                        n, t = steps[s - LAG]
                        pe.wait_ge(prod_ready, b * NT * TAPS + s - LAG + 1)
                        if t == 0 and n >= 2:
                            pe.wait_ge(filtered, b * NT + n - 1)
                        mm = nc.tensor.matmul(P[:, 4 + n % 2, :], ident[:, :], PROD[:, (s - LAG) % 4],
                                              start=t == 0, stop=t == TAPS - 1)
                        if t == TAPS - 1:
                            mm.then_inc(acc_done, 1)
                        else:
                            mm.then_inc(prod_used, 1)
                gate(pe, f_halo, b + 1, passed)
                conv(pe, b, G, WF, convf_done, None, lambda n: pe.wait_ge(mix_ready, b * NT + n - 3) if n >= 4 else None)

        @block.vector
        def _(dve):
            v = nc.vector
            for n, t in enumerate((W0, W3, WF)):
                v.memset(t[:, :, :], 0.0).then_inc(cleared, 1)
            v.memset(G[:, :, :], 0.0).then_inc(chain0, 1)
            v.memset(Y[:, :, :], 0.0).then_inc(chain0, 1)
            dve.wait_ge(chain0, 2)
            dve.wait_ge(const_loaded, 16 * len(consts))
            for t in range(TAPS):
                v.tensor_scalar(DW[:, t, :], ident[:, :], w1[:, t:t + 1], None, ALU.mult).then_inc(diag_ready, 1)
            dve.sem_inc(x_used, 1)
            dve.sem_inc(x2_stored, 1)
            with dve.Fori(0, B) as b:
                ch = Chain(dve, chain_dve, b * CPER, CPER)
                dve.wait_ge(x_loaded, b * 32 + 32)
                v.tensor_reduce(st[:, 0:1], X[:, :, :].rearrange("p r w -> p (r w)"), AX_X, ALU.add).then_inc(sum_ready, 1)
                dve.wait_ge(mean_ready, b + 1)
                v.tensor_scalar(st[:, 1:2], P[:, 7, 0:1], -1.0, None, ALU.mult).then_inc(negmean_ready, 1)
                dve.wait_ge(var_ready, b + 1)
                v.tensor_scalar(st[:, 3:4], P[:, 7, 0:1], GN_EPS, None, ALU.add).then_inc(vare_ready, 1)
                dve.wait_ge(std_ready, b + 1)
                ch(v.reciprocal(st[:, 5:6], st[:, 4:5]))
                v.tensor_scalar(st[:, 6:7], st[:, 1:2], st[:, 5:6], None, ALU.mult).then_inc(gnp_ready, 1)
                dve.wait_ge(gnp_ready, b + 1)
                ch(v.tensor_tensor(st[:, 8:9], st[:, 6:7], bias[:, 3:4], ALU.add))
                ch(v.tensor_scalar(st[:, 9:10], st[:, 5:6], 1.0, None, ALU.add))
                dve.wait_ge(gn_ready, b + 1)
                halo(v.tensor_copy, G).then_inc(gn_halo, 1)
                gate(dve, conv0_ev, b * NT + NT + 4, passed)
                halo(v.tensor_copy, Y).then_inc(y_halo, 1)
                v.tensor_reduce(st[:, 7:8], ms[:, :], AX_X, ALU.add).then_inc(ysum_ready, 1)
                dve.wait_ge(m3_done, b + 1)
                ch(v.tensor_tensor(m3[:, 0:3], P[:, 7, 0:3], w2[:, :], ALU.mult))
                ch(v.tensor_reduce(m3[:, 3:4], m3[:, 0:3], AX_X, ALU.add))
                v.tensor_scalar(m3[:, 3:4], m3[:, 3:4], bias[:, 1:2], bias[:, 2:3], ALU.add, ALU.add).then_inc(dbias_ready, 1)

                def leaky(n):
                    dve.wait_ge(relu_ready, b * NT + n + 3)
                    v.scalar_tensor_tensor(G[:, 1 + TR * n:1 + TR * n + TR, 1:1 + W],
                                           P[:, 4 + n % 2, :].rearrange("p (r w) -> p r w", r=TR), 0.2,
                                           RL[:, n % 2], ALU.mult, ALU.add).then_inc(filtered, 1)
                for n in range(NT):
                    for t, (dy, dx) in enumerate(t9):
                        s = n * TAPS + t
                        dve.wait_ge(fil_done, b * NT * TAPS + s + 1)
                        if s >= 4:
                            n4, t4 = (s - 4) // TAPS, (s - 4) % TAPS
                            if t4 == TAPS - 1:
                                dve.wait_ge(acc_done, b * NT + n4 + 1)
                            else:
                                dve.wait_ge(prod_used, b * NT * (TAPS - 1) + n4 * (TAPS - 1) + t4 + 1)
                        v.scalar_tensor_tensor(PROD[:, s % 4], P[:, s % 4, :].rearrange("p (r w) -> p r w", r=TR), b3[:, t:t + 1],
                                               Y[:, TR * n + dy:TR * n + dy + TR, dx:dx + W], ALU.add, ALU.mult
                                               ).then_inc(prod_ready, 1)
                        if t == 5 and n >= 1:
                            leaky(n - 1)
                leaky(NT - 1)
                dve.wait_ge(filtered, b * NT + NT)
                halo(v.tensor_copy, G).then_inc(f_halo, 1)
                for n in range(NT):
                    dve.wait_ge(convf_done, b * NT + n + 1)
                    v.scalar_tensor_tensor(T[:, TR * n:TR * n + TR, :], X[:, TR * n:TR * n + TR, :], st[:, 9:10],
                                           P[:, n % 4, :].rearrange("p (r w) -> p r w", r=TR), ALU.mult, ALU.add
                                           ).then_inc(mix_ready, 1)
                gate(dve, mix_ready, b * NT + NT, passed)
                dve.sem_inc(x_used, 1)
                ch.done()



S1, S2 = 32, 16


def layer2_small(nc, B, x2, y2, k):
    PRS = B // 2
    with phase(nc) as named, ExitStack() as ctx:
        def sb(name, shape, dt=F32):
            return ctx.enter_context(nc.sbuf_tensor("c_" + name, shape, dt))

        def sem(name):
            return named("c_" + name)

        X = sb("X", [128, 2, NPX])
        SQ = sb("SQ", [128, NPX // 4])
        WTS = sb("WTS", [128, 12, TAPS, 128])
        bias = sb("bias", [128, 12])
        gsum = sb("gsum", [128, 128])
        POOL1 = sb("POOL1", [128, HR, S1])
        POOL2 = sb("POOL2", [128, S1 // 2, S1])
        YP = sb("YP", [128, PRS, S1 + 2, S1 + 2])
        HP = sb("HP", [128, PRS, S1 + 2, S1 + 2])
        YQ = sb("YQ", [128, PRS, S2 + 2, S2 + 2])
        HQ = sb("HQ", [128, PRS, S2 + 2, S2 + 2])
        MX = sb("MX", [128, S1, S2])
        YE = sb("YE", [128, PRS, S2 + 2, S2])
        st = sb("st", [128, 16])
        sq4 = sb("sq4", [128, 4])
        P = ctx.enter_context(nc.psum_tensor("c_P", [128, 8, 512], F32))
        const_loaded = sem("const_loaded")
        cleared = sem("cleared")
        weights_loaded = sem("weights_loaded")
        x_loaded = [sem("x_loaded0"), sem("x_loaded1")]
        x_used = sem("x_used")
        chain_dve = sem("chain_dve")
        chain_tail = sem("chain_tail")
        passed = sem("passed")
        sum_ready = sem("sum_ready")
        mean_ready = sem("mean_ready")
        negmean_ready = sem("negmean_ready")
        sq_ready = sem("sq_ready")
        sqsum_ready = sem("sqsum_ready")
        var_ready = sem("var_ready")
        vare_ready = sem("vare_ready")
        std_ready = sem("std_ready")
        pooled = sem("pooled")
        conv_done = sem("conv_done")
        hid_ev = sem("hid_ev")
        hid_ready = sem("hid_ready")
        res_ready = sem("res_ready")
        maxed = sem("maxed")
        y2_ready = sem("y2_ready")
        y2_stored = sem("y2_stored")
        block = ctx.enter_context(nc.Block())
        n_items = {1: PRS * 2, 2: (PRS + 1) // 2}
        steps = [(bl, la, cv, it) for bl in (1, 2) for la in range(3) for cv in (0, 1) for it in range(n_items[bl])]

        def src_dst(bl, cv, it):
            if bl == 1:
                pr, tile = it // 2, it % 2
                s = (YP, HP)[cv][:, pr]
                d = (HP, YP)[cv][:, pr, 1 + 16 * tile:17 + 16 * tile, 1:1 + S1]
                return (lambda dy, dx: s[:, 16 * tile + dy:16 * tile + dy + 16, dx:dx + S1]), d, 512
            p0, p1 = 2 * it, min(2 * it + 2, PRS)
            s, d = ((YQ, HQ) if cv == 0 else (HQ, YQ))
            return (lambda dy, dx: s[:, p0:p1, dy:dy + S2, dx:dx + S2]), d[:, p0:p1, 1:1 + S2, 1:1 + S2], 256 * (p1 - p0)

        def psum(s, n, bl):
            o = P[:, s % 8, 0:n]
            return o.rearrange("p (r w) -> p r w", w=S1) if bl == 1 else o.rearrange("p (a r w) -> p a r w", r=S2, w=S2)

        hid_before = [sum(1 for q in steps[:s] if q[2] == 0) for s in range(len(steps) + 1)]
        res_before = [sum(1 for q in steps[:s] if q[2] == 1) for s in range(len(steps) + 1)]

        @block.sync
        def _(sp):
            sp.dma_start(gsum[:], k["gsum"]).then_inc(const_loaded, 16)
            sp.dma_start(bias[:], k["bias2"]).then_inc(const_loaded, 16)
            with sp.Fori(0, PRS) as pr:
                for bb in range(2):
                    sp.wait_ge(x_used, pr * 2 + bb + 1)
                    for h in range(2):
                        sp.dma_start(X[64 * h:64 * h + 64, bb], x2[pr * 2 + bb, :, HR * h:HR * h + HR, :].rearrange("c r w -> c (r w)")
                                     ).then_inc(x_loaded[bb], 16)
            sp.wait_ge(y2_ready, 1)
            for b in range(B):
                sp.dma_start(y2[b], YE[64 * (b % 2):64 * (b % 2) + 64, b // 2]).then_inc(y2_stored, 16)
            sp.wait_ge(y2_stored, 16 * B)

        @block.scalar
        def _(act):
            act.wait_ge(cleared, 1)
            for h in range(2):
                act.dma_start(WTS[64 * h:64 * h + 64, :, :, 64 * h:64 * h + 64].rearrange("p a t c -> p (a t) c"),
                              k["blocks"]).then_inc(weights_loaded, 16)
            with act.Fori(0, PRS) as pr:
                for bb in range(2):
                    b = pr * 2 + bb
                    act.wait_ge(negmean_ready, b + 1)
                    for m in range(4):
                        if m:
                            act.wait_ge(sq_ready, b * 4 + m)
                        nc.scalar.activation(SQ[:, :], X[:, bb, m * (NPX // 4):(m + 1) * (NPX // 4)], ACT.Square,
                                             bias=st[:, 1:2], accum_out=sq4[:, m:m + 1]).then_inc(sq_ready, 1)
                    act.wait_ge(vare_ready, b + 1)
                    nc.scalar.activation(st[:, 4:5], st[:, 3:4], ACT.Sqrt).then_inc(std_ready, 1)
            for s, (bl, la, cv, it) in enumerate(steps):
                if cv == 0:
                    _, d, n = src_dst(bl, cv, it)
                    w = (bl - 1) * 6 + la * 2
                    act.wait_ge(conv_done, s + 1)
                    nc.scalar.activation(d, psum(s, n, bl), ACT.Identity, bias=bias[:, w:w + 1]).then_inc(hid_ev, 1)

        @block.tensor
        def _(pe):
            pe.wait_ge(const_loaded, 32)
            with pe.Fori(0, PRS) as pr:
                for bb in range(2):
                    b = pr * 2 + bb
                    pe.wait_ge(sum_ready, b + 1)
                    nc.tensor.matmul(P[:, 0, 0:1], gsum[:, :], st[:, 0:1], start=True, stop=True).then_inc(mean_ready, 1)
                    pe.wait_ge(sqsum_ready, b + 1)
                    nc.tensor.matmul(P[:, 0, 0:1], gsum[:, :], st[:, 2:3], start=True, stop=True).then_inc(var_ready, 1)
            pe.wait_ge(weights_loaded, 32)
            pe.wait_ge(pooled, B)
            for s, (bl, la, cv, it) in enumerate(steps):
                f, _, n = src_dst(bl, cv, it)
                w = (bl - 1) * 6 + la * 2 + cv
                if s >= 8:
                    if steps[s - 8][2] == 0:
                        pe.wait_ge(hid_ev, hid_before[s - 7])
                    else:
                        pe.wait_ge(res_ready, res_before[s - 7])
                first = s - it
                if bl == 2 and la == 0 and cv == 0:
                    pe.wait_ge(maxed, 1)
                need = first - n_items[bl] + (it // 2 * 2 + 2 if bl == 1 else it + 1)
                if cv == 1:
                    pe.wait_ge(hid_ready, hid_before[need])
                elif la > 0:
                    pe.wait_ge(res_ready, res_before[need])
                for t in range(TAPS):
                    mm = nc.tensor.matmul(P[:, s % 8, 0:n], WTS[:, w, t, :], f(t // 3, t % 3), start=t == 0, stop=t == TAPS - 1)
                mm.then_inc(conv_done, 1)

        @block.vector
        def _(dve):
            v = nc.vector
            v.memset(WTS[:, :, :, :], 0.0).then_inc(cleared, 1)
            for t in (YP, HP, YQ, HQ):
                v.memset(t[:, :, :, :], 0.0).then_inc(chain_tail, 1)
            dve.wait_ge(chain_tail, 4)
            dve.sem_inc(x_used, 2)
            with dve.Fori(0, PRS) as pr:
                for bb in range(2):
                    b = pr * 2 + bb
                    CPER = 7
                    ch = Chain(dve, chain_dve, b * CPER, CPER)
                    dve.wait_ge(x_loaded[bb], pr * 32 + 32)
                    ch(v.tensor_reduce(POOL1[:, :, :], X[:, bb].rearrange("p (r q w) -> p r q w", r=HR, q=S1), AX_X, ALU.add))
                    ch(v.tensor_reduce(POOL2[:, :, :], POOL1[:, :, :].rearrange("p (a r) q -> p a q r", r=4), AX_X, ALU.add))
                    v.tensor_reduce(st[:, 0:1], POOL2[:, :, :].rearrange("p a q -> p (a q)"), AX_X, ALU.add).then_inc(sum_ready, 1)
                    dve.wait_ge(mean_ready, b + 1)
                    v.tensor_scalar(st[:, 1:2], P[:, 0, 0:1], -1.0, None, ALU.mult).then_inc(negmean_ready, 1)
                    dve.wait_ge(sq_ready, b * 4 + 4)
                    dve.sem_inc(x_used, 1)
                    v.tensor_reduce(st[:, 2:3], sq4[:, :], AX_X, ALU.add).then_inc(sqsum_ready, 1)
                    dve.wait_ge(var_ready, b + 1)
                    v.tensor_scalar(st[:, 3:4], P[:, 0, 0:1], GN_EPS, None, ALU.add).then_inc(vare_ready, 1)
                    dve.wait_ge(std_ready, b + 1)
                    ch(v.reciprocal(st[:, 5:6], st[:, 4:5]))
                    ch(v.tensor_scalar(st[:, 6:7], st[:, 1:2], st[:, 5:6], None, ALU.mult))
                    ch(v.tensor_scalar(st[:, 7:8], st[:, 5:6], 1.0 / 16, None, ALU.mult))
                    for h in range(2):
                        ins = v.tensor_scalar(YP[64 * bb:64 * bb + 64, pr, 1 + 16 * h:17 + 16 * h, 1:1 + S1],
                                              POOL2[64 * h:64 * h + 64], st[64 * h:64 * h + 64, 7:8],
                                              st[64 * h:64 * h + 64, 6:7], ALU.mult, ALU.add)
                        if h == 0:
                            ch(ins)
                        else:
                            ins.then_inc(pooled, 1)
                    dve.wait_ge(pooled, b + 1)
                    ch(v.tensor_copy(st[:, 8:9], st[:, 7:8]))
                    ch.done()
            for s, (bl, la, cv, it) in enumerate(steps):
                if bl == 2 and la == 0 and cv == 0 and it == 0:
                    dve.wait_ge(res_ready, res_before[s])
                    for pr in range(PRS):
                        yi = YP[:, pr, 1:1 + S1, 1:1 + S1]
                        v.tensor_tensor(MX[:, :, :], yi[:, :, 0:S1:2], yi[:, :, 1:S1:2], ALU.max).then_inc(chain_tail, 1)
                        dve.wait_ge(chain_tail, 4 + 2 * pr + 1)
                        v.tensor_tensor(YQ[:, pr, 1:1 + S2, 1:1 + S2], MX[:, 0:S1:2, :], MX[:, 1:S1:2, :], ALU.max
                                        ).then_inc(chain_tail, 1)
                        dve.wait_ge(chain_tail, 4 + 2 * pr + 2)
                    dve.sem_inc(maxed, 1)
                _, d, n = src_dst(bl, cv, it)
                if cv == 0:
                    dve.wait_ge(hid_ev, hid_before[s + 1])
                    items = [d] if bl == 1 else [d[:, q] for q in range(n // 256)]
                    for e in items:
                        ins = v.scalar_tensor_tensor(e, e, 0.1, e, ALU.mult, ALU.max)
                    ins.then_inc(hid_ready, 1)
                else:
                    w = (bl - 1) * 6 + la * 2 + 1
                    dve.wait_ge(conv_done, s + 1)
                    o = psum(s, n, bl)
                    items = [(d, o)] if bl == 1 else [(d[:, q], o[:, q]) for q in range(n // 256)]
                    for e, ps in items:
                        ins = v.scalar_tensor_tensor(e, ps, bias[:, w:w + 1], e, ALU.add, ALU.add)
                    ins.then_inc(res_ready, 1)
            dve.wait_ge(res_ready, res_before[-1])
            base = 4 + 2 * PRS
            v.tensor_copy(YE[:, :, 1:1 + S2, :], YQ[:, :, 1:1 + S2, 1:1 + S2]).then_inc(chain_tail, 1)
            v.tensor_copy(YE[:, :, 0, :], YQ[:, :, 1, 1:1 + S2]).then_inc(chain_tail, 1)
            v.tensor_copy(YE[:, :, S2 + 1, :], YQ[:, :, S2, 1:1 + S2]).then_inc(chain_tail, 1)
            dve.wait_ge(chain_tail, base + 3)
            dve.sem_inc(y2_ready, 1)


def layer2_apply(nc, B, x2, y2, x3, g3, k):
    NAP = S2 + 1
    CPER = 5
    with phase(nc) as named, ExitStack() as ctx:
        def sb(name, shape, dt=F32):
            return ctx.enter_context(nc.sbuf_tensor("d_" + name, shape, dt))

        def sem(name):
            return named("d_" + name)

        X = sb("X", [128, HR, W])
        G = sb("G", [128, PR, PW])
        T = sb("T", [128, HR, W])
        WT = sb("WT", [32, NAP // 2 + 1, TAPS, 2, C])
        U = sb("U", [32, 2, 512])
        YE = sb("YE", [C, S2 + 2, S2])
        tok = sb("tok", [C, TAPS * C])
        tokb = sb("tokb", [1, TAPS * C])
        one = sb("one", [1, 32])
        ident = sb("ident", [128, 128])
        gsum = sb("gsum", [128, 128])
        st = sb("st", [128, 16])
        PROD = sb("PROD", [128, 4, TR, W])
        P = ctx.enter_context(nc.psum_tensor("d_P", [128, 8, 512], F32))
        const_loaded = sem("const_loaded")
        x_loaded = sem("x_loaded")
        y_loaded = sem("y_loaded")
        x_used = sem("x_used")
        y_used = sem("y_used")
        x3_stored = sem("x3_stored")
        g3_stored = sem("g3_stored")
        x3_ready = sem("x3_ready")
        passed = sem("passed")
        chain_dve = sem("chain_dve")
        sum_ready = sem("sum_ready")
        mean_ready = sem("mean_ready")
        negmean_ready = sem("negmean_ready")
        sq_ready = sem("sq_ready")
        var_ready = sem("var_ready")
        vare_ready = sem("vare_ready")
        std_ready = sem("std_ready")
        gnp_ready = sem("gnp_ready")
        gn_ready = sem("gn_ready")
        wt_done = sem("wt_done")
        wt_ev = sem("wt_ev")
        fil_done = sem("fil_done")
        prod_ready = sem("prod_ready")
        prod_used = sem("prod_used")
        acc_done = sem("acc_done")
        acc_ev = sem("acc_ev")
        g3_ready = sem("g3_ready")
        consts = [(ident, "ident"), (gsum, "gsum"), (U, "U"), (tok, "tok"), (tokb, "tokb"), (one, "one")]
        block = ctx.enter_context(nc.Block())
        def inner(t):
            return t[:, 1:1 + HR, 1:1 + W]

        @block.sync
        def _(sp):
            for t, name in consts:
                sp.dma_start(t[:], k[name]).then_inc(const_loaded, 16)
            with sp.Fori(0, B) as b:
                sp.wait_ge(y_used, b + 1)
                sp.dma_start(YE[:, :, :], y2[b]).then_inc(y_loaded, 16)
                sp.wait_ge(x_used, b + 1)
                for h in range(2):
                    sp.dma_start(X[64 * h:64 * h + 64], x2[b, :, HR * h:HR * h + HR, :]).then_inc(x_loaded, 16)
                sp.wait_ge(x3_ready, b + 1)
                for h in range(2):
                    sp.dma_start(x3[b, HR * h:HR * h + HR, :, :].rearrange("y c x -> c y x"), T[64 * h:64 * h + 64]
                                 ).then_inc(x3_stored, 16)
                sp.wait_ge(g3_ready, b + 1)
                for h in range(2):
                    sp.dma_start(g3[b, HR * h:HR * h + HR, :, :].rearrange("y c x -> c y x"), inner(G)[64 * h:64 * h + 64]
                                 ).then_inc(g3_stored, 16)
            sp.wait_ge(x3_stored, 32 * B + 1)
            sp.wait_ge(g3_stored, 32 * B + 1)

        @block.scalar
        def _(act):
            with act.Fori(0, B) as b:
                gate(act, negmean_ready, b * 2 + 1, passed)
                gate(act, x3_stored, b * 32 + 1, passed)
                gate(act, g3_stored, b * 32 + 1, passed)
                nc.scalar.activation(inner(G), X[:, :, :], ACT.Square, bias=st[:, 1:2], accum_out=st[:, 2:3]
                                     ).then_inc(sq_ready, 1)
                act.wait_ge(vare_ready, b * 2 + 1)
                nc.scalar.activation(st[:, 4:5], st[:, 3:4], ACT.Sqrt).then_inc(std_ready, 1)
                act.wait_ge(gnp_ready, b * 2 + 1)
                nc.scalar.activation(inner(G), X[:, :, :], ACT.Identity, bias=st[:, 6:7], scale=st[:, 5:6]
                                     ).then_inc(gn_ready, 1)
                for a in range(NAP):
                    act.wait_ge(wt_done, b * NAP + a + 1)
                    for h in range(2):
                        if h * 8 <= a <= h * 8 + 8:
                            for u in range(2):
                                n0, n1 = (0, 5) if u == 0 else (5, TAPS)
                                ins = nc.scalar.activation(
                                    WT[:, a - 8 * h, n0:n1, h, :],
                                    P[0:32, (2 * a + u) % 4, 0:(n1 - n0) * C].rearrange("p (t c) -> p t c", c=C), ACT.Copy)
                    ins.then_inc(wt_ev, 1)
                act.wait_ge(negmean_ready, b * 2 + 2)
                nc.scalar.activation(inner(G), T[:, :, :], ACT.Square, bias=st[:, 1:2], accum_out=st[:, 2:3]
                                     ).then_inc(sq_ready, 1)
                act.wait_ge(vare_ready, b * 2 + 2)
                nc.scalar.activation(st[:, 4:5], st[:, 3:4], ACT.Sqrt).then_inc(std_ready, 1)
                act.wait_ge(gnp_ready, b * 2 + 2)
                nc.scalar.activation(inner(G), T[:, :, :], ACT.Identity, bias=st[:, 6:7], scale=st[:, 5:6]
                                     ).then_inc(g3_ready, 1)

        @block.tensor
        def _(pe):
            pe.wait_ge(const_loaded, 16 * len(consts))

            def stats(n):
                gate(pe, sum_ready, n + 1, passed)
                nc.tensor.matmul(P[:, 7, 0:1], gsum[:, :], st[:, 0:1], start=True, stop=True).then_inc(mean_ready, 1)
                gate(pe, sq_ready, n + 1, passed)
                nc.tensor.matmul(P[:, 7, 0:1], gsum[:, :], st[:, 2:3], start=True, stop=True).then_inc(var_ready, 1)

            with pe.Fori(0, B) as b:
                stats(b * 2)
                gate(pe, y_loaded, b * 16 + 16, passed)
                for a in range(NAP):
                    if a >= 2:
                        gate(pe, wt_ev, b * NAP + a - 1, passed)
                    for u in range(2):
                        n0, n1 = (0, 5 * C) if u == 0 else (5 * C, TAPS * C)
                        o = P[0:32, (2 * a + u) % 4, 0:n1 - n0]
                        nc.tensor.matmul(o, YE[:, a:a + 2, :].rearrange("p a w -> p (a w)"), tok[:, n0:n1],
                                         start=True, stop=False)
                        mm = nc.tensor.matmul(o, one[:, :], tokb[:, n0:n1], start=False, stop=True)
                    mm.then_inc(wt_done, 1)
                gate(pe, gn_ready, b + 1, passed)
                gate(pe, wt_ev, b * NAP + NAP, passed)
                steps = [(n, t) for n in range(NT) for t in range(TAPS)]
                LAG = 3
                for s in range(len(steps) + LAG):
                    if s < len(steps):
                        n, t = steps[s]
                        if s >= 4:
                            gate(pe, prod_ready, b * NT * TAPS + s - 3, passed)
                        a = (n + 1) // 2
                        nc.tensor.matmul(P[:, s % 4, :], WT[:, a, t].rearrange("p h c -> p (h c)"), U[:, n % 2, :],
                                         start=True, stop=True).then_inc(fil_done, 1)
                    if s >= LAG:
                        n, t = steps[s - LAG]
                        pe.wait_ge(prod_ready, b * NT * TAPS + s - LAG + 1)
                        if t == 0 and n >= 2:
                            pe.wait_ge(acc_ev, b * NT + n - 1)
                        mm = nc.tensor.matmul(P[:, 4 + n % 2, :], ident[:, :], PROD[:, (s - LAG) % 4],
                                              start=t == 0, stop=t == TAPS - 1)
                        if t == TAPS - 1:
                            mm.then_inc(acc_done, 1)
                        else:
                            mm.then_inc(prod_used, 1)
                stats(b * 2 + 1)

        @block.vector
        def _(dve):
            v = nc.vector
            dve.sem_inc(x_used, 1)
            dve.sem_inc(y_used, 1)
            dve.sem_inc(x3_stored, 1)
            dve.sem_inc(g3_stored, 1)
            with dve.Fori(0, B) as b:
                ch = Chain(dve, chain_dve, b * CPER, CPER)

                def stats(n, t):
                    v.tensor_reduce(st[:, 0:1], t[:, :, :].rearrange("p r w -> p (r w)"), AX_X, ALU.add).then_inc(sum_ready, 1)
                    dve.wait_ge(mean_ready, n + 1)
                    v.tensor_scalar(st[:, 1:2], P[:, 7, 0:1], -1.0, None, ALU.mult).then_inc(negmean_ready, 1)
                    dve.wait_ge(var_ready, n + 1)
                    v.tensor_scalar(st[:, 3:4], P[:, 7, 0:1], GN_EPS, None, ALU.add).then_inc(vare_ready, 1)
                    dve.wait_ge(std_ready, n + 1)
                    ch(v.reciprocal(st[:, 5:6], st[:, 4:5]))
                    v.tensor_scalar(st[:, 6:7], st[:, 1:2], st[:, 5:6], None, ALU.mult).then_inc(gnp_ready, 1)

                dve.wait_ge(x_loaded, b * 32 + 32)
                stats(b * 2, X)
                dve.wait_ge(gn_ready, b + 1)
                ch(v.tensor_copy(G[:, 1:1 + HR, 0:1], G[:, 1:1 + HR, 1:2]))
                ch(v.tensor_copy(G[:, 1:1 + HR, PW - 1:PW], G[:, 1:1 + HR, PW - 2:PW - 1]))
                v.tensor_copy(G[0:64, 0, :], G[0:64, 1, :])
                v.tensor_copy(G[64:128, PR - 1, :], G[64:128, PR - 2, :])
                v.tensor_copy(G[0:64, PR - 1, :], G[64:128, 1, :])
                ch(v.tensor_copy(G[64:128, 0, :], G[0:64, HR, :]))

                def total(n):
                    dve.wait_ge(acc_done, b * NT + n + 1)
                    if n == 0:
                        dve.wait_ge(x3_stored, b * 32 + 1)
                    v.tensor_tensor(T[:, TR * n:TR * n + TR, :], P[:, 4 + n % 2, :].rearrange("p (r w) -> p r w", r=TR),
                                    X[:, TR * n:TR * n + TR, :], ALU.add).then_inc(acc_ev, 1)
                for n in range(NT):
                    for t in range(TAPS):
                        dy, dx = t // 3, t % 3
                        s = n * TAPS + t
                        dve.wait_ge(fil_done, b * NT * TAPS + s + 1)
                        if s >= 4:
                            n4, t4 = (s - 4) // TAPS, (s - 4) % TAPS
                            if t4 == TAPS - 1:
                                dve.wait_ge(acc_done, b * NT + n4 + 1)
                            else:
                                dve.wait_ge(prod_used, b * NT * (TAPS - 1) + n4 * (TAPS - 1) + t4 + 1)
                        v.tensor_tensor(PROD[:, s % 4], P[:, s % 4, :].rearrange("p (r w) -> p r w", r=TR),
                                        G[:, TR * n + dy:TR * n + dy + TR, dx:dx + W], ALU.mult).then_inc(prod_ready, 1)
                        if t == 5 and n >= 1:
                            total(n - 1)
                total(NT - 1)
                dve.wait_ge(acc_ev, b * NT + NT)
                dve.sem_inc(x_used, 1)
                dve.sem_inc(y_used, 1)
                dve.sem_inc(x3_ready, 1)
                stats(b * 2 + 1, T)
                ch.done()



NM = 16
NF = 2 * NM
UP = 2.0 ** 30


def layer3_modes(nc, B, g3, modes, k):
    MB = 64
    NCH = NF * NM // MB
    with phase(nc) as named, ExitStack() as ctx:
        def sb(name, shape, dt=F32):
            return ctx.enter_context(nc.sbuf_tensor("e_" + name, shape, dt))

        def sem(name):
            return named("e_" + name)

        GY = sb("GY", [128, 2, C, W])
        T1 = sb("T1", [128, 2, C, NF])
        XM = sb("XM", [128, NF * NM, B])
        WA = sb("WA", [128, 2, MB * C])
        WN = sb("WN", [128, 2, MB * C])
        OM = sb("OM", [C, NF, NM, B])
        OF = sb("OF", [NF, 2, C, NM])
        crow = sb("crow", [128, NF])
        ccol = sb("ccol", [128, 2, NM])
        sign = sb("sign", [128, 1])
        ident = sb("ident", [128, 128])
        P = ctx.enter_context(nc.psum_tensor("e_P", [128, 8, 512], F32))
        const_loaded = sem("const_loaded")
        g_loaded = [sem("g_loaded0"), sem("g_loaded1")]
        w_loaded = [sem("w_loaded0"), sem("w_loaded1")]
        rows_done = sem("rows_done")
        rows_ev = sem("rows_ev")
        cols_done = sem("cols_done")
        cols_ev = sem("cols_ev")
        w_ready = sem("w_ready")
        mix_done = sem("mix_done")
        mix_ev = sem("mix_ev")
        turn_done = sem("turn_done")
        turn_ev = sem("turn_ev")
        modes_stored = [sem("modes_stored0"), sem("modes_stored1")]
        passed = sem("passed")
        consts = [(crow, "crow"), (ccol, "ccol"), (sign, "sign"), (ident, "ident")]
        block = ctx.enter_context(nc.Block())

        @block.sync
        def _(sp):
            for t, name in consts:
                sp.dma_start(t[:], k[name]).then_inc(const_loaded, 16)
            for b in range(B):
                if b >= 2:
                    sp.wait_ge(rows_done, (b - 1) * 4)
                sp.dma_start(GY[:, b % 2], g3[b]).then_inc(g_loaded[b % 2], 16)
            for b in range(B):
                sp.wait_ge(turn_ev, 2 * b + 2)
                sp.dma_start(modes[b], OF[:, b % 2].rearrange("p o g -> p (o g)")).then_inc(modes_stored[b % 2], 16)
            for n in range(2):
                sp.wait_ge(modes_stored[n], 16 * (B // 2))

        @block.gpsimd
        def _(pool):
            for n in range(NCH):
                if n >= 2:
                    pool.wait_ge(mix_done, n - 1)
                for t, name in ((WA, "w_at"), (WN, "w_neg")):
                    for h in range(2):
                        pool.dma_start(t[64 * h:64 * h + 64, n % 2, :], k[name][:, n * MB * C:(n + 1) * MB * C]
                                       ).then_inc(w_loaded[n % 2], 16)

        @block.tensor
        def _(pe):
            pe.wait_ge(const_loaded, 16 * len(consts))
            for b in range(B):
                pe.wait_ge(g_loaded[b % 2], 16 * (b // 2) + 16)
                for q in range(4):
                    n = b * 4 + q
                    if n >= 4:
                        pe.wait_ge(rows_ev, n - 3)
                    for c in range(16):
                        mm = nc.tensor.matmul(P[:, q, NF * c:NF * c + NF], GY[:, b % 2, q * 16 + c, :], crow[:, :],
                                              start=True, stop=True)
                    mm.then_inc(rows_done, 1)
                pe.wait_ge(rows_ev, 4 * b + 4)
                if b >= 2:
                    pe.wait_ge(cols_ev, b - 1)
                for s in range(2):
                    for f in range(NF):
                        fs = f if s == 0 else f // NM * NM + (-f) % NM
                        mm = nc.tensor.matmul(P[64 * s:64 * s + 64, 4 + b % 2, NM * f:NM * f + NM], T1[:, b % 2, :, fs],
                                              ccol[:, s, :], start=True, stop=True)
                mm.then_inc(cols_done, 1)
            pe.wait_ge(cols_ev, B)
            for n in range(NCH):
                pe.wait_ge(w_ready, n + 1)
                if n >= 2:
                    pe.wait_ge(mix_ev, n - 1)
                for m in range(MB):
                    mm = nc.tensor.matmul(P[0:64, 6 + n % 2, B * m:B * m + B], WA[:, n % 2, C * m:C * m + C],
                                          XM[:, n * MB + m, :], start=True, stop=True)
                mm.then_inc(mix_done, 1)
            pe.wait_ge(mix_ev, NCH)
            for n in range(2 * B):
                if n >= 4:
                    pe.wait_ge(turn_ev, n - 3)
                for g in range(8):
                    mm = nc.tensor.transpose(P[0:NF, n % 4, C * g:C * g + C], OM[:, :, (n % 2) * 8 + g, n // 2], ident[0:C, 0:C])
                mm.then_inc(turn_done, 1)

        @block.scalar
        def _(act):
            for b in range(B):
                for q in range(4):
                    act.wait_ge(rows_done, b * 4 + q + 1)
                    if b >= 2:
                        act.wait_ge(cols_done, b - 1)
                    nc.scalar.activation(T1[:, b % 2, 16 * q:16 * q + 16, :], P[:, q, :].rearrange("p (c f) -> p c f", f=NF),
                                         ACT.Copy).then_inc(rows_ev, 1)

        @block.vector
        def _(dve):
            v = nc.vector
            dve.wait_ge(const_loaded, 16 * len(consts))
            for b in range(B):
                dve.wait_ge(cols_done, b + 1)
                v.tensor_copy(XM[:, :, b], P[:, 4 + b % 2, :]).then_inc(cols_ev, 1)
            for n in range(NCH):
                dve.wait_ge(w_loaded[n % 2], 64 * (n // 2) + 64)
                v.scalar_tensor_tensor(WA[:, n % 2], WN[:, n % 2], sign[:, 0:1], WA[:, n % 2], ALU.mult, ALU.add
                                       ).then_inc(w_ready, 1)
                if n >= 1:
                    dve.wait_ge(mix_done, n)
                    v.tensor_copy(OM[:, :, :, :].rearrange("p f g b -> p (f g b)")[:, MB * B * (n - 1):MB * B * n], P[0:64, 6 + (n - 1) % 2, 0:MB * B]
                                  ).then_inc(mix_ev, 1)
            dve.wait_ge(mix_done, NCH)
            v.tensor_copy(OM[:, :, :, :].rearrange("p f g b -> p (f g b)")[:, MB * B * (NCH - 1):], P[0:64, 6 + (NCH - 1) % 2, 0:MB * B]
                          ).then_inc(mix_ev, 1)
            for n in range(2 * B):
                dve.wait_ge(turn_done, n + 1)
                if n >= 4:
                    dve.wait_ge(modes_stored[n // 2 % 2], 16 * (n // 4))
                v.tensor_copy(OF[:, n // 2 % 2, :, (n % 2) * 8:(n % 2) * 8 + 8], P[0:NF, n % 4, :].rearrange("p (g o) -> p o g", o=C)
                              ).then_inc(turn_ev, 1)


def layer3_phase(nc, B, x3, g3, modes, out, k):
    CG = 4
    NG = C // CG
    with phase(nc) as named, ExitStack() as ctx:
        def sb(name, shape, dt=F32):
            return ctx.enter_context(nc.sbuf_tensor("f_" + name, shape, dt))

        def sem(name):
            return named("f_" + name)

        XY = sb("XY", [128, 2, C, W])
        GY = sb("GY", [128, 2, C, W])
        MO = sb("MO", [NF, 2, C * NM])
        T2 = sb("T2", [128, 2, CG, 2 * W])
        SC = sb("SC", [128, 2, CG * W])
        SS = sb("SS", [128, 2, CG * W])
        ZZ = sb("ZZ", [128, 2, CG * W])
        RT = sb("RT", [128, 2, CG * W])
        IV = sb("IV", [128, 2, 128])
        cas2 = sb("cas2", [128, 2 * W])
        casup = sb("casup", [128, 2 * W])
        cinv1 = sb("cinv1", [NF, W])
        cblk = sb("cblk", [128, 2, CG * W])
        P = ctx.enter_context(nc.psum_tensor("f_P", [128, 8, 512], F32))
        const_loaded = sem("const_loaded")
        loaded = [sem("loaded0"), sem("loaded1")]
        stored = sem("stored")
        passed = sem("passed")
        batch_free = sem("batch_free")
        first_done = sem("first_done")
        first_ev = sem("first_ev")
        second_done = sem("second_done")
        inv1_done = sem("inv1_done")
        inv1_ev = sem("inv1_ev")
        inv2_done = sem("inv2_done")
        cos_sq = sem("cos_sq")
        sin_sq = sem("sin_sq")
        root_ready = sem("root_ready")
        squares_ready = sem("squares_ready")
        step = sem("step")
        cos_read = sem("cos_read")
        y_read = sem("y_read")
        slots_used = sem("slots_used")
        out_ready = sem("out_ready")
        consts = [(cas2, "cas2"), (casup, "casup"), (cinv1, "cinv1"), (cblk, "cblk")]
        block = ctx.enter_context(nc.Block())
        PRS = B // 2

        @block.sync
        def _(sp):
            for t, name in consts:
                sp.dma_start(t[:], k[name]).then_inc(const_loaded, 16)

            def load(b, bb):
                sp.dma_start(GY[:, bb], g3[b]).then_inc(loaded[bb], 16)
                sp.dma_start(XY[:, bb], x3[b]).then_inc(loaded[bb], 16)
                sp.dma_start(MO[:, bb], modes[b]).then_inc(loaded[bb], 16)
            for b in range(B):
                if b < 2:
                    load(b, b % 2)
            for b in range(B):
                sp.wait_ge(out_ready, b * NG + NG)
                sp.dma_start(out[b].rearrange("c y x -> y c x"), XY[:, b % 2]).then_inc(stored, 16)
                if b + 2 < B:
                    sp.wait_ge(stored, 16 * b + 16)
                    load(b + 2, b % 2)
            sp.wait_ge(stored, 16 * B)

        @block.tensor
        def _(pe):
            pe.wait_ge(const_loaded, 16 * len(consts))
            with pe.Fori(0, PRS) as pr:
                for bb in range(2):
                    def first(i):
                        n = (pr * 2 + bb) * NG + i
                        gate(pe, first_ev, n + 1, passed)
                        for c in range(CG):
                            mm = nc.tensor.matmul(P[:, c // 2, (c % 2) * 256:(c % 2) * 256 + 256], GY[:, bb, i * CG + c, :],
                                                  cas2[:, :], start=True, stop=True)
                        mm.then_inc(first_done, 1)

                    def second(i):
                        n = (pr * 2 + bb) * NG + i
                        gate(pe, first_ev, n + 2, passed)
                        gate(pe, cos_read, n + 1, passed)
                        gate(pe, sin_sq, n + 1, passed)
                        for s in range(2):
                            for c in range(CG):
                                mm = nc.tensor.matmul(P[:, 2 + 2 * s + i % 2, c * W:c * W + W], T2[:, i % 2, c, s * W:s * W + W],
                                                      casup[:, s * W:s * W + W], start=True, stop=True)
                        mm.then_inc(second_done, 1)

                    def inverse(i):
                        n = (pr * 2 + bb) * NG + i
                        if i % 2 == 0:
                            gate(pe, inv1_ev, (pr * 2 + bb) * (NG // 2) + i // 2 + 1, passed)
                            nc.tensor.matmul(P[:, 7, 0:128], MO[:, bb, i // 2 * 128:i // 2 * 128 + 128], cinv1[:, :],
                                             start=True, stop=True).then_inc(inv1_done, 1)
                            gate(pe, inv1_ev, (pr * 2 + bb) * (NG // 2) + i // 2 + 2, passed)
                        gate(pe, y_read, n + 1, passed)
                        nc.tensor.matmul(P[:, 6, :], IV[:, i // 2 % 2, :], cblk[:, i % 2, :], start=True, stop=True
                                         ).then_inc(inv2_done, 1)

                    gate(pe, loaded[bb], pr * 48 + 48, passed)
                    first(0)
                    for i in range(NG):
                        if i + 1 < NG:
                            first(i + 1)
                        second(i)
                        inverse(i)

        @block.scalar
        def _(act):
            act.sem_inc(first_ev, 1)
            act.sem_inc(sin_sq, 2)
            with act.Fori(0, PRS) as pr:
                for bb in range(2):
                    def evict(i):
                        n = (pr * 2 + bb) * NG + i
                        act.wait_ge(first_done, n + 1)
                        nc.scalar.activation(T2[:, i % 2].rearrange("p c w -> p (c w)"), P[:, 0:2, :].rearrange("p a w -> p (a w)"),
                                             ACT.Copy).then_inc(first_ev, 1)

                    def root(i):
                        n = (pr * 2 + bb) * NG + i
                        act.wait_ge(squares_ready, n + 1)
                        nc.scalar.activation(RT[:, i % 2], SC[:, i % 2], ACT.Sqrt).then_inc(root_ready, 1)
                    evict(0)
                    for i in range(NG):
                        n = (pr * 2 + bb) * NG + i
                        if i + 1 < NG:
                            evict(i + 1)
                        act.wait_ge(second_done, n + 1)
                        act.wait_ge(slots_used, n + 1)
                        nc.scalar.activation(SC[:, i % 2], P[:, 2 + i % 2, :], ACT.Square).then_inc(cos_sq, 1)
                        nc.scalar.activation(SS[:, i % 2], P[:, 4 + i % 2, :], ACT.Square).then_inc(sin_sq, 1)
                        if i >= 1:
                            root(i - 1)
                    root(NG - 1)

        @block.vector
        def _(dve):
            v = nc.vector
            dve.sem_inc(inv1_ev, 1)
            dve.sem_inc(y_read, 1)
            dve.sem_inc(cos_read, 2)
            dve.sem_inc(slots_used, 2)
            with dve.Fori(0, PRS) as pr:
                for bb in range(2):
                    ch = Chain(dve, step, (pr * 2 + bb) * (NG * 4), NG * 4)

                    def squares(i):
                        n = (pr * 2 + bb) * NG + i
                        dve.wait_ge(cos_sq, n + 1)
                        dve.wait_ge(sin_sq, n + 3)
                        ch(v.tensor_tensor(SS[:, i % 2], SS[:, i % 2], SC[:, i % 2], ALU.add))
                        v.scalar_tensor_tensor(ZZ[:, i % 2], SS[:, i % 2], 0.0, P[:, 2 + i % 2, :], ALU.is_equal, ALU.add
                                               ).then_inc(cos_read, 1)
                        v.scalar_tensor_tensor(SC[:, i % 2], SS[:, i % 2], 0.0, SS[:, i % 2], ALU.is_equal, ALU.add
                                               ).then_inc(squares_ready, 1)

                    def finish(i):
                        n = (pr * 2 + bb) * NG + i
                        x = XY[:, bb, CG * i:CG * i + CG, :].rearrange("p c w -> p (c w)")
                        dve.wait_ge(root_ready, n + 1)
                        ch(v.reciprocal(RT[:, i % 2], RT[:, i % 2]))
                        dve.wait_ge(cos_read, n + 3)
                        ch(v.tensor_tensor(ZZ[:, i % 2], ZZ[:, i % 2], RT[:, i % 2], ALU.mult))
                        dve.wait_ge(inv2_done, n + 1)
                        v.tensor_tensor(ZZ[:, i % 2], ZZ[:, i % 2], P[:, 6, :], ALU.mult).then_inc(y_read, 1)
                        dve.wait_ge(y_read, n + 2)
                        ch(v.tensor_tensor(x, x, ZZ[:, i % 2], ALU.add))
                        dve.sem_inc(out_ready, 1)
                        dve.sem_inc(slots_used, 1)

                    dve.wait_ge(loaded[bb], pr * 48 + 48)
                    for i in range(NG):
                        if i % 2 == 0:
                            dve.wait_ge(inv1_done, (pr * 2 + bb) * (NG // 2) + i // 2 + 1)
                            v.tensor_copy(IV[:, i // 2 % 2, :], P[:, 7, 0:128]).then_inc(inv1_ev, 1)
                        squares(i)
                        if i >= 1:
                            finish(i - 1)
                    finish(NG - 1)
                    ch.done()


def cas(n):
    j = np.arange(n, dtype=np.float32)
    a = (np.float32(2.0 * np.pi) / np.float32(n) * (j[:, None] * j[None, :])).astype(np.float32)
    return (np.cos(a) + np.sin(a)).astype(np.float32)


def constants():
    f = np.float32
    k = {}
    part = np.arange(128)
    c = part % C
    k["iota"] = np.tile(np.arange(128, dtype=f), (128, 1))
    k["ident"] = np.eye(128, dtype=f)
    k["anti"] = np.eye(128, dtype=f)[::-1]
    k["gsum"] = (c[:, None] // 2 == c[None, :] // 2).astype(f) / f(2 * W * W)
    k["shift"] = np.stack([c[:, None] == c[None, :] + m - 1 for m in range(3)], 1).astype(f) / f(W * W)
    line = np.linspace(-1, 1, W, dtype=f) * f((W - 1) / 2)
    k["jc"] = np.stack([line, -line], 1)
    k["ic"] = np.tile(line[:HR], (128, 1))
    k["base"] = np.tile(np.linspace(0, 180, NA, dtype=f), (128, 1))
    pos = np.arange(W, dtype=f) * f((NA - 1) / (W - 1))
    k["ftab"] = np.tile((pos - np.minimum(np.floor(pos), NA - 2)).astype(f), (128, 1))
    k["one"] = np.ones((1, 32), f)
    src = (np.arange(W) + 0.5) / 8 - 0.5
    i0 = np.floor(src).astype(int)
    col = np.zeros((S2, W))
    for x in range(W):
        col[max(i0[x], 0), x] += 1 - (src[x] - i0[x])
        col[min(i0[x] + 1, S2 - 1), x] += src[x] - i0[x]
    u = np.zeros((2, S2, 2, TR, W))
    for odd in range(2):
        for r in range(TR):
            low = ((TR * odd + r + 0.5) / 8 - 0.5) % 1
            u[0, :, odd, r] = (1 - low) * col
            u[1, :, odd, r] = low * col
    k["U"] = u.reshape(32, 2, TR * W).astype(f)
    full = cas(W)
    kept = np.r_[0:NM, W - NM:W]
    g = np.arange(NM)
    k["crow"] = full[:, kept]
    k["ccol"] = np.stack([full[:, g], full[:, (-g) % NM]], 1)
    k["sign"] = np.repeat(np.array([1, -1], f), C)[:, None]
    k["cas2"] = np.concatenate([full, full[::-1]], 1)
    k["casup"] = k["cas2"] * f(UP)
    k["cinv1"] = full[kept] * f(0.5 / (W * W))
    cb = np.zeros((8, NM, 2, 4, W), f)
    for o in range(8):
        cb[o, :, o // 4, o % 4, :] = full[:NM]
    k["cblk"] = cb.reshape(128, 2, 4 * W)
    return k


def layouts(a):
    k = {}
    twice = lambda v: np.tile(v, 2)
    k["lin1"] = a["L0_conv_lin1_w"].reshape(32, C, 2, 2, 4).transpose(2, 1, 3, 4, 0).reshape(128, 8, 32)
    k["lin2"] = a["L0_conv_lin2_w"].T
    k["lin1b"] = a["L0_conv_lin1_b"][:, None]
    k["lin2b"] = np.tile(a["L0_conv_lin2_b"], (128, 1))
    k["wf0"] = np.tile(a["L0_conv_wf0"].reshape(1, 3), (C, 1))
    k["wf1"] = np.tile(a["L0_conv_wf1"].reshape(1, 5), (C, 1))
    k["fuse"] = a["L0_conv_fuse_w"].reshape(C, C, 2).transpose(1, 2, 0)
    k["bn"] = np.stack([twice(a["L0_conv_" + n]) for n in ("bn_gamma", "bn_beta", "bn_mean", "bn_var", "fuse_b")], 1)
    k["w0"] = a["L1_conv_w0"].transpose(1, 2, 3, 0).reshape(C, TAPS, C)
    k["wf"] = a["L1_conv_wf"].transpose(1, 2, 3, 0).reshape(C, TAPS, C)
    k["w3"] = a["L1_conv_w3"].reshape(C, TAPS, C).transpose(2, 1, 0)
    k["w1"] = np.tile(a["L1_conv_w1"].reshape(C, TAPS), (2, 1))
    k["b3"] = np.tile(a["L1_conv_b3"].reshape(C, TAPS), (2, 1))
    k["w2"] = np.tile(a["L1_conv_w2"].reshape(1, 3), (128, 1))
    k["bias1"] = np.stack([twice(a["L1_conv_b0"]), twice(a["L1_conv_b1"]), np.tile(a["L1_conv_b2"], 128),
                           twice(a["L1_conv_bf"])], 1)
    convs = [(b, n, j) for b in ("blk1", "blk2") for n in range(3) for j in "12"]
    k["blocks"] = np.stack([a[f"L2_conv_{b}_w{j}"][n].transpose(1, 2, 3, 0).reshape(C, TAPS, C) for b, n, j in convs], 1
                           ).reshape(C, -1, C)
    k["bias2"] = np.stack([twice(a[f"L2_conv_{b}_b{j}"][n]) for b, n, j in convs], 1)
    k["tok"] = a["L2_conv_tok_w"].reshape(C, TAPS, C).transpose(2, 1, 0).reshape(C, TAPS * C)
    k["tokb"] = a["L2_conv_tok_b"].reshape(C, TAPS).T.reshape(1, TAPS * C)
    w = np.stack([a["L3_conv_weights1"], a["L3_conv_weights2"]])
    neg = (-np.arange(NM)) % NM
    k["w_at"] = w.transpose(1, 0, 3, 4, 2).reshape(C, -1)
    k["w_neg"] = w[:, :, :, neg][:, :, :, :, neg].transpose(1, 0, 3, 4, 2).reshape(C, -1)
    return k


def program(nc, x, out, k):
    B = x.shape[0]

    def scratch(name, shape):
        return nc.dram_tensor(name, shape, F32, kind="Internal").ap()

    x1 = scratch("x1_dram", (B, C, W, W))
    x2 = scratch("x2_dram", (B, C, W, W))
    y2 = scratch("y2_dram", (B, C, S2 + 2, S2))
    x3 = scratch("x3_dram", (B, W, C, W))
    g3 = scratch("g3_dram", (B, W, C, W))
    modes = scratch("modes_dram", (B, NF, C * NM))
    layer0(nc, B, x, x1, k)
    layer1(nc, B, x1, x2, k)
    layer2_small(nc, B, x2, y2, k)
    layer2_apply(nc, B, x2, y2, x3, g3, k)
    layer3_modes(nc, B, g3, modes, k)
    layer3_phase(nc, B, x3, g3, modes, out, k)


def kernel(**inputs):
    import concourse.bacc as _bacc
    from concourse.bass_utils import run_bass_kernel_spmd as _run

    nc = _bacc.Bacc("TRN2", target_bir_lowering=False, num_devices=1)
    a = {name: np.ascontiguousarray(v) for name, v in inputs.items()}
    arrays = {"in_x_dram": a["x"]}
    for name, v in {**constants(), **layouts(a)}.items():
        arrays[f"in_{name}_dram"] = np.ascontiguousarray(v)
    aps = {name: nc.dram_tensor(name, v.shape, mybir.dt.from_np(v.dtype), kind="ExternalInput").ap()
           for name, v in arrays.items()}
    out = nc.dram_tensor("out_dram", a["x"].shape, F32, kind="ExternalOutput").ap()
    program(nc, aps["in_x_dram"], out, {name[3:-5]: ap for name, ap in aps.items() if name != "in_x_dram"})
    r = _run(nc, [arrays], core_ids=[0])
    return r.results[0]["out_dram"]
```

```python
import numpy as np
from contextlib import ExitStack, contextmanager

import concourse.bass as bass
from concourse import mybir

F32 = mybir.dt.float32
ALU = mybir.AluOpType
ACT = mybir.ActivationFunctionType
AX_X = mybir.AxisListType.X

C = 64
W = 128
HR = W // 2
NPX = HR * W
NA = 6
GN_EPS = 1e-5
BN_EPS = 1e-5


class Chain:

    def __init__(self, eng, sem, base, per):
        self.eng, self.sem, self.base, self.per, self.n = eng, sem, base, per, 0

    def __call__(self, ins):
        self.n += 1
        ins.then_inc(self.sem, 1)
        self.eng.wait_ge(self.sem, self.base + self.n)

    def done(self):
        assert self.n == self.per, self.n


def gate(eng, sem, value, passed):
    eng.wait_ge(sem, value)
    eng.sem_inc(passed, 1)


@contextmanager
def phase(nc):
    held = []

    def named(name):
        held.append(nc.alloc_semaphore(name=name))
        return held[-1]

    yield named
    for s in held:
        nc.gpsimd.sem_clear(s)
        nc.release_semaphore(s)
    nc.all_engine_barrier()


def bc(ap, shape):
    return ap.broadcast_to(shape)


def layer0(nc, B, x, x1, k):
    PAIRS = NA // 2
    GR = 4
    GPP = 2 * HR // GR
    CPER = 66
    with phase(nc) as named, ExitStack() as ctx:
        def sb(name, shape, dt=F32):
            return ctx.enter_context(nc.sbuf_tensor("a_" + name, shape, dt))

        def sem(name):
            return named("a_" + name)

        X = sb("X", [128, NPX])
        R = sb("R", [128, 128, 128])
        Rf = R[:, :, :].rearrange("p a b -> p (a b)")
        V = Rf[:, 0:NPX]
        GN = Rf[:, NPX:2 * NPX]
        XT = sb("XT", [128, 128, 2, C])
        D = sb("D", [128, 2, 2, GR, 128])
        T = sb("T", [128, 2, 2, GR, 128])
        COORD = sb("COORD", [128, 2, PAIRS * 128])
        iota = sb("iota", [128, 128])
        ident = sb("ident", [128, 128])
        anti = sb("anti", [128, 128])
        gsum = sb("gsum", [128, 128])
        lin1 = sb("lin1", [128, 8, 32])
        lin2 = sb("lin2", [32, NA])
        lin1b = sb("lin1b", [32, 1])
        lin2b = sb("lin2b", [128, NA])
        base = sb("base", [128, NA])
        jc = sb("jc", [128, 2])
        ic = sb("ic", [128, HR])
        ftab = sb("ftab", [128, W])
        wf0 = sb("wf0", [C, 3])
        wf1 = sb("wf1", [C, 5])
        fuse = sb("fuse", [C, 2, C])
        bn = sb("bn", [128, 5])
        st = sb("st", [128, 16])
        bnp = sb("bnp", [128, 4])
        PB1 = sb("PB1", [128, HR, 4])
        PB = sb("PB", [128, 8])
        PBn = sb("PBn", [128, 8])
        h1 = sb("h1", [32, 1])
        h1b = sb("h1b", [32, 128])
        ones32 = sb("ones32", [32, 128])
        ang = sb("ang", [128, 8, NA])
        trig = sb("trig", [128, 2, NA])
        jt = sb("jt", [128, 2, NA])
        SIG = sb("SIG", [128, PAIRS * 128])
        SP = sb("SP", [C, NA, W + 2])
        CUR = sb("CUR", [C, NA, HR + 4])
        F1 = sb("F1", [C, NA, HR])
        F2 = sb("F2", [C, NA, HR // 2 + 2])
        U1 = sb("U1", [C, NA, HR + 2])
        QT = sb("QT", [C, NA, HR + 2])
        CC = sb("CC", [C, NA, W, 2])
        Z = sb("Z", [128, NA, HR])
        DZ = sb("DZ", [128, NA - 1, HR])
        P = ctx.enter_context(nc.psum_tensor("a_P", [128, 8, 512], F32))

        const_loaded = sem("const_loaded")
        x_loaded = sem("x_loaded")
        x_used = sem("x_used")
        x1_stored = sem("x1_stored")
        init_done = sem("init_done")
        chain_dve = sem("chain_dve")
        chain_act = sem("chain_act")
        sum_ready = sem("sum_ready")
        mean_ready = sem("mean_ready")
        negmean_ready = sem("negmean_ready")
        sq_ready = sem("sq_ready")
        var_ready = sem("var_ready")
        vare_ready = sem("vare_ready")
        std_ready = sem("std_ready")
        gnp_ready = sem("gnp_ready")
        gn_ready = sem("gn_ready")
        pooled_ready = sem("pooled_ready")
        lin1_done = sem("lin1_done")
        h1_ready = sem("h1_ready")
        h1b_ready = sem("h1b_ready")
        lin2_done = sem("lin2_done")
        theta_ready = sem("theta_ready")
        trig_ready = sem("trig_ready")
        coord_ready = sem("coord_ready")
        tr_done = sem("tr_done")
        tr_ev = sem("tr_ev")
        rot_done = sem("rot_done")
        rot_ev = sem("rot_ev")
        diff_ready = sem("diff_ready")
        abs_ready = sem("abs_ready")
        tents_ready = sem("tents_ready")
        rows_done = sem("rows_done")
        rows_evicted = sem("rows_evicted")
        sig_ready = sem("sig_ready")
        sig_evicted = sem("sig_evicted")
        coef_ready = sem("coef_ready")
        fuse_done = sem("fuse_done")
        blend_ready = sem("blend_ready")
        relu_ready = sem("relu_ready")
        out_ready = sem("out_ready")
        tr_ev0 = sem("tr_ev0")
        rot_ev0 = sem("rot_ev0")
        bn_std = sem("bn_std")
        passed = sem("passed")
        consts = [(iota, "iota"), (ident, "ident"), (anti, "anti"), (gsum, "gsum"), (lin1, "lin1"),
                  (lin2, "lin2"), (lin1b, "lin1b"), (lin2b, "lin2b"), (base, "base"), (jc, "jc"),
                  (ic, "ic"), (ftab, "ftab"), (wf0, "wf0"), (wf1, "wf1"), (fuse, "fuse"), (bn, "bn")]
        CONST = 16 * len(consts)
        block = ctx.enter_context(nc.Block())

        def pair_no(b, p):
            return b * PAIRS + p

        @block.sync
        def _(sp):
            for t, name in consts:
                sp.dma_start(t[:], k[name]).then_inc(const_loaded, 16)
            with sp.Fori(0, B) as b:
                sp.wait_ge(x_used, b + 1)
                for h in range(2):
                    sp.dma_start(X[64 * h:64 * h + 64, :], x[b, :, HR * h:HR * h + HR, :].rearrange("c r w -> c (r w)")
                                 ).then_inc(x_loaded, 16)
                sp.wait_ge(out_ready, b + 1)
                for h in range(2):
                    sp.dma_start(x1[b, :, HR * h:HR * h + HR, :].rearrange("c r w -> c (r w)"), V[64 * h:64 * h + 64, :]
                                 ).then_inc(x1_stored, 16)
            sp.wait_ge(x1_stored, 32 * B + 1)

        @block.scalar
        def _(act):
            act.wait_ge(init_done, 4)
            nc.scalar.activation(bnp[:, 1:2], bnp[:, 0:1], ACT.Sqrt).then_inc(bn_std, 1)
            act.sem_inc(abs_ready, 2)
            act.sem_inc(rows_evicted, 2)
            with act.Fori(0, B) as b:
                ch = Chain(act, chain_act, b * 2, 2)
                act.wait_ge(negmean_ready, b + 1)
                nc.scalar.activation(GN, X[:, :], ACT.Square, bias=st[:, 1:2], accum_out=st[:, 2:3]
                                     ).then_inc(sq_ready, 1)
                act.wait_ge(vare_ready, b + 1)
                nc.scalar.activation(st[:, 4:5], st[:, 3:4], ACT.Sqrt).then_inc(std_ready, 1)
                act.wait_ge(gnp_ready, b + 1)
                nc.scalar.activation(GN, X[:, :], ACT.Identity, bias=st[:, 6:7], scale=st[:, 5:6]
                                     ).then_inc(gn_ready, 1)
                act.wait_ge(lin1_done, b + 1)
                nc.scalar.activation(h1[:, :], P[0:32, 2, 0:1], ACT.Relu, bias=lin1b[:, 0:1]).then_inc(h1_ready, 1)
                for n in range(1, 16, 2):
                    act.wait_ge(tr_done, b * 16 + n + 1)
                    for h in range(2):
                        ins = nc.scalar.activation(XT[:, HR * h + 4 * n:HR * h + 4 * n + 4, 0, :],
                                                   P[:, 4 + n % 4, :].rearrange("p (r h c) -> p h r c", r=4, h=2)[:, h],
                                                   ACT.Copy)
                    ins.then_inc(tr_ev, 1)
                act.wait_ge(theta_ready, b + 1)
                nc.scalar.activation(trig[:, 0, :], ang[:, 2, :], ACT.Sin).then_inc(chain_act, 1)
                nc.scalar.activation(trig[:, 1, :], ang[:, 3, :], ACT.Sin).then_inc(trig_ready, 1)
                for n in range(1, 16, 2):
                    act.wait_ge(rot_done, b * 16 + n + 1)
                    nc.scalar.activation(XT[:, 127 - 8 * n:(119 - 8 * n) if n < 15 else None:-1, 1, :],
                                         P[:, 4 + n % 4, :].rearrange("p (r c) -> p r c", r=8), ACT.Copy
                                         ).then_inc(rot_ev, 1)

                def absolute(p, q, u):
                    g = (b * PAIRS + p) * GPP + q * 2 + u
                    act.wait_ge(diff_ready, g + 1)
                    act.wait_ge(rows_done, g + 1)
                    nc.scalar.activation(T[:, u].rearrange("p a r w -> p (a r w)"),
                                         D[:, u].rearrange("p a r w -> p (a r w)"), ACT.Abs
                                         ).then_inc(abs_ready, 1)

                def evict(p, q, u):
                    g = (b * PAIRS + p) * GPP + q * 2 + u
                    act.wait_ge(rows_done, g + 3)
                    nc.scalar.activation(R[:, bass.ds(q * 2 * GR + u * GR, GR), :],
                                         P[:, u, :].rearrange("p (r w) -> p r w", r=GR), ACT.Copy
                                         ).then_inc(rows_evicted, 1)

                with act.Fori(0, PAIRS) as p:
                    absolute(p, 0, 0)
                    absolute(p, 0, 1)
                    act.wait_ge(sig_ready, b * PAIRS + p + 1)
                    act.wait_ge(x1_stored, b * 32 + 1)
                    with act.Fori(1, GPP // 2) as q:
                        absolute(p, q, 0)
                        evict(p, q - 1, 0)
                        absolute(p, q, 1)
                        evict(p, q - 1, 1)
                    evict(p, GPP // 2 - 1, 0)
                    evict(p, GPP // 2 - 1, 1)
                act.wait_ge(blend_ready, b + 1)
                nc.scalar.activation(V, V, ACT.Relu, bias=bnp[:, 3:4], scale=bnp[:, 2:3]).then_inc(relu_ready, 1)

        @block.tensor
        def _(pe):
            pe.sem_inc(rows_done, 2)
            pe.sem_inc(sig_ready, 1)
            pe.wait_ge(const_loaded, CONST)
            with pe.Fori(0, B) as b:
                pe.wait_ge(sum_ready, b + 1)
                nc.tensor.matmul(P[:, 2, 0:1], gsum[:, :], st[:, 0:1], start=True, stop=True).then_inc(mean_ready, 1)
                pe.wait_ge(sq_ready, b + 1)
                pe.wait_ge(negmean_ready, b + 1)
                nc.tensor.matmul(P[:, 2, 0:1], gsum[:, :], st[:, 2:3], start=True, stop=True).then_inc(var_ready, 1)
                pe.wait_ge(pooled_ready, b + 1)
                for n in range(8):
                    mm = nc.tensor.matmul(P[0:32, 2, 0:1], lin1[:, n, :], PBn[:, n:n + 1], start=n == 0, stop=n == 7)
                mm.then_inc(lin1_done, 1)
                pe.wait_ge(h1b_ready, b + 1)
                nc.tensor.matmul(P[:, 2, 0:NA], h1b[:, :], lin2[:, :], start=True, stop=True).then_inc(lin2_done, 1)
                pe.wait_ge(gn_ready, b + 1)
                for n in range(16):
                    if n >= 4:
                        pe.wait_ge(tr_ev if n % 2 else tr_ev0, b * 8 + (n - 4) // 2 + 1)
                    for r in range(4):
                        mm = nc.tensor.transpose(P[:, 4 + n % 4, 128 * r:128 * r + 128],
                                                 GN[:, (4 * n + r) * W:(4 * n + r + 1) * W], ident[:, :])
                    mm.then_inc(tr_done, 1)
                for n in range(16):
                    pe.wait_ge(tr_ev, b * 8 + 8)
                    pe.wait_ge(tr_ev0, b * 8 + 8)
                    if n >= 4:
                        pe.wait_ge(rot_ev if n % 2 else rot_ev0, b * 8 + (n - 4) // 2 + 1)
                    nc.tensor.matmul(P[:, 4 + n % 4, :], anti[:, :], XT[:, 8 * n:8 * n + 8, 0, :],
                                     start=True, stop=True).then_inc(rot_done, 1)
                gate(pe, rot_ev, b * 8 + 8, passed)
                gate(pe, rot_ev0, b * 8 + 8, passed)
                with pe.Fori(0, PAIRS) as p:
                    with pe.Fori(0, GPP // 2) as q:
                        for u in range(2):
                            g = (b * PAIRS + p) * GPP + q * 2 + u
                            pe.wait_ge(tents_ready, g + 1)
                            pe.wait_ge(rows_evicted, g + 1)
                            for r in range(GR):
                                mm = nc.tensor.matmul(P[:, u, 128 * r:128 * r + 128], T[:, u, 0, r, :], T[:, u, 1, r, :],
                                                      start=True, stop=True)
                            mm.then_inc(rows_done, 1)
                    pe.wait_ge(rows_evicted, (b * PAIRS + p) * GPP + GPP + 2)
                    pe.wait_ge(sig_evicted, b * PAIRS + p + 1)
                    for y in range(W):
                        mm = nc.tensor.matmul(P[:, 3, 0:128], XT[:, y].rearrange("p v c -> p (v c)"), R[:, :, y],
                                              start=y == 0, stop=y == W - 1)
                    mm.then_inc(sig_ready, 1)
                gate(pe, coef_ready, b + 1, passed)
                for h in range(2):
                    for s in range(2):
                        mm = nc.tensor.matmul(P[64 * h:64 * h + 64, 2, 0:NA * HR], fuse[:, s, :],
                                              CC[:, :, HR * s + HR // 2 * h:HR * s + HR // 2 * (h + 1), :], start=s == 0, stop=s == 1)
                mm.then_inc(fuse_done, 1)

        @block.vector
        def _(dve):
            v = nc.vector
            dve.wait_ge(const_loaded, CONST)
            v.memset(ones32[:, :], 1.0).then_inc(init_done, 1)
            v.memset(SP[:, :, :], 0.0).then_inc(init_done, 1)
            v.memset(CUR[:, :, :], 0.0).then_inc(init_done, 1)
            v.tensor_scalar(bnp[:, 0:1], bn[:, 3:4], BN_EPS, None, ALU.add).then_inc(init_done, 1)
            dve.wait_ge(bn_std, 1)
            v.reciprocal(bnp[:, 1:2], bnp[:, 1:2]).then_inc(init_done, 1)
            dve.wait_ge(init_done, 5)
            v.tensor_tensor(bnp[:, 2:3], bnp[:, 1:2], bn[:, 0:1], ALU.mult).then_inc(init_done, 1)
            v.tensor_tensor(bnp[:, 3:4], bn[:, 4:5], bn[:, 2:3], ALU.subtract).then_inc(init_done, 1)
            dve.wait_ge(init_done, 7)
            v.scalar_tensor_tensor(bnp[:, 3:4], bnp[:, 3:4], bnp[:, 2:3], bn[:, 1:2], ALU.mult, ALU.add
                                   ).then_inc(init_done, 1)
            dve.wait_ge(init_done, 8)
            dve.sem_inc(x1_stored, 1)
            dve.sem_inc(x_used, 1)
            dve.sem_inc(sig_evicted, 1)
            with dve.Fori(0, B) as b:
                ch = Chain(dve, chain_dve, b * CPER, CPER)
                dve.wait_ge(x_loaded, b * 32 + 32)
                ch(v.tensor_reduce(PB1[:, :, :], X[:, :].rearrange("p (r q w) -> p r q w", r=HR, q=4), AX_X, ALU.add))
                ch(v.tensor_reduce(PB[:, :].rearrange("p (a q) -> p a q", a=2),
                                   PB1[:, :, :].rearrange("p (a r) q -> p a q r", a=2), AX_X, ALU.add))
                v.tensor_reduce(st[:, 0:1], PB[:, :], AX_X, ALU.add).then_inc(sum_ready, 1)
                dve.wait_ge(mean_ready, b + 1)
                v.tensor_scalar(st[:, 1:2], P[:, 2, 0:1], -1.0, None, ALU.mult).then_inc(negmean_ready, 1)
                dve.wait_ge(var_ready, b + 1)
                v.tensor_scalar(st[:, 3:4], P[:, 2, 0:1], GN_EPS, None, ALU.add).then_inc(vare_ready, 1)
                dve.wait_ge(std_ready, b + 1)
                ch(v.reciprocal(st[:, 5:6], st[:, 4:5]))
                v.tensor_scalar(st[:, 6:7], st[:, 1:2], st[:, 5:6], None, ALU.mult).then_inc(gnp_ready, 1)
                dve.wait_ge(gnp_ready, b + 1)
                ch(v.tensor_scalar(PBn[:, :], PB[:, :], 1.0 / 1024, None, ALU.mult))
                v.tensor_scalar(PBn[:, :], PBn[:, :], st[:, 5:6], st[:, 6:7], ALU.mult, ALU.add
                                ).then_inc(pooled_ready, 1)
                dve.wait_ge(h1_ready, b + 1)
                v.tensor_scalar(h1b[:, :], ones32[:, :], h1[:, 0:1], None, ALU.mult).then_inc(h1b_ready, 1)
                dve.wait_ge(lin2_done, b + 1)
                ch(v.tensor_tensor(ang[:, 0, :], P[:, 2, 0:NA], lin2b[:, :], ALU.add))
                ch(v.scalar_tensor_tensor(ang[:, 0, :], ang[:, 0, :], 30.0, base[:, :], ALU.mult, ALU.add))
                ch(v.tensor_scalar(ang[:, 0, :], ang[:, 0, :], 0.0, 180.0, ALU.max, ALU.min))
                a, o = 0, 1
                for n in range(NA):
                    if n % 2 == 0:
                        lo, hi = slice(0, NA, 2), slice(1, NA, 2)
                    else:
                        lo, hi = slice(1, NA - 1, 2), slice(2, NA - 1, 2)
                        ch(v.tensor_copy(ang[:, o, 0:NA:NA - 1], ang[:, a, 0:NA:NA - 1]))
                    ch(v.tensor_tensor(ang[:, o, lo], ang[:, a, lo], ang[:, a, hi], ALU.min))
                    ch(v.tensor_tensor(ang[:, o, hi], ang[:, a, lo], ang[:, a, hi], ALU.max))
                    a, o = o, a
                ch(v.tensor_scalar(ang[:, 2, :], ang[:, a, :], float(np.float32(np.pi / 180)), None, ALU.mult))
                v.tensor_scalar(ang[:, 3, :], ang[:, 2, :], -1.0, float(np.pi / 2), ALU.mult, ALU.add
                                ).then_inc(theta_ready, 1)
                for n in range(0, 16, 2):
                    dve.wait_ge(tr_done, b * 16 + n + 1)
                    for h in range(2):
                        ins = v.tensor_copy(XT[:, HR * h + 4 * n:HR * h + 4 * n + 4, 0, :],
                                            P[:, 4 + n % 4, :].rearrange("p (r h c) -> p h r c", r=4, h=2)[:, h])
                    ins.then_inc(tr_ev0, 1)
                for n in range(0, 16, 2):
                    dve.wait_ge(rot_done, b * 16 + n + 1)
                    v.tensor_copy(XT[:, 127 - 8 * n:119 - 8 * n:-1, 1, :],
                                  P[:, 4 + n % 4, :].rearrange("p (r c) -> p r c", r=8)).then_inc(rot_ev0, 1)
                dve.wait_ge(trig_ready, b + 1)
                dve.wait_ge(chain_act, b + 1)
                ch(v.tensor_scalar(jt[:, 0, :], trig[:, 1, :], jc[:, 0:1], 63.5, ALU.mult, ALU.add))
                ch(v.tensor_scalar(jt[:, 1, :], trig[:, 0, :], jc[:, 1:2], 63.5, ALU.mult, ALU.add))
                icb = bc(ic[:, :].unsqueeze(1), [128, NA, HR])
                for m in range(2):
                    cm = COORD[:, m, :].rearrange("p (k i) -> p k i", k=NA)
                    ch(v.tensor_tensor(cm, icb, bc(trig[:, m, :].unsqueeze(2), [128, NA, HR]), ALU.mult))
                    ch(v.tensor_tensor(cm, cm, bc(jt[:, m, :].unsqueeze(2), [128, NA, HR]), ALU.add))

                dve.sem_inc(passed, 1)

                def diff(p, q, u):
                    g = (b * PAIRS + p) * GPP + q * 2 + u
                    dve.wait_ge(abs_ready, g + 1)
                    c = COORD[:, :, bass.ds(p * 128 + q * (2 * GR) + u * GR, GR)]
                    v.tensor_tensor(D[:, u], bc(iota[:, :].unsqueeze(1).unsqueeze(1), [128, 2, GR, 128]),
                                    bc(c.unsqueeze(3), [128, 2, GR, 128]), ALU.subtract).then_inc(diff_ready, 1)

                def tent(p, q, u):
                    g = (b * PAIRS + p) * GPP + q * 2 + u
                    dve.wait_ge(abs_ready, g + 3)
                    t = T[:, u].rearrange("p a r w -> p (a r w)")
                    v.tensor_scalar(t, t, 1.0, 1.0, ALU.min, ALU.subtract).then_inc(tents_ready, 1)

                with dve.Fori(0, PAIRS) as p:
                    diff(p, 0, 0)
                    diff(p, 0, 1)
                    with dve.Fori(1, GPP // 2) as q:
                        tent(p, q - 1, 0)
                        diff(p, q, 0)
                        tent(p, q - 1, 1)
                        diff(p, q, 1)
                    tent(p, GPP // 2 - 1, 0)
                    tent(p, GPP // 2 - 1, 1)
                    dve.wait_ge(sig_ready, b * PAIRS + p + 2)
                    v.tensor_copy(SIG[:, bass.ds(p * 128, 128)], P[:, 3, 0:128]).then_inc(sig_evicted, 1)
                dve.wait_ge(sig_evicted, b * PAIRS + PAIRS + 1)
                sig = SIG[:, :].rearrange("p (k i) -> p k i", k=NA)
                ch(v.tensor_copy(SP[:, :, 1:1 + HR], sig[0:64]))
                ch(v.tensor_copy(SP[:, :, W:HR:-1], sig[64:128]))
                ch(v.tensor_scalar(CC[:, :, :, 0], SP[:, :, 0:W], wf0[:, 0:1], None, ALU.mult))
                for t in (1, 2):
                    ch(v.scalar_tensor_tensor(CC[:, :, :, 0], SP[:, :, t:t + W], wf0[:, t:t + 1], CC[:, :, :, 0], ALU.mult, ALU.add))
                cur = CUR[:, :, 2:2 + HR]
                ch(v.tensor_tensor(cur, SP[:, :, 1:W:2], SP[:, :, 2:W + 1:2], ALU.add))
                ch(v.tensor_scalar(cur, cur, 0.5, None, ALU.mult))
                ch(v.tensor_scalar(F1[:, :, :], CUR[:, :, 0:HR], wf1[:, 0:1], None, ALU.mult))
                for t in range(1, 5):
                    ch(v.scalar_tensor_tensor(F1[:, :, :], CUR[:, :, t:t + HR], wf1[:, t:t + 1], F1[:, :, :], ALU.mult, ALU.add))
                L = HR // 2
                ch(v.tensor_tensor(F2[:, :, 1:1 + L], F1[:, :, 0:HR:2], F1[:, :, 1:HR:2], ALU.add))
                ch(v.tensor_scalar(F2[:, :, 1:1 + L], F2[:, :, 1:1 + L], 0.5, None, ALU.mult))
                for src, dst, n in ((F2, U1[:, :, 1:1 + HR], L), (U1, CC[:, :, :, 1], HR)):
                    ch(v.tensor_copy(src[:, :, 0:1], src[:, :, 1:2]))
                    ch(v.tensor_copy(src[:, :, n + 1:n + 2], src[:, :, n:n + 1]))
                    ch(v.tensor_scalar(QT[:, :, 0:n + 2], src[:, :, 0:n + 2], 0.25, None, ALU.mult))
                    ch(v.scalar_tensor_tensor(dst[:, :, 0:2 * n:2], src[:, :, 1:n + 1], 0.75, QT[:, :, 0:n], ALU.mult, ALU.add))
                    ch(v.scalar_tensor_tensor(dst[:, :, 1:2 * n:2], src[:, :, 1:n + 1], 0.75, QT[:, :, 2:n + 2], ALU.mult, ALU.add))
                dve.sem_inc(coef_ready, 1)
                dve.wait_ge(fuse_done, b + 1)
                ch(v.tensor_copy(Z[:, :, :], P[:, 2, 0:NA * HR].rearrange("p (k i) -> p k i", k=NA)))
                ch(v.tensor_tensor(DZ[:, :, :], Z[:, 1:NA, :], Z[:, 0:NA - 1, :], ALU.subtract))
                Vw = V.rearrange("p (r w) -> p r w", r=HR)
                for m, (w0, w1) in enumerate(segments()):
                    n = w1 - w0
                    ch(v.tensor_tensor(Vw[:, :, w0:w1], bc(DZ[:, m, :].unsqueeze(2), [128, HR, n]),
                                       bc(ftab[:, w0:w1].unsqueeze(1), [128, HR, n]), ALU.mult))
                for m, (w0, w1) in enumerate(segments()):
                    n = w1 - w0
                    ch(v.tensor_tensor(Vw[:, :, w0:w1], Vw[:, :, w0:w1], bc(Z[:, m, :].unsqueeze(2), [128, HR, n]), ALU.add))
                dve.sem_inc(blend_ready, 1)
                dve.wait_ge(relu_ready, b + 1)
                ch(v.tensor_tensor(V, V, X[:, :], ALU.add))
                dve.sem_inc(x_used, 1)
                dve.sem_inc(out_ready, 1)
                ch.done()


def segments():
    pos = np.arange(W, dtype=np.float32) * np.float32((NA - 1) / (W - 1))
    i0 = np.minimum(np.floor(pos).astype(int), NA - 2)
    return [(int(np.argmax(i0 == m)), int(W - np.argmax(i0[::-1] == m))) for m in range(NA - 1)]



TAPS = 9
TR = 4
NT = HR // TR
PR, PW = HR + 2, W + 2


class TapGroups:

    def __init__(self, sizes):
        assert sum(sizes) == TAPS
        self.n = len(sizes)
        self.adds = TAPS - self.n
        self.firsts = [sum(sizes[:g]) for g in range(self.n)]

    def group(self, t):
        return max(g for g in range(self.n) if self.firsts[g] <= t)

    def first(self, t):
        return self.firsts[self.group(t)]

    def is_last(self, t):
        return t == TAPS - 1 or t + 1 in self.firsts

    def adds_to(self, t):
        return t - self.group(t)


def layer1(nc, B, x1, x2, k):
    CPER = 5
    NS = 4
    QT = 4
    NQ = NT // QT
    QR = QT * TR
    CONV0 = [NT - 2, NT - 1] + list(range(NT - 2))
    DEPTH = [NT - 1] + list(range(NT - 1))
    LATE = 3
    BEHIND = 4
    ADDS = TAPS - 1
    DEPTH0 = NT * ADDS
    GACT = 16
    with phase(nc) as named, ExitStack() as ctx:
        def sb(name, shape, dt=F32):
            return ctx.enter_context(nc.sbuf_tensor("b_" + name, shape, dt))

        def sem(name):
            return named("b_" + name)

        X = sb("X", [128, HR, W])
        G = sb("G", [128, PR, PW])
        Y = sb("Y", [128, PR, PW])
        T = sb("T", [128, HR, W])
        W0 = sb("W0", [128, TAPS, 128])
        W3 = sb("W3", [128, TAPS, 128])
        WF = sb("WF", [128, TAPS, 128])
        gsum = sb("gsum", [128, 128])
        shift = sb("shift", [128, 3, 128])
        w1 = sb("w1", [128, TAPS])
        b3 = sb("b3", [128, TAPS])
        b3m = sb("b3m", [128, TAPS])
        w2 = sb("w2", [128, 3])
        bias = sb("bias", [128, 4])
        st = sb("st", [128, 16])
        xs = sb("xs", [128, NQ])
        ms = sb("ms", [128, NT])
        m3 = sb("m3", [128, 4])
        PROD = sb("PROD", [128, NS, TR, W])
        ACC = sb("ACC", [128, 2, TR, W])
        P = ctx.enter_context(nc.psum_tensor("b_P", [128, 8, 512], F32))
        const_loaded = sem("const_loaded")
        cleared = sem("cleared")
        weights_loaded = sem("weights_loaded")
        x_loaded = [sem("x_loaded%d" % q) for q in range(NQ)]
        x2_stored = sem("x2_stored")
        out_ready = sem("out_ready")
        passed = sem("passed")
        chain_dve = sem("chain_dve")
        chain_pads = sem("chain_pads")
        xs_ready = sem("xs_ready")
        sum_ready = sem("sum_ready")
        mean_ready = sem("mean_ready")
        negmean_ready = sem("negmean_ready")
        sq_ready = sem("sq_ready")
        var_ready = sem("var_ready")
        vare_ready = sem("vare_ready")
        std_ready = sem("std_ready")
        gnp_ready = sem("gnp_ready")
        gn_ready = sem("gn_ready")
        gn_low = sem("gn_low")
        gn_halo = sem("gn_halo")
        conv0_done = sem("conv0_done")
        conv0_ev = sem("conv0_ev")
        y_halo = sem("y_halo")
        ysum_ready = sem("ysum_ready")
        m3_done = sem("m3_done")
        dbias_ready = sem("dbias_ready")
        b3_done = sem("b3_done")
        b3_ready = sem("b3_ready")
        tap0_ready = sem("tap0_ready")
        depth_step = sem("depth_step")
        fil_done = sem("fil_done")
        prod_ready = sem("prod_ready")
        added = sem("added")
        filtered = sem("filtered")
        f_halo = sem("f_halo")
        convf_done = sem("convf_done")
        mix_ready = sem("mix_ready")
        consts = [(gsum, "gsum"), (shift, "shift"), (w1, "w1"), (b3, "b3"), (w2, "w2"), (bias, "bias1")]
        block = ctx.enter_context(nc.Block())
        t9 = [(t // 3, t % 3) for t in range(TAPS)]

        def tile(t, n, dy=0, dx=0):
            return t[:, TR * n + dy:TR * n + dy + TR, dx:dx + W]

        def bank(m):
            return P[:, m, :].rearrange("p (r w) -> p r w", r=TR)

        @block.sync
        def _(sp):
            for t, name in consts:
                sp.dma_start(t[:], k[name]).then_inc(const_loaded, 16)
            sp.wait_ge(cleared, 3)
            for t, name in ((W0, "w0"), (W3, "w3"), (WF, "wf")):
                for h in range(2):
                    sp.dma_start(t[64 * h:64 * h + 64, :, 64 * h:64 * h + 64], k[name]).then_inc(weights_loaded, 16)

            def load(b, q):
                for h in range(2):
                    sp.dma_start(X[64 * h:64 * h + 64, QR * q:QR * q + QR], x1[b, :, HR * h + QR * q:HR * h + QR * q + QR, :]
                                 ).then_inc(x_loaded[q], 16)

            def store(b, q):
                sp.wait_ge(out_ready, b * NT + QT * q + QT)
                for h in range(2):
                    sp.dma_start(x2[b, :, HR * h + QR * q:HR * h + QR * q + QR, :], T[64 * h:64 * h + 64, QR * q:QR * q + QR]
                                 ).then_inc(x2_stored, 16)

            for q in range(NQ):
                load(0, q)
            with sp.Fori(0, B - 1) as b:
                for q in range(NQ):
                    store(b, q)
                    load(b + 1, q)
            for q in range(NQ):
                store(B - 1, q)
            sp.wait_ge(x2_stored, 32 * NQ * B + 1)

        def inner(t):
            return t[:, 1:1 + HR, 1:1 + W]

        def halo(copy, t):
            copy(t[0:64, PR - 1, :], t[64:128, 1, :])
            return copy(t[64:128, 0, :], t[0:64, HR, :])

        @block.scalar
        def _(act):
            act.sem_inc(conv0_ev, 4)
            with act.Fori(0, B) as b:
                gate(act, negmean_ready, b + 1, passed)
                nc.scalar.activation(inner(Y), X[:, :, :], ACT.Square, bias=st[:, 1:2], accum_out=st[:, 2:3]
                                     ).then_inc(sq_ready, 1)
                act.wait_ge(vare_ready, b + 1)
                nc.scalar.activation(st[:, 4:5], st[:, 3:4], ACT.Sqrt).then_inc(std_ready, 1)
                act.wait_ge(gnp_ready, b + 1)
                nc.scalar.activation(G[:, 1:1 + GACT, 1:1 + W], X[:, 0:GACT, :], ACT.Identity, bias=st[:, 6:7], scale=st[:, 5:6]
                                     ).then_inc(gn_ready, 1)

                def tap0(j):
                    nc.scalar.activation(tile(T, DEPTH[j]), tile(Y, DEPTH[j]), ACT.Copy, scale=w1[:, 0:1]).then_inc(tap0_ready, 1)

                for m, n in enumerate(CONV0):
                    act.wait_ge(conv0_done, b * NT + m + 1)
                    nc.scalar.activation(Y[:, 1 + TR * n:1 + TR * n + TR, 1:1 + W], bank(m % 4),
                                         ACT.Identity, bias=bias[:, 0:1], accum_out=ms[:, n:n + 1]).then_inc(conv0_ev, 1)
                    if m == 3:
                        gate(act, y_halo, b + 1, passed)
                        gate(act, x2_stored, b * (32 * NQ) + 1, passed)
                        tap0(0)
                    if m >= 3:
                        act.wait_ge(conv0_ev, b * NT + m + 5)
                        tap0(m - 2)
                tap0(NT - 2)
                tap0(NT - 1)
                for n in range(NT):
                    act.wait_ge(mix_ready, b * NT + n + 3)
                    nc.scalar.activation(tile(T, n), tile(T, n), ACT.Identity, bias=st[:, 8:9]).then_inc(out_ready, 1)

        @block.tensor
        def _(pe):
            pe.wait_ge(const_loaded, 16 * len(consts))
            pe.wait_ge(weights_loaded, 96)
            with pe.Fori(0, B) as b:
                pe.wait_ge(sum_ready, b + 1)
                nc.tensor.matmul(P[:, 7, 0:1], gsum[:, :], st[:, 0:1], start=True, stop=True).then_inc(mean_ready, 1)
                gate(pe, sq_ready, b + 1, passed)
                pe.wait_ge(negmean_ready, b + 1)
                nc.tensor.matmul(P[:, 7, 0:1], gsum[:, :], st[:, 2:3], start=True, stop=True).then_inc(var_ready, 1)
                gate(pe, gn_ready, b + 1, passed)
                gate(pe, gn_halo, b + 1, passed)
                for m, n in enumerate(CONV0):
                    pe.wait_ge(conv0_ev, b * NT + m + 1)
                    for t, (dy, dx) in enumerate(t9):
                        mm = nc.tensor.matmul(P[:, m % 4, :], W0[:, t, :], tile(G, n, dy, dx), start=t == 0, stop=t == TAPS - 1)
                    mm.then_inc(conv0_done, 1)
                gate(pe, ysum_ready, b + 1, passed)
                for m in range(3):
                    mm = nc.tensor.matmul(P[:, 7, m:m + 1], shift[:, m, :], st[:, 7:8], start=True, stop=True)
                mm.then_inc(m3_done, 1)
                gate(pe, dbias_ready, b + 1, passed)
                for t in range(TAPS):
                    mm = nc.tensor.matmul(P[:, 7, t:t + 1], W3[:, t, :], m3[:, 3:4], start=True, stop=True)
                mm.then_inc(b3_done, 1)
                gate(pe, conv0_ev, b * NT + NT + 4, passed)

                def last_conv(c, t):
                    if t == 0:
                        pe.wait_ge(mix_ready, b * NT + c + 1)
                        gate(pe, filtered, b * NT + min(c + 3, NT), passed)
                        if c == 0:
                            gate(pe, f_halo, b + 1, passed)
                    mm = nc.tensor.matmul(P[:, 4 + c % 2, :], WF[:, t, :], tile(G, c, *t9[t]), start=t == 0, stop=t == TAPS - 1)
                    if t == TAPS - 1:
                        mm.then_inc(convf_done, 1)

                for m, n in enumerate(DEPTH):
                    gate(pe, depth_step, b * (NT * ADDS) + DEPTH0 + (m + 1) * ADDS, passed)
                    for t in range(TAPS):
                        s = m * TAPS + t
                        if s >= 4:
                            pe.wait_ge(prod_ready, b * (NT * TAPS) + s - 3)
                        nc.tensor.matmul(P[:, s % 4, :], W3[:, t, :], tile(T, n), start=True, stop=True).then_inc(fil_done, 1)
                        if m >= BEHIND:
                            last_conv(m - BEHIND, t)
                for c in range(NT - BEHIND, NT):
                    for t in range(TAPS):
                        last_conv(c, t)

        @block.vector
        def _(dve):
            v = nc.vector
            for n, t in enumerate((W0, W3, WF)):
                v.memset(t[:, :, :], 0.0).then_inc(cleared, 1)
            v.memset(G[:, :, :], 0.0).then_inc(chain_pads, 1)
            v.memset(Y[:, :, :], 0.0).then_inc(chain_pads, 1)
            dve.wait_ge(chain_pads, 2)
            dve.wait_ge(const_loaded, 16 * len(consts))
            dve.sem_inc(x2_stored, 1)
            dve.sem_inc(mix_ready, 2)
            dve.sem_inc(depth_step, DEPTH0)
            with dve.Fori(0, B) as b:
                ch = Chain(dve, chain_dve, b * CPER, CPER)
                for q in range(NQ):
                    dve.wait_ge(x_loaded[q], b * 32 + 32)
                    v.tensor_reduce(xs[:, q:q + 1], X[:, QR * q:QR * q + QR].rearrange("p r w -> p (r w)"), AX_X, ALU.add
                                    ).then_inc(xs_ready, 1)
                dve.wait_ge(xs_ready, b * NQ + NQ)
                v.tensor_reduce(st[:, 0:1], xs[:, :], AX_X, ALU.add).then_inc(sum_ready, 1)
                dve.wait_ge(mean_ready, b + 1)
                v.tensor_scalar(st[:, 1:2], P[:, 7, 0:1], -1.0, None, ALU.mult).then_inc(negmean_ready, 1)
                dve.wait_ge(var_ready, b + 1)
                v.tensor_scalar(st[:, 3:4], P[:, 7, 0:1], GN_EPS, None, ALU.add).then_inc(vare_ready, 1)
                dve.wait_ge(std_ready, b + 1)
                ch(v.reciprocal(st[:, 5:6], st[:, 4:5]))
                v.tensor_scalar(st[:, 6:7], st[:, 1:2], st[:, 5:6], None, ALU.mult).then_inc(gnp_ready, 1)
                dve.wait_ge(gnp_ready, b + 1)
                v.tensor_scalar(G[:, 1 + GACT:1 + HR, 1:1 + W], X[:, GACT:HR, :], st[:, 5:6], st[:, 6:7], ALU.mult, ALU.add
                                ).then_inc(gn_low, 1)
                ch(v.tensor_tensor(st[:, 8:9], st[:, 6:7], bias[:, 3:4], ALU.add))
                ch(v.tensor_scalar(st[:, 9:10], st[:, 5:6], 1.0, None, ALU.add))
                dve.wait_ge(gn_low, b + 1)
                dve.wait_ge(gn_ready, b + 1)
                halo(v.tensor_copy, G).then_inc(gn_halo, 1)
                gate(dve, conv0_ev, b * NT + 3 + 4, passed)
                halo(v.tensor_copy, Y).then_inc(y_halo, 1)

                def depth(j, t):
                    if t == 1:
                        dve.wait_ge(tap0_ready, b * NT + j + 1)
                    else:
                        dve.wait_ge(depth_step, b * (NT * ADDS) + DEPTH0 + j * ADDS + t - 1)
                    n = DEPTH[j]
                    v.scalar_tensor_tensor(tile(T, n), tile(Y, n, *t9[t]), w1[:, t:t + 1], tile(T, n), ALU.mult, ALU.add
                                           ).then_inc(depth_step, 1)

                for j in range(NT - LATE):
                    for t in range(1, TAPS):
                        depth(j, t)
                gate(dve, conv0_ev, b * NT + NT + 4, passed)
                v.tensor_reduce(st[:, 7:8], ms[:, :], AX_X, ALU.add).then_inc(ysum_ready, 1)
                dve.wait_ge(m3_done, b + 1)
                ch(v.tensor_tensor(m3[:, 0:3], P[:, 7, 0:3], w2[:, :], ALU.mult))
                ch(v.tensor_reduce(m3[:, 3:4], m3[:, 0:3], AX_X, ALU.add))
                v.tensor_scalar(m3[:, 3:4], m3[:, 3:4], bias[:, 1:2], bias[:, 2:3], ALU.add, ALU.add).then_inc(dbias_ready, 1)
                dve.wait_ge(b3_done, b + 1)
                v.tensor_tensor(b3m[:, :], P[:, 7, 0:TAPS], b3[:, :], ALU.add).then_inc(b3_ready, 1)
                dve.wait_ge(b3_ready, b + 1)

                def add(s):
                    m, t = s // TAPS, s % TAPS
                    dve.wait_ge(prod_ready, b * (NT * TAPS) + s + 1)
                    if t > 1:
                        dve.wait_ge(added, b * (NT * ADDS) + m * ADDS + t - 1)
                    v.tensor_tensor(ACC[:, m % 2], PROD[:, (s - 1) % NS] if t == 1 else ACC[:, m % 2], PROD[:, s % NS], ALU.add
                                    ).then_inc(added, 1)

                def leaky(m):
                    dve.wait_ge(added, b * (NT * ADDS) + m * ADDS + ADDS)
                    n = DEPTH[m]
                    v.scalar_tensor_tensor(G[:, 1 + TR * n:1 + TR * n + TR, 1:1 + W], ACC[:, m % 2], 0.2, ACC[:, m % 2],
                                           ALU.mult, ALU.max).then_inc(filtered, 1)
                    if m == 1:
                        gate(dve, filtered, b * NT + 2, passed)
                        halo(v.tensor_copy, G).then_inc(f_halo, 1)

                def mix(c):
                    dve.wait_ge(convf_done, b * NT + c + 1)
                    v.scalar_tensor_tensor(tile(T, c), tile(X, c), st[:, 9:10], bank(4 + c % 2), ALU.mult, ALU.add
                                           ).then_inc(mix_ready, 1)

                late = [(j, t) for j in range(NT - LATE, NT) for t in range(1, TAPS)]
                for s in range(NT * TAPS):
                    m, t = s // TAPS, s % TAPS
                    dve.wait_ge(fil_done, b * (NT * TAPS) + s + 1)
                    v.scalar_tensor_tensor(PROD[:, s % NS], bank(s % 4), b3m[:, t:t + 1], tile(Y, DEPTH[m], *t9[t]),
                                           ALU.add, ALU.mult).then_inc(prod_ready, 1)
                    if (s - 1) % TAPS >= 1 and s >= 1:
                        add(s - 1)
                    if m >= 1 and t == 1:
                        leaky(m - 1)
                    if m > BEHIND and t == 4:
                        mix(m - BEHIND - 1)
                    if s >= TAPS and s % 2 and late:
                        depth(*late.pop(0))
                add(NT * TAPS - 1)
                leaky(NT - 1)
                for c in range(NT - BEHIND - 1, NT):
                    mix(c)
                ch.done()



S1, S2 = 32, 16


def layer2_small(nc, B, x2, y2, k):
    PRS = B // 2
    with phase(nc) as named, ExitStack() as ctx:
        def sb(name, shape, dt=F32):
            return ctx.enter_context(nc.sbuf_tensor("c_" + name, shape, dt))

        def sem(name):
            return named("c_" + name)

        X = sb("X", [128, 2, NPX])
        SQ = sb("SQ", [128, NPX // 4])
        WTS = sb("WTS", [128, 12, TAPS, 128])
        bias = sb("bias", [128, 12])
        gsum = sb("gsum", [128, 128])
        POOL1 = sb("POOL1", [128, HR, S1])
        POOL2 = sb("POOL2", [128, S1 // 2, S1])
        YP = sb("YP", [128, PRS, S1 + 2, S1 + 2])
        HP = sb("HP", [128, PRS, S1 + 2, S1 + 2])
        YQ = sb("YQ", [128, PRS, S2 + 2, S2 + 2])
        HQ = sb("HQ", [128, PRS, S2 + 2, S2 + 2])
        MX = sb("MX", [128, S1, S2])
        YE = sb("YE", [128, PRS, S2 + 2, S2])
        st = sb("st", [128, 16])
        sq4 = sb("sq4", [128, 4])
        P = ctx.enter_context(nc.psum_tensor("c_P", [128, 8, 512], F32))
        const_loaded = sem("const_loaded")
        cleared = sem("cleared")
        weights_loaded = sem("weights_loaded")
        x_loaded = [sem("x_loaded0"), sem("x_loaded1")]
        x_used = sem("x_used")
        chain_dve = sem("chain_dve")
        chain_tail = sem("chain_tail")
        passed = sem("passed")
        sum_ready = sem("sum_ready")
        mean_ready = sem("mean_ready")
        negmean_ready = sem("negmean_ready")
        sq_ready = sem("sq_ready")
        sqsum_ready = sem("sqsum_ready")
        var_ready = sem("var_ready")
        vare_ready = sem("vare_ready")
        std_ready = sem("std_ready")
        pooled = sem("pooled")
        conv_done = sem("conv_done")
        hid_ev = sem("hid_ev")
        hid_ready = sem("hid_ready")
        res_ready = sem("res_ready")
        maxed = sem("maxed")
        y2_ready = sem("y2_ready")
        y2_stored = sem("y2_stored")
        block = ctx.enter_context(nc.Block())
        n_items = {1: PRS * 2, 2: (PRS + 1) // 2}
        steps = [(bl, la, cv, it) for bl in (1, 2) for la in range(3) for cv in (0, 1) for it in range(n_items[bl])]

        def src_dst(bl, cv, it):
            if bl == 1:
                pr, tile = it // 2, it % 2
                s = (YP, HP)[cv][:, pr]
                d = (HP, YP)[cv][:, pr, 1 + 16 * tile:17 + 16 * tile, 1:1 + S1]
                return (lambda dy, dx: s[:, 16 * tile + dy:16 * tile + dy + 16, dx:dx + S1]), d, 512
            p0, p1 = 2 * it, min(2 * it + 2, PRS)
            s, d = ((YQ, HQ) if cv == 0 else (HQ, YQ))
            return (lambda dy, dx: s[:, p0:p1, dy:dy + S2, dx:dx + S2]), d[:, p0:p1, 1:1 + S2, 1:1 + S2], 256 * (p1 - p0)

        def psum(s, n, bl):
            o = P[:, s % 8, 0:n]
            return o.rearrange("p (r w) -> p r w", w=S1) if bl == 1 else o.rearrange("p (a r w) -> p a r w", r=S2, w=S2)

        hid_before = [sum(1 for q in steps[:s] if q[2] == 0) for s in range(len(steps) + 1)]
        res_before = [sum(1 for q in steps[:s] if q[2] == 1) for s in range(len(steps) + 1)]

        @block.sync
        def _(sp):
            sp.dma_start(gsum[:], k["gsum"]).then_inc(const_loaded, 16)
            sp.dma_start(bias[:], k["bias2"]).then_inc(const_loaded, 16)
            with sp.Fori(0, PRS) as pr:
                for bb in range(2):
                    sp.wait_ge(x_used, pr * 2 + bb + 1)
                    for h in range(2):
                        sp.dma_start(X[64 * h:64 * h + 64, bb], x2[pr * 2 + bb, :, HR * h:HR * h + HR, :].rearrange("c r w -> c (r w)")
                                     ).then_inc(x_loaded[bb], 16)
            sp.wait_ge(y2_ready, 1)
            for b in range(B):
                sp.dma_start(y2[b], YE[64 * (b % 2):64 * (b % 2) + 64, b // 2]).then_inc(y2_stored, 16)
            sp.wait_ge(y2_stored, 16 * B)

        @block.scalar
        def _(act):
            act.wait_ge(cleared, 1)
            for h in range(2):
                act.dma_start(WTS[64 * h:64 * h + 64, :, :, 64 * h:64 * h + 64].rearrange("p a t c -> p (a t) c"),
                              k["blocks"]).then_inc(weights_loaded, 16)
            with act.Fori(0, PRS) as pr:
                for bb in range(2):
                    b = pr * 2 + bb
                    act.wait_ge(negmean_ready, b + 1)
                    for m in range(4):
                        if m:
                            act.wait_ge(sq_ready, b * 4 + m)
                        nc.scalar.activation(SQ[:, :], X[:, bb, m * (NPX // 4):(m + 1) * (NPX // 4)], ACT.Square,
                                             bias=st[:, 1:2], accum_out=sq4[:, m:m + 1]).then_inc(sq_ready, 1)
                    act.wait_ge(vare_ready, b + 1)
                    nc.scalar.activation(st[:, 4:5], st[:, 3:4], ACT.Sqrt).then_inc(std_ready, 1)
            for s, (bl, la, cv, it) in enumerate(steps):
                if cv == 0:
                    _, d, n = src_dst(bl, cv, it)
                    w = (bl - 1) * 6 + la * 2
                    act.wait_ge(conv_done, s + 1)
                    nc.scalar.activation(d, psum(s, n, bl), ACT.Identity, bias=bias[:, w:w + 1]).then_inc(hid_ev, 1)

        @block.tensor
        def _(pe):
            pe.wait_ge(const_loaded, 32)
            with pe.Fori(0, PRS) as pr:
                for bb in range(2):
                    b = pr * 2 + bb
                    pe.wait_ge(sum_ready, b + 1)
                    nc.tensor.matmul(P[:, 0, 0:1], gsum[:, :], st[:, 0:1], start=True, stop=True).then_inc(mean_ready, 1)
                    pe.wait_ge(sqsum_ready, b + 1)
                    nc.tensor.matmul(P[:, 0, 0:1], gsum[:, :], st[:, 2:3], start=True, stop=True).then_inc(var_ready, 1)
            pe.wait_ge(weights_loaded, 32)
            pe.wait_ge(pooled, B)
            for s, (bl, la, cv, it) in enumerate(steps):
                f, _, n = src_dst(bl, cv, it)
                w = (bl - 1) * 6 + la * 2 + cv
                if s >= 8:
                    if steps[s - 8][2] == 0:
                        pe.wait_ge(hid_ev, hid_before[s - 7])
                    else:
                        pe.wait_ge(res_ready, res_before[s - 7])
                first = s - it
                if bl == 2 and la == 0 and cv == 0:
                    pe.wait_ge(maxed, 1)
                need = first - n_items[bl] + (it // 2 * 2 + 2 if bl == 1 else it + 1)
                if cv == 1:
                    pe.wait_ge(hid_ready, hid_before[need])
                elif la > 0:
                    pe.wait_ge(res_ready, res_before[need])
                for t in range(TAPS):
                    mm = nc.tensor.matmul(P[:, s % 8, 0:n], WTS[:, w, t, :], f(t // 3, t % 3), start=t == 0, stop=t == TAPS - 1)
                mm.then_inc(conv_done, 1)

        @block.vector
        def _(dve):
            v = nc.vector
            v.memset(WTS[:, :, :, :], 0.0).then_inc(cleared, 1)
            for t in (YP, HP, YQ, HQ):
                v.memset(t[:, :, :, :], 0.0).then_inc(chain_tail, 1)
            dve.wait_ge(chain_tail, 4)
            dve.sem_inc(x_used, 2)
            with dve.Fori(0, PRS) as pr:
                for bb in range(2):
                    b = pr * 2 + bb
                    CPER = 7
                    ch = Chain(dve, chain_dve, b * CPER, CPER)
                    dve.wait_ge(x_loaded[bb], pr * 32 + 32)
                    ch(v.tensor_reduce(POOL1[:, :, :], X[:, bb].rearrange("p (r q w) -> p r q w", r=HR, q=S1), AX_X, ALU.add))
                    ch(v.tensor_reduce(POOL2[:, :, :], POOL1[:, :, :].rearrange("p (a r) q -> p a q r", r=4), AX_X, ALU.add))
                    v.tensor_reduce(st[:, 0:1], POOL2[:, :, :].rearrange("p a q -> p (a q)"), AX_X, ALU.add).then_inc(sum_ready, 1)
                    dve.wait_ge(mean_ready, b + 1)
                    v.tensor_scalar(st[:, 1:2], P[:, 0, 0:1], -1.0, None, ALU.mult).then_inc(negmean_ready, 1)
                    dve.wait_ge(sq_ready, b * 4 + 4)
                    dve.sem_inc(x_used, 1)
                    v.tensor_reduce(st[:, 2:3], sq4[:, :], AX_X, ALU.add).then_inc(sqsum_ready, 1)
                    dve.wait_ge(var_ready, b + 1)
                    v.tensor_scalar(st[:, 3:4], P[:, 0, 0:1], GN_EPS, None, ALU.add).then_inc(vare_ready, 1)
                    dve.wait_ge(std_ready, b + 1)
                    ch(v.reciprocal(st[:, 5:6], st[:, 4:5]))
                    ch(v.tensor_scalar(st[:, 6:7], st[:, 1:2], st[:, 5:6], None, ALU.mult))
                    ch(v.tensor_scalar(st[:, 7:8], st[:, 5:6], 1.0 / 16, None, ALU.mult))
                    for h in range(2):
                        ins = v.tensor_scalar(YP[64 * bb:64 * bb + 64, pr, 1 + 16 * h:17 + 16 * h, 1:1 + S1],
                                              POOL2[64 * h:64 * h + 64], st[64 * h:64 * h + 64, 7:8],
                                              st[64 * h:64 * h + 64, 6:7], ALU.mult, ALU.add)
                        if h == 0:
                            ch(ins)
                        else:
                            ins.then_inc(pooled, 1)
                    dve.wait_ge(pooled, b + 1)
                    ch(v.tensor_copy(st[:, 8:9], st[:, 7:8]))
                    ch.done()
            for s, (bl, la, cv, it) in enumerate(steps):
                if bl == 2 and la == 0 and cv == 0 and it == 0:
                    dve.wait_ge(res_ready, res_before[s])
                    for pr in range(PRS):
                        yi = YP[:, pr, 1:1 + S1, 1:1 + S1]
                        v.tensor_tensor(MX[:, :, :], yi[:, :, 0:S1:2], yi[:, :, 1:S1:2], ALU.max).then_inc(chain_tail, 1)
                        dve.wait_ge(chain_tail, 4 + 2 * pr + 1)
                        v.tensor_tensor(YQ[:, pr, 1:1 + S2, 1:1 + S2], MX[:, 0:S1:2, :], MX[:, 1:S1:2, :], ALU.max
                                        ).then_inc(chain_tail, 1)
                        dve.wait_ge(chain_tail, 4 + 2 * pr + 2)
                    dve.sem_inc(maxed, 1)
                _, d, n = src_dst(bl, cv, it)
                if cv == 0:
                    dve.wait_ge(hid_ev, hid_before[s + 1])
                    items = [d] if bl == 1 else [d[:, q] for q in range(n // 256)]
                    for e in items:
                        ins = v.scalar_tensor_tensor(e, e, 0.1, e, ALU.mult, ALU.max)
                    ins.then_inc(hid_ready, 1)
                else:
                    w = (bl - 1) * 6 + la * 2 + 1
                    dve.wait_ge(conv_done, s + 1)
                    o = psum(s, n, bl)
                    items = [(d, o)] if bl == 1 else [(d[:, q], o[:, q]) for q in range(n // 256)]
                    for e, ps in items:
                        ins = v.scalar_tensor_tensor(e, ps, bias[:, w:w + 1], e, ALU.add, ALU.add)
                    ins.then_inc(res_ready, 1)
            dve.wait_ge(res_ready, res_before[-1])
            base = 4 + 2 * PRS
            v.tensor_copy(YE[:, :, 1:1 + S2, :], YQ[:, :, 1:1 + S2, 1:1 + S2]).then_inc(chain_tail, 1)
            v.tensor_copy(YE[:, :, 0, :], YQ[:, :, 1, 1:1 + S2]).then_inc(chain_tail, 1)
            v.tensor_copy(YE[:, :, S2 + 1, :], YQ[:, :, S2, 1:1 + S2]).then_inc(chain_tail, 1)
            dve.wait_ge(chain_tail, base + 3)
            dve.sem_inc(y2_ready, 1)


def layer2_apply(nc, B, x2, y2, x3, g3, k):
    BF16 = mybir.dt.bfloat16
    GROUPS = TapGroups((2, 1, 1, 2, 1, 1, 1))
    NS = 8
    NAP = S2 + 1
    CPER = 5
    with phase(nc) as named, ExitStack() as ctx:
        def sb(name, shape, dt=F32):
            return ctx.enter_context(nc.sbuf_tensor("d_" + name, shape, dt))

        def sem(name):
            return named("d_" + name)

        X = sb("X", [128, HR, W])
        G = sb("G", [128, PR, PW])
        T = sb("T", [128, HR, W])
        WT = sb("WT", [128, NAP // 2 + 1, TAPS, 2, C], BF16)
        U32 = sb("U32", [128, 2, 512])
        U = sb("U", [128, 2, 512], BF16)
        REST = sb("REST", [32, 2, TAPS, C])
        MID = sb("MID", [32, 2, TAPS, C], BF16)
        YE = sb("YE", [C + 1, S2 + 2, S2])
        tok = sb("tok", [C + 1, TAPS * C])
        ident = sb("ident", [128, 128])
        gsum = sb("gsum", [128, 128])
        st = sb("st", [128, 16])
        PROD = sb("PROD", [128, NS, TR, W])
        P = ctx.enter_context(nc.psum_tensor("d_P", [128, 8, 512], F32))
        const_loaded = sem("const_loaded")
        x_loaded = sem("x_loaded")
        y_loaded = sem("y_loaded")
        x_used = sem("x_used")
        y_used = sem("y_used")
        x3_stored = sem("x3_stored")
        g3_stored = sem("g3_stored")
        x3_ready = sem("x3_ready")
        passed = sem("passed")
        chain_dve = sem("chain_dve")
        sum_ready = sem("sum_ready")
        mean_ready = sem("mean_ready")
        negmean_ready = sem("negmean_ready")
        sq_ready = sem("sq_ready")
        var_ready = sem("var_ready")
        vare_ready = sem("vare_ready")
        std_ready = sem("std_ready")
        gnp_ready = sem("gnp_ready")
        gn_ready = sem("gn_ready")
        wt_done = sem("wt_done")
        hi_ready = sem("hi_ready")
        rest_ready = sem("rest_ready")
        mid_ready = sem("mid_ready")
        mid_stacked = sem("mid_stacked")
        low_ready = sem("low_ready")
        init_done = sem("init_done")
        u_ready = sem("u_ready")
        fil_done = sem("fil_done")
        prod_ready = sem("prod_ready")
        prod_used = sem("prod_used")
        added = sem("added")
        acc_done = sem("acc_done")
        acc_ev = sem("acc_ev")
        g3_ready = sem("g3_ready")
        consts = [(ident[:], k["ident"]), (gsum[:], k["gsum"]), (tok[0:C], k["tok"]), (tok[C:C + 1], k["tokb"])]
        consts += [(U32[32 * part:32 * part + 32], k["U"]) for part in range(3)]
        block = ctx.enter_context(nc.Block())
        CUT = ((0, 5), (5, TAPS))

        def inner(t):
            return t[:, 1:1 + HR, 1:1 + W]

        def halves(a):
            return [h for h in range(2) if h * 8 <= a <= h * 8 + 8]

        def filters(a, u):
            n0, n1 = CUT[u]
            return P[0:32, (2 * a + u) % 4, 0:(n1 - n0) * C].rearrange("p (t c) -> p t c", c=C)

        @block.sync
        def _(sp):
            sp.wait_ge(init_done, 3)
            for t, src in consts:
                sp.dma_start(t, src).then_inc(const_loaded, 16)
            with sp.Fori(0, B) as b:
                sp.wait_ge(y_used, b + 1)
                sp.dma_start(YE[0:C, :, :], y2[b]).then_inc(y_loaded, 16)
                sp.wait_ge(x_used, b + 1)
                for h in range(2):
                    sp.dma_start(X[64 * h:64 * h + 64], x2[b, :, HR * h:HR * h + HR, :]).then_inc(x_loaded, 16)
                sp.wait_ge(x3_ready, b + 1)
                for h in range(2):
                    sp.dma_start(x3[b, HR * h:HR * h + HR, :, :].rearrange("y c x -> c y x"), T[64 * h:64 * h + 64]
                                 ).then_inc(x3_stored, 16)
                sp.wait_ge(g3_ready, b + 1)
                for h in range(2):
                    sp.dma_start(g3[b, HR * h:HR * h + HR, :, :].rearrange("y c x -> c y x"), inner(G)[64 * h:64 * h + 64]
                                 ).then_inc(g3_stored, 16)
            sp.wait_ge(x3_stored, 32 * B + 1)
            sp.wait_ge(g3_stored, 32 * B + 1)

        @block.scalar
        def _(act):
            with act.Fori(0, B) as b:
                gate(act, negmean_ready, b * 2 + 1, passed)
                gate(act, x3_stored, b * 32 + 1, passed)
                gate(act, g3_stored, b * 32 + 1, passed)
                nc.scalar.activation(inner(G), X[:, :, :], ACT.Square, bias=st[:, 1:2], accum_out=st[:, 2:3]
                                     ).then_inc(sq_ready, 1)
                act.wait_ge(vare_ready, b * 2 + 1)
                nc.scalar.activation(st[:, 4:5], st[:, 3:4], ACT.Sqrt).then_inc(std_ready, 1)
                act.wait_ge(gnp_ready, b * 2 + 1)
                nc.scalar.activation(inner(G), X[:, :, :], ACT.Identity, bias=st[:, 6:7], scale=st[:, 5:6]
                                     ).then_inc(gn_ready, 1)
                for a in range(NAP):
                    act.wait_ge(wt_done, b * NAP + a + 1)
                    for h in halves(a):
                        for u, (n0, n1) in enumerate(CUT):
                            ins = nc.scalar.activation(WT[0:32, a - 8 * h, n0:n1, h, :], filters(a, u), ACT.Copy)
                    ins.then_inc(hi_ready, 1)
                    act.wait_ge(rest_ready, b * NAP + a + 1)
                    if a >= 2:
                        act.wait_ge(low_ready, b * NAP + a - 1)
                    nc.scalar.activation(MID[:, a % 2], REST[:, a % 2], ACT.Copy).then_inc(mid_ready, 1)
                    for h in halves(a):
                        ins = nc.scalar.activation(WT[32:64, a - 8 * h, :, h, :], REST[:, a % 2], ACT.Copy)
                    ins.then_inc(mid_stacked, 1)
                act.wait_ge(negmean_ready, b * 2 + 2)
                nc.scalar.activation(inner(G), T[:, :, :], ACT.Square, bias=st[:, 1:2], accum_out=st[:, 2:3]
                                     ).then_inc(sq_ready, 1)
                act.wait_ge(vare_ready, b * 2 + 2)
                nc.scalar.activation(st[:, 4:5], st[:, 3:4], ACT.Sqrt).then_inc(std_ready, 1)
                act.wait_ge(gnp_ready, b * 2 + 2)
                nc.scalar.activation(inner(G), T[:, :, :], ACT.Identity, bias=st[:, 6:7], scale=st[:, 5:6]
                                     ).then_inc(g3_ready, 1)

        @block.tensor
        def _(pe):
            pe.wait_ge(const_loaded, 16 * len(consts))
            pe.wait_ge(u_ready, 1)

            def stats(n):
                gate(pe, sum_ready, n + 1, passed)
                nc.tensor.matmul(P[:, 7, 0:1], gsum[:, :], st[:, 0:1], start=True, stop=True).then_inc(mean_ready, 1)
                gate(pe, sq_ready, n + 1, passed)
                nc.tensor.matmul(P[:, 7, 0:1], gsum[:, :], st[:, 2:3], start=True, stop=True).then_inc(var_ready, 1)

            with pe.Fori(0, B) as b:
                stats(b * 2)
                gate(pe, y_loaded, b * 16 + 16, passed)
                for a in range(NAP):
                    if a >= 2:
                        gate(pe, rest_ready, b * NAP + a - 1, passed)
                    for u, (n0, n1) in enumerate(CUT):
                        mm = nc.tensor.matmul(P[0:32, (2 * a + u) % 4, 0:(n1 - n0) * C], YE[:, a:a + 2, :].rearrange("p a w -> p (a w)"),
                                              tok[:, n0 * C:n1 * C], start=True, stop=True)
                    mm.then_inc(wt_done, 1)
                gate(pe, gn_ready, b + 1, passed)
                gate(pe, mid_stacked, b * NAP + NAP, passed)
                gate(pe, low_ready, b * NAP + NAP, passed)
                steps = [(n, t) for n in range(NT) for t in range(TAPS)]
                LAG = 3
                for s in range(len(steps) + LAG):
                    if s < len(steps):
                        n, t = steps[s]
                        if s >= 4:
                            gate(pe, prod_ready, b * NT * TAPS + s - 3, passed)
                        a = (n + 1) // 2
                        nc.tensor.matmul(P[:, s % 4, :], WT[:, a, t].rearrange("p h c -> p (h c)"), U[:, n % 2, :],
                                         start=True, stop=True).then_inc(fil_done, 1)
                    if s >= LAG:
                        n, t = steps[s - LAG]
                        if not GROUPS.is_last(t):
                            continue
                        g, f = GROUPS.group(t), GROUPS.first(t)
                        if f == t:
                            pe.wait_ge(prod_ready, b * NT * TAPS + s - LAG + 1)
                        else:
                            pe.wait_ge(added, (b * NT + n) * GROUPS.adds + GROUPS.adds_to(t))
                        if g == 0 and n >= 2:
                            pe.wait_ge(acc_ev, b * NT + n - 1)
                        mm = nc.tensor.matmul(P[:, 4 + n % 2, :], ident[:, :], PROD[:, (n * TAPS + f) % NS],
                                              start=g == 0, stop=g == GROUPS.n - 1)
                        mm.then_inc(acc_done if g == GROUPS.n - 1 else prod_used, 1)
                stats(b * 2 + 1)

        @block.vector
        def _(dve):
            v = nc.vector
            v.memset(U32[:, :, :], 0.0).then_inc(init_done, 1)
            v.memset(WT[:, :, :, :, :], 0.0).then_inc(init_done, 1)
            v.memset(YE[C:C + 1, :, :], 1.0).then_inc(init_done, 1)
            dve.wait_ge(const_loaded, 16 * len(consts))
            v.tensor_copy(U[:, :, :], U32[:, :, :]).then_inc(u_ready, 1)
            dve.sem_inc(x_used, 1)
            dve.sem_inc(y_used, 1)
            dve.sem_inc(x3_stored, 1)
            dve.sem_inc(g3_stored, 1)
            with dve.Fori(0, B) as b:
                ch = Chain(dve, chain_dve, b * CPER, CPER)

                def stats(n, t):
                    v.tensor_reduce(st[:, 0:1], t[:, :, :].rearrange("p r w -> p (r w)"), AX_X, ALU.add).then_inc(sum_ready, 1)
                    dve.wait_ge(mean_ready, n + 1)
                    v.tensor_scalar(st[:, 1:2], P[:, 7, 0:1], -1.0, None, ALU.mult).then_inc(negmean_ready, 1)
                    dve.wait_ge(var_ready, n + 1)
                    v.tensor_scalar(st[:, 3:4], P[:, 7, 0:1], GN_EPS, None, ALU.add).then_inc(vare_ready, 1)
                    dve.wait_ge(std_ready, n + 1)
                    ch(v.reciprocal(st[:, 5:6], st[:, 4:5]))
                    v.tensor_scalar(st[:, 6:7], st[:, 1:2], st[:, 5:6], None, ALU.mult).then_inc(gnp_ready, 1)

                dve.wait_ge(x_loaded, b * 32 + 32)
                stats(b * 2, X)
                for a in range(NAP):
                    dve.wait_ge(hi_ready, b * NAP + a + 1)
                    if a >= 2:
                        dve.wait_ge(mid_stacked, b * NAP + a - 1)
                    for u, (n0, n1) in enumerate(CUT):
                        h = halves(a)[0]
                        ins = v.tensor_tensor(REST[:, a % 2, n0:n1], filters(a, u), WT[0:32, a - 8 * h, n0:n1, h, :], ALU.subtract)
                    ins.then_inc(rest_ready, 1)
                    dve.wait_ge(mid_ready, b * NAP + a + 1)
                    for h in halves(a):
                        ins = v.tensor_tensor(WT[64:96, a - 8 * h, :, h, :], REST[:, a % 2], MID[:, a % 2], ALU.subtract)
                    ins.then_inc(low_ready, 1)
                dve.wait_ge(gn_ready, b + 1)
                ch(v.tensor_copy(G[:, 1:1 + HR, 0:1], G[:, 1:1 + HR, 1:2]))
                ch(v.tensor_copy(G[:, 1:1 + HR, PW - 1:PW], G[:, 1:1 + HR, PW - 2:PW - 1]))
                v.tensor_copy(G[0:64, 0, :], G[0:64, 1, :])
                v.tensor_copy(G[64:128, PR - 1, :], G[64:128, PR - 2, :])
                v.tensor_copy(G[0:64, PR - 1, :], G[64:128, 1, :])
                ch(v.tensor_copy(G[64:128, 0, :], G[0:64, HR, :]))

                def total(n):
                    dve.wait_ge(acc_done, b * NT + n + 1)
                    if n == 0:
                        dve.wait_ge(x3_stored, b * 32 + 1)
                    v.tensor_tensor(T[:, TR * n:TR * n + TR, :], P[:, 4 + n % 2, :].rearrange("p (r w) -> p r w", r=TR),
                                    X[:, TR * n:TR * n + TR, :], ALU.add).then_inc(acc_ev, 1)

                def add(s):
                    n, t = s // TAPS, s % TAPS
                    f = n * TAPS + GROUPS.first(t)
                    dve.wait_ge(prod_ready, b * NT * TAPS + s + 1)
                    if s - f > 1:
                        dve.wait_ge(added, (b * NT + n) * GROUPS.adds + GROUPS.adds_to(t) - 1)
                    v.tensor_tensor(PROD[:, f % NS], PROD[:, f % NS], PROD[:, s % NS], ALU.add).then_inc(added, 1)

                for n in range(NT):
                    for t in range(TAPS):
                        dy, dx = t // 3, t % 3
                        s = n * TAPS + t
                        dve.wait_ge(fil_done, b * NT * TAPS + s + 1)
                        if s >= NS:
                            n8, t8 = (s - NS) // TAPS, (s - NS) % TAPS
                            if t8 != GROUPS.first(t8):
                                dve.wait_ge(added, (b * NT + n8) * GROUPS.adds + GROUPS.adds_to(t8))
                            elif GROUPS.group(t8) == GROUPS.n - 1:
                                dve.wait_ge(acc_done, b * NT + n8 + 1)
                            else:
                                dve.wait_ge(prod_used, (b * NT + n8) * (GROUPS.n - 1) + GROUPS.group(t8) + 1)
                        v.tensor_tensor(PROD[:, s % NS], P[:, s % 4, :].rearrange("p (r w) -> p r w", r=TR),
                                        G[:, TR * n + dy:TR * n + dy + TR, dx:dx + W], ALU.mult).then_inc(prod_ready, 1)
                        if s >= 1 and (s - 1) % TAPS != GROUPS.first((s - 1) % TAPS):
                            add(s - 1)
                        if t == 5 and n >= 1:
                            total(n - 1)
                total(NT - 1)
                dve.wait_ge(acc_ev, b * NT + NT)
                dve.sem_inc(x_used, 1)
                dve.sem_inc(y_used, 1)
                dve.sem_inc(x3_ready, 1)
                stats(b * 2 + 1, T)
                ch.done()



NM = 16
NF = 2 * NM
UP = 2.0 ** 30


def layer3_modes(nc, B, g3, modes, k):
    MB = 64
    NCH = NF * NM // MB
    with phase(nc) as named, ExitStack() as ctx:
        def sb(name, shape, dt=F32):
            return ctx.enter_context(nc.sbuf_tensor("e_" + name, shape, dt))

        def sem(name):
            return named("e_" + name)

        GY = sb("GY", [128, 2, C, W])
        T1 = sb("T1", [128, 2, C, NF])
        XM = sb("XM", [128, NF * NM, B])
        WA = sb("WA", [128, 2, MB * C])
        WN = sb("WN", [128, 2, MB * C])
        OM = sb("OM", [C, NF, NM, B])
        OF = sb("OF", [NF, 2, C, NM])
        crow = sb("crow", [128, NF])
        ccol = sb("ccol", [128, 2, NM])
        sign = sb("sign", [128, 1])
        ident = sb("ident", [128, 128])
        P = ctx.enter_context(nc.psum_tensor("e_P", [128, 8, 512], F32))
        const_loaded = sem("const_loaded")
        g_loaded = [sem("g_loaded0"), sem("g_loaded1")]
        w_loaded = [sem("w_loaded0"), sem("w_loaded1")]
        rows_done = sem("rows_done")
        rows_ev = sem("rows_ev")
        cols_done = sem("cols_done")
        cols_ev = sem("cols_ev")
        w_ready = sem("w_ready")
        mix_done = sem("mix_done")
        mix_ev = sem("mix_ev")
        turn_done = sem("turn_done")
        turn_ev = sem("turn_ev")
        modes_stored = [sem("modes_stored0"), sem("modes_stored1")]
        passed = sem("passed")
        consts = [(crow, "crow"), (ccol, "ccol"), (sign, "sign"), (ident, "ident")]
        block = ctx.enter_context(nc.Block())

        @block.sync
        def _(sp):
            for t, name in consts:
                sp.dma_start(t[:], k[name]).then_inc(const_loaded, 16)
            for b in range(B):
                if b >= 2:
                    sp.wait_ge(rows_done, (b - 1) * 4)
                sp.dma_start(GY[:, b % 2], g3[b]).then_inc(g_loaded[b % 2], 16)
            for b in range(B):
                sp.wait_ge(turn_ev, 2 * b + 2)
                sp.dma_start(modes[b], OF[:, b % 2].rearrange("p o g -> p (o g)")).then_inc(modes_stored[b % 2], 16)
            for n in range(2):
                sp.wait_ge(modes_stored[n], 16 * (B // 2))

        @block.gpsimd
        def _(pool):
            for n in range(NCH):
                if n >= 2:
                    pool.wait_ge(mix_done, n - 1)
                for t, name in ((WA, "w_at"), (WN, "w_neg")):
                    for h in range(2):
                        pool.dma_start(t[64 * h:64 * h + 64, n % 2, :], k[name][:, n * MB * C:(n + 1) * MB * C]
                                       ).then_inc(w_loaded[n % 2], 16)

        @block.tensor
        def _(pe):
            pe.wait_ge(const_loaded, 16 * len(consts))
            for b in range(B):
                pe.wait_ge(g_loaded[b % 2], 16 * (b // 2) + 16)
                for q in range(4):
                    n = b * 4 + q
                    if n >= 4:
                        pe.wait_ge(rows_ev, n - 3)
                    for c in range(16):
                        mm = nc.tensor.matmul(P[:, q, NF * c:NF * c + NF], GY[:, b % 2, q * 16 + c, :], crow[:, :],
                                              start=True, stop=True)
                    mm.then_inc(rows_done, 1)
                pe.wait_ge(rows_ev, 4 * b + 4)
                if b >= 2:
                    pe.wait_ge(cols_ev, b - 1)
                for s in range(2):
                    for f in range(NF):
                        fs = f if s == 0 else f // NM * NM + (-f) % NM
                        mm = nc.tensor.matmul(P[64 * s:64 * s + 64, 4 + b % 2, NM * f:NM * f + NM], T1[:, b % 2, :, fs],
                                              ccol[:, s, :], start=True, stop=True)
                mm.then_inc(cols_done, 1)
            pe.wait_ge(cols_ev, B)
            for n in range(NCH):
                pe.wait_ge(w_ready, n + 1)
                if n >= 2:
                    pe.wait_ge(mix_ev, n - 1)
                for m in range(MB):
                    mm = nc.tensor.matmul(P[0:64, 6 + n % 2, B * m:B * m + B], WA[:, n % 2, C * m:C * m + C],
                                          XM[:, n * MB + m, :], start=True, stop=True)
                mm.then_inc(mix_done, 1)
            pe.wait_ge(mix_ev, NCH)
            for n in range(2 * B):
                if n >= 4:
                    pe.wait_ge(turn_ev, n - 3)
                for g in range(8):
                    mm = nc.tensor.transpose(P[0:NF, n % 4, C * g:C * g + C], OM[:, :, (n % 2) * 8 + g, n // 2], ident[0:C, 0:C])
                mm.then_inc(turn_done, 1)

        @block.scalar
        def _(act):
            for b in range(B):
                for q in range(4):
                    act.wait_ge(rows_done, b * 4 + q + 1)
                    if b >= 2:
                        act.wait_ge(cols_done, b - 1)
                    nc.scalar.activation(T1[:, b % 2, 16 * q:16 * q + 16, :], P[:, q, :].rearrange("p (c f) -> p c f", f=NF),
                                         ACT.Copy).then_inc(rows_ev, 1)

        @block.vector
        def _(dve):
            v = nc.vector
            dve.wait_ge(const_loaded, 16 * len(consts))
            for b in range(B):
                dve.wait_ge(cols_done, b + 1)
                v.tensor_copy(XM[:, :, b], P[:, 4 + b % 2, :]).then_inc(cols_ev, 1)
            for n in range(NCH):
                dve.wait_ge(w_loaded[n % 2], 64 * (n // 2) + 64)
                v.scalar_tensor_tensor(WA[:, n % 2], WN[:, n % 2], sign[:, 0:1], WA[:, n % 2], ALU.mult, ALU.add
                                       ).then_inc(w_ready, 1)
                if n >= 1:
                    dve.wait_ge(mix_done, n)
                    v.tensor_copy(OM[:, :, :, :].rearrange("p f g b -> p (f g b)")[:, MB * B * (n - 1):MB * B * n], P[0:64, 6 + (n - 1) % 2, 0:MB * B]
                                  ).then_inc(mix_ev, 1)
            dve.wait_ge(mix_done, NCH)
            v.tensor_copy(OM[:, :, :, :].rearrange("p f g b -> p (f g b)")[:, MB * B * (NCH - 1):], P[0:64, 6 + (NCH - 1) % 2, 0:MB * B]
                          ).then_inc(mix_ev, 1)
            for n in range(2 * B):
                dve.wait_ge(turn_done, n + 1)
                if n >= 4:
                    dve.wait_ge(modes_stored[n // 2 % 2], 16 * (n // 4))
                v.tensor_copy(OF[:, n // 2 % 2, :, (n % 2) * 8:(n % 2) * 8 + 8], P[0:NF, n % 4, :].rearrange("p (g o) -> p o g", o=C)
                              ).then_inc(turn_ev, 1)


def layer3_phase(nc, B, x3, g3, modes, out, k):
    CG = 4
    NG = C // CG
    with phase(nc) as named, ExitStack() as ctx:
        def sb(name, shape, dt=F32):
            return ctx.enter_context(nc.sbuf_tensor("f_" + name, shape, dt))

        def sem(name):
            return named("f_" + name)

        XY = sb("XY", [128, 2, C, W])
        GY = sb("GY", [128, 2, C, W])
        MO = sb("MO", [NF, 2, C * NM])
        T2 = sb("T2", [128, 2, CG, 2 * W])
        SC = sb("SC", [128, 2, CG * W])
        SS = sb("SS", [128, 2, CG * W])
        ZZ = sb("ZZ", [128, 2, CG * W])
        RT = sb("RT", [128, 2, CG * W])
        IV = sb("IV", [128, 2, 128])
        cas2 = sb("cas2", [128, 2 * W])
        casup = sb("casup", [128, 2 * W])
        cinv1 = sb("cinv1", [NF, W])
        cblk = sb("cblk", [128, 2, CG * W])
        P = ctx.enter_context(nc.psum_tensor("f_P", [128, 8, 512], F32))
        const_loaded = sem("const_loaded")
        loaded = [sem("loaded0"), sem("loaded1")]
        stored = sem("stored")
        passed = sem("passed")
        batch_free = sem("batch_free")
        first_done = sem("first_done")
        first_ev = sem("first_ev")
        second_done = sem("second_done")
        inv1_done = sem("inv1_done")
        inv1_ev = sem("inv1_ev")
        inv2_done = sem("inv2_done")
        cos_sq = sem("cos_sq")
        sin_sq = sem("sin_sq")
        root_ready = sem("root_ready")
        squares_ready = sem("squares_ready")
        step = sem("step")
        cos_read = sem("cos_read")
        y_read = sem("y_read")
        slots_used = sem("slots_used")
        out_ready = sem("out_ready")
        consts = [(cas2, "cas2"), (casup, "casup"), (cinv1, "cinv1"), (cblk, "cblk")]
        block = ctx.enter_context(nc.Block())
        PRS = B // 2

        @block.sync
        def _(sp):
            for t, name in consts:
                sp.dma_start(t[:], k[name]).then_inc(const_loaded, 16)

            def load(b, bb):
                sp.dma_start(GY[:, bb], g3[b]).then_inc(loaded[bb], 16)
                sp.dma_start(XY[:, bb], x3[b]).then_inc(loaded[bb], 16)
                sp.dma_start(MO[:, bb], modes[b]).then_inc(loaded[bb], 16)
            for b in range(B):
                if b < 2:
                    load(b, b % 2)
            for b in range(B):
                sp.wait_ge(out_ready, b * NG + NG)
                sp.dma_start(out[b].rearrange("c y x -> y c x"), XY[:, b % 2]).then_inc(stored, 16)
                if b + 2 < B:
                    sp.wait_ge(stored, 16 * b + 16)
                    load(b + 2, b % 2)
            sp.wait_ge(stored, 16 * B)

        @block.tensor
        def _(pe):
            pe.wait_ge(const_loaded, 16 * len(consts))
            with pe.Fori(0, PRS) as pr:
                for bb in range(2):
                    def first(i):
                        n = (pr * 2 + bb) * NG + i
                        gate(pe, first_ev, n + 1, passed)
                        for c in range(CG):
                            mm = nc.tensor.matmul(P[:, c // 2, (c % 2) * 256:(c % 2) * 256 + 256], GY[:, bb, i * CG + c, :],
                                                  cas2[:, :], start=True, stop=True)
                        mm.then_inc(first_done, 1)

                    def second(i):
                        n = (pr * 2 + bb) * NG + i
                        gate(pe, first_ev, n + 2, passed)
                        gate(pe, cos_read, n + 1, passed)
                        gate(pe, sin_sq, n + 1, passed)
                        for s in range(2):
                            for c in range(CG):
                                mm = nc.tensor.matmul(P[:, 2 + 2 * s + i % 2, c * W:c * W + W], T2[:, i % 2, c, s * W:s * W + W],
                                                      casup[:, s * W:s * W + W], start=True, stop=True)
                        mm.then_inc(second_done, 1)

                    def inverse(i):
                        n = (pr * 2 + bb) * NG + i
                        if i % 2 == 0:
                            gate(pe, inv1_ev, (pr * 2 + bb) * (NG // 2) + i // 2 + 1, passed)
                            nc.tensor.matmul(P[:, 7, 0:128], MO[:, bb, i // 2 * 128:i // 2 * 128 + 128], cinv1[:, :],
                                             start=True, stop=True).then_inc(inv1_done, 1)
                            gate(pe, inv1_ev, (pr * 2 + bb) * (NG // 2) + i // 2 + 2, passed)
                        gate(pe, y_read, n + 1, passed)
                        nc.tensor.matmul(P[:, 6, :], IV[:, i // 2 % 2, :], cblk[:, i % 2, :], start=True, stop=True
                                         ).then_inc(inv2_done, 1)

                    gate(pe, loaded[bb], pr * 48 + 48, passed)
                    first(0)
                    for i in range(NG):
                        if i + 1 < NG:
                            first(i + 1)
                        second(i)
                        inverse(i)

        @block.scalar
        def _(act):
            act.sem_inc(first_ev, 1)
            act.sem_inc(sin_sq, 2)
            with act.Fori(0, PRS) as pr:
                for bb in range(2):
                    def evict(i):
                        n = (pr * 2 + bb) * NG + i
                        act.wait_ge(first_done, n + 1)
                        nc.scalar.activation(T2[:, i % 2].rearrange("p c w -> p (c w)"), P[:, 0:2, :].rearrange("p a w -> p (a w)"),
                                             ACT.Copy).then_inc(first_ev, 1)

                    def root(i):
                        n = (pr * 2 + bb) * NG + i
                        act.wait_ge(squares_ready, n + 1)
                        nc.scalar.activation(RT[:, i % 2], SC[:, i % 2], ACT.Sqrt).then_inc(root_ready, 1)
                    evict(0)
                    for i in range(NG):
                        n = (pr * 2 + bb) * NG + i
                        if i + 1 < NG:
                            evict(i + 1)
                        act.wait_ge(second_done, n + 1)
                        act.wait_ge(slots_used, n + 1)
                        nc.scalar.activation(SC[:, i % 2], P[:, 2 + i % 2, :], ACT.Square).then_inc(cos_sq, 1)
                        nc.scalar.activation(SS[:, i % 2], P[:, 4 + i % 2, :], ACT.Square).then_inc(sin_sq, 1)
                        if i >= 1:
                            root(i - 1)
                    root(NG - 1)

        @block.vector
        def _(dve):
            v = nc.vector
            dve.sem_inc(inv1_ev, 1)
            dve.sem_inc(y_read, 1)
            dve.sem_inc(cos_read, 2)
            dve.sem_inc(slots_used, 2)
            with dve.Fori(0, PRS) as pr:
                for bb in range(2):
                    ch = Chain(dve, step, (pr * 2 + bb) * (NG * 4), NG * 4)

                    def squares(i):
                        n = (pr * 2 + bb) * NG + i
                        dve.wait_ge(cos_sq, n + 1)
                        dve.wait_ge(sin_sq, n + 3)
                        ch(v.tensor_tensor(SS[:, i % 2], SS[:, i % 2], SC[:, i % 2], ALU.add))
                        v.scalar_tensor_tensor(ZZ[:, i % 2], SS[:, i % 2], 0.0, P[:, 2 + i % 2, :], ALU.is_equal, ALU.add
                                               ).then_inc(cos_read, 1)
                        v.scalar_tensor_tensor(SC[:, i % 2], SS[:, i % 2], 0.0, SS[:, i % 2], ALU.is_equal, ALU.add
                                               ).then_inc(squares_ready, 1)

                    def finish(i):
                        n = (pr * 2 + bb) * NG + i
                        x = XY[:, bb, CG * i:CG * i + CG, :].rearrange("p c w -> p (c w)")
                        dve.wait_ge(root_ready, n + 1)
                        ch(v.reciprocal(RT[:, i % 2], RT[:, i % 2]))
                        dve.wait_ge(cos_read, n + 3)
                        ch(v.tensor_tensor(ZZ[:, i % 2], ZZ[:, i % 2], RT[:, i % 2], ALU.mult))
                        dve.wait_ge(inv2_done, n + 1)
                        v.tensor_tensor(ZZ[:, i % 2], ZZ[:, i % 2], P[:, 6, :], ALU.mult).then_inc(y_read, 1)
                        dve.wait_ge(y_read, n + 2)
                        ch(v.tensor_tensor(x, x, ZZ[:, i % 2], ALU.add))
                        dve.sem_inc(out_ready, 1)
                        dve.sem_inc(slots_used, 1)

                    dve.wait_ge(loaded[bb], pr * 48 + 48)
                    for i in range(NG):
                        if i % 2 == 0:
                            dve.wait_ge(inv1_done, (pr * 2 + bb) * (NG // 2) + i // 2 + 1)
                            v.tensor_copy(IV[:, i // 2 % 2, :], P[:, 7, 0:128]).then_inc(inv1_ev, 1)
                        squares(i)
                        if i >= 1:
                            finish(i - 1)
                    finish(NG - 1)
                    ch.done()


def cas(n):
    j = np.arange(n, dtype=np.float32)
    a = (np.float32(2.0 * np.pi) / np.float32(n) * (j[:, None] * j[None, :])).astype(np.float32)
    return (np.cos(a) + np.sin(a)).astype(np.float32)


def constants():
    f = np.float32
    k = {}
    part = np.arange(128)
    c = part % C
    k["iota"] = np.tile(np.arange(128, dtype=f), (128, 1))
    k["ident"] = np.eye(128, dtype=f)
    k["anti"] = np.eye(128, dtype=f)[::-1]
    k["gsum"] = (c[:, None] // 2 == c[None, :] // 2).astype(f) / f(2 * W * W)
    k["shift"] = np.stack([c[:, None] == c[None, :] + m - 1 for m in range(3)], 1).astype(f) / f(W * W)
    line = np.linspace(-1, 1, W, dtype=f) * f((W - 1) / 2)
    k["jc"] = np.stack([line, -line], 1)
    k["ic"] = np.tile(line[:HR], (128, 1))
    k["base"] = np.tile(np.linspace(0, 180, NA, dtype=f), (128, 1))
    pos = np.arange(W, dtype=f) * f((NA - 1) / (W - 1))
    k["ftab"] = np.tile((pos - np.minimum(np.floor(pos), NA - 2)).astype(f), (128, 1))
    k["one"] = np.ones((1, 32), f)
    src = (np.arange(W) + 0.5) / 8 - 0.5
    i0 = np.floor(src).astype(int)
    col = np.zeros((S2, W))
    for x in range(W):
        col[max(i0[x], 0), x] += 1 - (src[x] - i0[x])
        col[min(i0[x] + 1, S2 - 1), x] += src[x] - i0[x]
    u = np.zeros((2, S2, 2, TR, W))
    for odd in range(2):
        for r in range(TR):
            low = ((TR * odd + r + 0.5) / 8 - 0.5) % 1
            u[0, :, odd, r] = (1 - low) * col
            u[1, :, odd, r] = low * col
    k["U"] = u.reshape(32, 2, TR * W).astype(f)
    full = cas(W)
    kept = np.r_[0:NM, W - NM:W]
    g = np.arange(NM)
    k["crow"] = full[:, kept]
    k["ccol"] = np.stack([full[:, g], full[:, (-g) % NM]], 1)
    k["sign"] = np.repeat(np.array([1, -1], f), C)[:, None]
    k["cas2"] = np.concatenate([full, full[::-1]], 1)
    k["casup"] = k["cas2"] * f(UP)
    k["cinv1"] = full[kept] * f(0.5 / (W * W))
    cb = np.zeros((8, NM, 2, 4, W), f)
    for o in range(8):
        cb[o, :, o // 4, o % 4, :] = full[:NM]
    k["cblk"] = cb.reshape(128, 2, 4 * W)
    return k


def layouts(a):
    k = {}
    twice = lambda v: np.tile(v, 2)
    k["lin1"] = a["L0_conv_lin1_w"].reshape(32, C, 2, 2, 4).transpose(2, 1, 3, 4, 0).reshape(128, 8, 32)
    k["lin2"] = a["L0_conv_lin2_w"].T
    k["lin1b"] = a["L0_conv_lin1_b"][:, None]
    k["lin2b"] = np.tile(a["L0_conv_lin2_b"], (128, 1))
    k["wf0"] = np.tile(a["L0_conv_wf0"].reshape(1, 3), (C, 1))
    k["wf1"] = np.tile(a["L0_conv_wf1"].reshape(1, 5), (C, 1))
    k["fuse"] = a["L0_conv_fuse_w"].reshape(C, C, 2).transpose(1, 2, 0)
    k["bn"] = np.stack([twice(a["L0_conv_" + n]) for n in ("bn_gamma", "bn_beta", "bn_mean", "bn_var", "fuse_b")], 1)
    k["w0"] = a["L1_conv_w0"].transpose(1, 2, 3, 0).reshape(C, TAPS, C)
    k["wf"] = a["L1_conv_wf"].transpose(1, 2, 3, 0).reshape(C, TAPS, C)
    k["w3"] = a["L1_conv_w3"].reshape(C, TAPS, C).transpose(2, 1, 0)
    k["w1"] = np.tile(a["L1_conv_w1"].reshape(C, TAPS), (2, 1))
    k["b3"] = np.tile(a["L1_conv_b3"].reshape(C, TAPS), (2, 1))
    k["w2"] = np.tile(a["L1_conv_w2"].reshape(1, 3), (128, 1))
    k["bias1"] = np.stack([twice(a["L1_conv_b0"]), twice(a["L1_conv_b1"]), np.tile(a["L1_conv_b2"], 128),
                           twice(a["L1_conv_bf"])], 1)
    convs = [(b, n, j) for b in ("blk1", "blk2") for n in range(3) for j in "12"]
    k["blocks"] = np.stack([a[f"L2_conv_{b}_w{j}"][n].transpose(1, 2, 3, 0).reshape(C, TAPS, C) for b, n, j in convs], 1
                           ).reshape(C, -1, C)
    k["bias2"] = np.stack([twice(a[f"L2_conv_{b}_b{j}"][n]) for b, n, j in convs], 1)
    k["tok"] = a["L2_conv_tok_w"].reshape(C, TAPS, C).transpose(2, 1, 0).reshape(C, TAPS * C)
    k["tokb"] = a["L2_conv_tok_b"].reshape(C, TAPS).T.reshape(1, TAPS * C)
    w = np.stack([a["L3_conv_weights1"], a["L3_conv_weights2"]])
    neg = (-np.arange(NM)) % NM
    k["w_at"] = w.transpose(1, 0, 3, 4, 2).reshape(C, -1)
    k["w_neg"] = w[:, :, :, neg][:, :, :, :, neg].transpose(1, 0, 3, 4, 2).reshape(C, -1)
    return k


def program(nc, x, out, k):
    B = x.shape[0]

    def scratch(name, shape):
        return nc.dram_tensor(name, shape, F32, kind="Internal").ap()

    x1 = scratch("x1_dram", (B, C, W, W))
    x2 = scratch("x2_dram", (B, C, W, W))
    y2 = scratch("y2_dram", (B, C, S2 + 2, S2))
    x3 = scratch("x3_dram", (B, W, C, W))
    g3 = scratch("g3_dram", (B, W, C, W))
    modes = scratch("modes_dram", (B, NF, C * NM))
    layer0(nc, B, x, x1, k)
    layer1(nc, B, x1, x2, k)
    layer2_small(nc, B, x2, y2, k)
    layer2_apply(nc, B, x2, y2, x3, g3, k)
    layer3_modes(nc, B, g3, modes, k)
    layer3_phase(nc, B, x3, g3, modes, out, k)


def kernel(**inputs):
    import concourse.bacc as _bacc
    from concourse.bass_utils import run_bass_kernel_spmd as _run

    nc = _bacc.Bacc("TRN2", target_bir_lowering=False, num_devices=1)
    a = {name: np.ascontiguousarray(v) for name, v in inputs.items()}
    arrays = {"in_x_dram": a["x"]}
    for name, v in {**constants(), **layouts(a)}.items():
        arrays[f"in_{name}_dram"] = np.ascontiguousarray(v)
    aps = {name: nc.dram_tensor(name, v.shape, mybir.dt.from_np(v.dtype), kind="ExternalInput").ap()
           for name, v in arrays.items()}
    out = nc.dram_tensor("out_dram", a["x"].shape, F32, kind="ExternalOutput").ap()
    program(nc, aps["in_x_dram"], out, {name[3:-5]: ap for name, ap in aps.items() if name != "in_x_dram"})
    r = _run(nc, [arrays], core_ids=[0])
    return r.results[0]["out_dram"]
```

```python
import numpy as np
from contextlib import ExitStack, contextmanager

import concourse.bass as bass
from concourse import mybir

F32 = mybir.dt.float32
F32R = mybir.dt.float32r
ALU = mybir.AluOpType
ACT = mybir.ActivationFunctionType
AX_X = mybir.AxisListType.X

C = 64
W = 128
HR = W // 2
NPX = HR * W
NA = 6
GN_EPS = 1e-5
BN_EPS = 1e-5


class Chain:

    def __init__(self, eng, sem, base, per):
        self.eng, self.sem, self.base, self.per, self.n = eng, sem, base, per, 0

    def __call__(self, ins):
        self.n += 1
        ins.then_inc(self.sem, 1)
        self.eng.wait_ge(self.sem, self.base + self.n)

    def done(self):
        assert self.n == self.per, self.n


def gate(eng, sem, value, passed):
    eng.wait_ge(sem, value)
    eng.sem_inc(passed, 1)


@contextmanager
def phase(nc):
    held = []

    def named(name):
        held.append(nc.alloc_semaphore(name=name))
        return held[-1]

    yield named
    for s in held:
        nc.gpsimd.sem_clear(s)
        nc.release_semaphore(s)
    nc.all_engine_barrier()


def bc(ap, shape):
    return ap.broadcast_to(shape)


def layer0(nc, B, x, x1, stat1, k):
    PAIRS = NA // 2
    GR = 4
    GPP = 2 * HR // GR
    UN = 8
    POOLS = (3, 7)
    ROWS = (0, 1, 4, 5)
    NB = GPP // UN
    CPER = 81
    NQ = 4
    QR = HR // NQ
    QPX = QR * W
    GQ = 1
    with phase(nc) as named, ExitStack() as ctx:
        def sb(name, shape, dt=F32):
            return ctx.enter_context(nc.sbuf_tensor("a_" + name, shape, dt))

        def sem(name):
            return named("a_" + name)

        X = sb("X", [128, NPX])
        R = sb("R", [128, 128, 128])
        Rf = R[:, :, :].rearrange("p a b -> p (a b)")
        V = Rf[:, 0:NPX]
        Vw = V.rearrange("p (r w) -> p r w", r=HR)
        GN = Rf[:, NPX:2 * NPX]
        XT = sb("XT", [128, 128, 2, C])
        D = sb("D", [128, UN, 2, GR, 128])
        COORD = sb("COORD", [128, 2, PAIRS * 128])
        iota = sb("iota", [128, 128])
        ident = sb("ident", [128, 128])
        anti = sb("anti", [128, 128])
        gsum = sb("gsum", [128, 128])
        lin1 = sb("lin1", [128, 8, 32])
        lin2 = sb("lin2", [32, NA])
        lin1b = sb("lin1b", [32, 1])
        lin2b = sb("lin2b", [128, NA])
        base = sb("base", [128, NA])
        jc = sb("jc", [128, 2])
        ic = sb("ic", [128, HR])
        ftab = sb("ftab", [128, W])
        wf0 = sb("wf0", [C, 3])
        wf1 = sb("wf1", [C, 5])
        fuse = sb("fuse", [C, 2, C])
        bn = sb("bn", [128, 5])
        st = sb("st", [128, 16])
        bnp = sb("bnp", [128, 4])
        ts = sb("ts", [128, NQ + 1])
        stat = sb("stat", [128, NQ + 1])
        PB1 = sb("PB1", [128, HR, 4])
        PB = sb("PB", [128, 8])
        PBn = sb("PBn", [128, 8])
        h1 = sb("h1", [32, 1])
        h1b = sb("h1b", [32, 128])
        ones32 = sb("ones32", [32, 128])
        ang = sb("ang", [128, 8, NA])
        trig = sb("trig", [128, 2, NA])
        jt = sb("jt", [128, 2, NA])
        SIG = sb("SIG", [128, PAIRS * 128])
        Df = D[:, :, :, :, :].rearrange("p u m r w -> p (u m r w)")
        at = [0]

        def behind(width, rows=C, k=NA):
            at[0] += k * width
            return Df[0:rows, at[0] - k * width:at[0]].rearrange("p (k w) -> p k w", k=k)

        CC = behind(W * 2).rearrange("p k (w s) -> p k w s", s=2)
        SP = behind(W + 2)
        CUR = behind(HR + 4)
        F1 = behind(HR)
        F2 = behind(HR // 2 + 2)
        U1 = behind(HR + 2)
        QT = behind(HR + 2)
        Z = behind(HR, 128)
        DZ = behind(HR, 128, NA - 1)
        P = ctx.enter_context(nc.psum_tensor("a_P", [128, 8, 512], F32))

        const_loaded = sem("const_loaded")
        x_loaded = [sem("x_loaded%d" % q) for q in range(NQ)]
        x1_stored = sem("x1_stored")
        init_done = sem("init_done")
        chain_dve = sem("chain_dve")
        chain_act = sem("chain_act")
        sum_ready = sem("sum_ready")
        mean_ready = sem("mean_ready")
        negmean_ready = sem("negmean_ready")
        sq_ready = sem("sq_ready")
        var_ready = sem("var_ready")
        vare_ready = sem("vare_ready")
        std_ready = sem("std_ready")
        gnp_ready = sem("gnp_ready")
        gn_ready = sem("gn_ready")
        pooled_ready = sem("pooled_ready")
        lin1_done = sem("lin1_done")
        h1_ready = sem("h1_ready")
        h1b_ready = sem("h1b_ready")
        lin2_done = sem("lin2_done")
        theta_ready = sem("theta_ready")
        trig_ready = sem("trig_ready")
        coords_ready = sem("coords_ready")
        tr_done = sem("tr_done")
        tr_ev = sem("tr_ev")
        rot_done = sem("rot_done")
        rot_ev = sem("rot_ev")
        diff_ready = sem("diff_ready")
        diff_ready_pool = sem("diff_ready_pool")
        abs_ready = sem("abs_ready")
        tents_ready = sem("tents_ready")
        rows_done = sem("rows_done")
        rows_evicted = sem("rows_evicted")
        sig_ready = sem("sig_ready")
        sig_evicted = sem("sig_evicted")
        coef_ready = sem("coef_ready")
        fuse_done = sem("fuse_done")
        scaled_ready = sem("scaled_ready")
        steps_ready = sem("steps_ready")
        blend_ready = sem("blend_ready")
        gn_low = sem("gn_low")
        block_sums = sem("block_sums")
        ts_ready = sem("ts_ready")
        tsum_ready = sem("tsum_ready")
        tmean_ready = sem("tmean_ready")
        tneg_ready = sem("tneg_ready")
        tsq_ready = sem("tsq_ready")
        stat_stored = sem("stat_stored")
        relu_ready = sem("relu_ready")
        out_ready = sem("out_ready")
        tr_ev0 = sem("tr_ev0")
        rot_ev0 = sem("rot_ev0")
        bn_std = sem("bn_std")
        passed = sem("passed")
        consts = [(iota, "iota"), (ident, "ident"), (anti, "anti"), (gsum, "gsum"), (lin1, "lin1"),
                  (lin2, "lin2"), (lin1b, "lin1b"), (lin2b, "lin2b"), (base, "base"), (jc, "jc"),
                  (ic, "ic"), (ftab, "ftab"), (wf0, "wf0"), (wf1, "wf1"), (fuse, "fuse"), (bn, "bn")]
        CONST = 16 * len(consts)
        block = ctx.enter_context(nc.Block())

        def pair_no(b, p):
            return b * PAIRS + p

        def subtract(tensor_tensor, p, q, u):
            c = COORD[:, :, bass.ds(p * 128 + q * (UN * GR) + u * GR, GR)]
            return tensor_tensor(D[:, u], bc(iota[:, :].unsqueeze(1).unsqueeze(1), [128, 2, GR, 128]),
                                 bc(c.unsqueeze(3), [128, 2, GR, 128]), ALU.subtract)

        @block.sync
        def _(sp):
            for t, name in consts:
                sp.dma_start(t[:], k[name]).then_inc(const_loaded, 16)

            def load(b, q):
                for h in range(2):
                    sp.dma_start(X[64 * h:64 * h + 64, QPX * q:QPX * q + QPX],
                                 x[b, :, HR * h + QR * q:HR * h + QR * q + QR, :].rearrange("c r w -> c (r w)")
                                 ).then_inc(x_loaded[q], 16)

            def store(b, q):
                sp.wait_ge(out_ready, b * NQ + q + 1)
                for h in range(2):
                    sp.dma_start(x1[b, :, HR * h + QR * q:HR * h + QR * q + QR, :].rearrange("c r w -> c (r w)"),
                                 V[64 * h:64 * h + 64, QPX * q:QPX * q + QPX]).then_inc(x1_stored, 16)

            def store_stat(b):
                sp.wait_ge(tsq_ready, b * NQ + NQ)
                sp.dma_start(stat1[b], stat[:, :]).then_inc(stat_stored, 16)

            for q in range(NQ):
                load(0, q)
            with sp.Fori(0, B - 1) as b:
                for q in range(NQ):
                    store(b, q)
                    load(b + 1, q)
                store_stat(b)
            for q in range(NQ):
                store(B - 1, q)
            store_stat(B - 1)
            sp.wait_ge(x1_stored, 32 * NQ * B + 1)
            sp.wait_ge(stat_stored, 16 * B + 1)

        @block.scalar
        def _(act):
            act.wait_ge(init_done, 2)
            nc.scalar.activation(bnp[:, 1:2], bnp[:, 0:1], ACT.Sqrt).then_inc(bn_std, 1)
            act.sem_inc(rows_evicted, 4)
            with act.Fori(0, B) as b:
                ch = Chain(act, chain_act, b * 2, 2)
                act.wait_ge(negmean_ready, b + 1)
                nc.scalar.activation(GN, X[:, :], ACT.Square, bias=st[:, 1:2], accum_out=st[:, 2:3]
                                     ).then_inc(sq_ready, 1)
                act.wait_ge(vare_ready, b + 1)
                nc.scalar.activation(st[:, 4:5], st[:, 3:4], ACT.Sqrt).then_inc(std_ready, 1)
                act.wait_ge(gnp_ready, b + 1)
                nc.scalar.activation(GN[:, 0:GQ * QPX], X[:, 0:GQ * QPX], ACT.Identity, bias=st[:, 6:7], scale=st[:, 5:6]
                                     ).then_inc(gn_ready, 1)
                act.wait_ge(lin1_done, b + 1)
                nc.scalar.activation(h1[:, :], P[0:32, 2, 0:1], ACT.Relu, bias=lin1b[:, 0:1]).then_inc(h1_ready, 1)
                for n in range(1, 16, 2):
                    act.wait_ge(tr_done, b * 16 + n + 1)
                    for h in range(2):
                        ins = nc.scalar.activation(XT[:, HR * h + 4 * n:HR * h + 4 * n + 4, 0, :],
                                                   P[:, 4 + n % 4, :].rearrange("p (r h c) -> p h r c", r=4, h=2)[:, h],
                                                   ACT.Copy)
                    ins.then_inc(tr_ev, 1)
                act.wait_ge(theta_ready, b + 1)
                nc.scalar.activation(trig[:, 0, :], ang[:, 2, :], ACT.Sin).then_inc(chain_act, 1)
                nc.scalar.activation(trig[:, 1, :], ang[:, 3, :], ACT.Sin).then_inc(trig_ready, 1)
                for n in range(1, 16, 2):
                    act.wait_ge(rot_done, b * 16 + n + 1)
                    nc.scalar.activation(XT[:, 127 - 8 * n:(119 - 8 * n) if n < 15 else None:-1, 1, :],
                                         P[:, 4 + n % 4, :].rearrange("p (r c) -> p r c", r=8), ACT.Copy
                                         ).then_inc(rot_ev, 1)

                def absolute(p, q, u):
                    n = (b * PAIRS + p) * NB + q
                    before = sum(w < u for w in POOLS)
                    if u in POOLS:
                        act.wait_ge(diff_ready_pool, n * len(POOLS) + before + 1)
                    else:
                        act.wait_ge(diff_ready, n * (UN - len(POOLS)) + u - before + 1)
                    t = D[:, u].rearrange("p a r w -> p (a r w)")
                    nc.scalar.activation(t, t, ACT.Abs).then_inc(abs_ready, 1)

                def evict(p, q, u):
                    act.wait_ge(rows_done, ((b * PAIRS + p) * NB + q) * UN + u + 1 + UN)
                    nc.scalar.activation(R[:, bass.ds(q * (UN * GR) + u * GR, GR), :],
                                         P[:, ROWS[u % 4], :].rearrange("p (r w) -> p r w", r=GR), ACT.Copy
                                         ).then_inc(rows_evicted, 1)

                def distances(p, q):
                    for u in range(UN):
                        absolute(p, q, u)
                        if u >= 2:
                            evict(p, q, u - 2)
                        else:
                            evict(p, q - 1, UN + u - 2)

                with act.Fori(0, PAIRS) as p:
                    for u in range(UN):
                        absolute(p, 0, u)
                    act.wait_ge(sig_ready, b * PAIRS + p + 1)
                    act.wait_ge(x1_stored, b * (32 * NQ) + 1)
                    for u in range(UN - 2):
                        evict(p, 0, u)
                    with act.Fori(1, NB) as q:
                        distances(p, q)
                    evict(p, NB - 1, UN - 2)
                    evict(p, NB - 1, UN - 1)
                for q in range(NQ):
                    act.wait_ge(blend_ready, b * NQ + q + 1)
                    vq = V[:, QPX * q:QPX * q + QPX]
                    nc.scalar.activation(vq, vq, ACT.Relu, bias=bnp[:, 3:4], scale=bnp[:, 2:3]).then_inc(relu_ready, 1)
                for q in range(NQ):
                    act.wait_ge(out_ready, b * NQ + q + 1)
                    if q:
                        act.wait_ge(ts_ready, b * NQ + q)
                    nc.scalar.activation(P[:, 4:8, :].rearrange("p m w -> p (m w)"), V[:, QPX * q:QPX * q + QPX], ACT.Copy,
                                         accum_out=ts[:, q:q + 1]).then_inc(ts_ready, 1)
                gate(act, tneg_ready, b + 1, passed)
                for q in range(NQ):
                    if q:
                        act.wait_ge(tsq_ready, b * NQ + q)
                    nc.scalar.activation(P[:, 4:8, :].rearrange("p m w -> p (m w)"), V[:, QPX * q:QPX * q + QPX], ACT.Square,
                                         bias=stat[:, 0:1], accum_out=stat[:, 1 + q:2 + q]).then_inc(tsq_ready, 1)

        @block.tensor
        def _(pe):
            pe.sem_inc(rows_done, UN)
            pe.sem_inc(sig_ready, 1)
            pe.wait_ge(const_loaded, CONST)
            with pe.Fori(0, B) as b:
                pe.wait_ge(sum_ready, b + 1)
                nc.tensor.matmul(P[:, 2, 0:1], gsum[:, :], st[:, 0:1], start=True, stop=True).then_inc(mean_ready, 1)
                pe.wait_ge(sq_ready, b + 1)
                pe.wait_ge(negmean_ready, b + 1)
                nc.tensor.matmul(P[:, 2, 0:1], gsum[:, :], st[:, 2:3], start=True, stop=True).then_inc(var_ready, 1)
                pe.wait_ge(pooled_ready, b + 1)
                for n in range(8):
                    mm = nc.tensor.matmul(P[0:32, 2, 0:1], lin1[:, n, :], PBn[:, n:n + 1], start=n == 0, stop=n == 7)
                mm.then_inc(lin1_done, 1)
                pe.wait_ge(h1b_ready, b + 1)
                nc.tensor.matmul(P[:, 2, 0:NA], h1b[:, :], lin2[:, :], start=True, stop=True).then_inc(lin2_done, 1)
                pe.wait_ge(gn_ready, b + 1)
                pe.wait_ge(gn_low, b + 1)
                for n in range(16):
                    if n >= 4:
                        pe.wait_ge(tr_ev if n % 2 else tr_ev0, b * 8 + (n - 4) // 2 + 1)
                    for r in range(4):
                        mm = nc.tensor.transpose(P[:, 4 + n % 4, 128 * r:128 * r + 128],
                                                 GN[:, (4 * n + r) * W:(4 * n + r + 1) * W], ident[:, :])
                    mm.then_inc(tr_done, 1)
                for n in range(16):
                    pe.wait_ge(tr_ev, b * 8 + 8)
                    pe.wait_ge(tr_ev0, b * 8 + 8)
                    if n >= 4:
                        pe.wait_ge(rot_ev if n % 2 else rot_ev0, b * 8 + (n - 4) // 2 + 1)
                    nc.tensor.matmul(P[:, 4 + n % 4, :], anti[:, :], XT[:, 8 * n:8 * n + 8, 0, :],
                                     start=True, stop=True).then_inc(rot_done, 1)
                gate(pe, rot_ev, b * 8 + 8, passed)
                gate(pe, rot_ev0, b * 8 + 8, passed)
                with pe.Fori(0, PAIRS) as p:
                    with pe.Fori(0, NB) as q:
                        for u in range(UN):
                            g = ((b * PAIRS + p) * NB + q) * UN + u
                            pe.wait_ge(tents_ready, g + 1)
                            pe.wait_ge(rows_evicted, g + 1)
                            for r in range(GR):
                                mm = nc.tensor.matmul(P[:, ROWS[u % 4], 128 * r:128 * r + 128], D[:, u, 0, r, :], D[:, u, 1, r, :],
                                                      start=True, stop=True)
                            mm.then_inc(rows_done, 1)
                    pe.wait_ge(rows_evicted, (b * PAIRS + p) * GPP + GPP + 4)
                    pe.wait_ge(sig_evicted, b * PAIRS + p + 1)
                    for y in range(W):
                        mm = nc.tensor.matmul(P[:, 3, 0:128], XT[:, y].rearrange("p v c -> p (v c)"), R[:, :, y],
                                              start=y == 0, stop=y == W - 1)
                    mm.then_inc(sig_ready, 1)
                gate(pe, coef_ready, b + 1, passed)
                for h in range(2):
                    for s in range(2):
                        mm = nc.tensor.matmul(P[64 * h:64 * h + 64, 2, 0:NA * HR], fuse[:, s, :],
                                              CC[:, :, HR * s + HR // 2 * h:HR * s + HR // 2 * (h + 1), :], start=s == 0, stop=s == 1)
                mm.then_inc(fuse_done, 1)
                gate(pe, tsum_ready, b + 1, passed)
                nc.tensor.matmul(P[:, 2, 0:1], gsum[:, :], ts[:, NQ:NQ + 1], start=True, stop=True).then_inc(tmean_ready, 1)

        @block.vector
        def _(dve):
            v = nc.vector
            dve.wait_ge(const_loaded, CONST)
            v.memset(ones32[:, :], 1.0).then_inc(init_done, 1)
            v.tensor_scalar(bnp[:, 0:1], bn[:, 3:4], BN_EPS, None, ALU.add).then_inc(init_done, 1)
            dve.wait_ge(bn_std, 1)
            v.reciprocal(bnp[:, 1:2], bnp[:, 1:2]).then_inc(init_done, 1)
            dve.wait_ge(init_done, 3)
            v.tensor_tensor(bnp[:, 2:3], bnp[:, 1:2], bn[:, 0:1], ALU.mult).then_inc(init_done, 1)
            v.tensor_tensor(bnp[:, 3:4], bn[:, 4:5], bn[:, 2:3], ALU.subtract).then_inc(init_done, 1)
            dve.wait_ge(init_done, 5)
            v.scalar_tensor_tensor(bnp[:, 3:4], bnp[:, 3:4], bnp[:, 2:3], bn[:, 1:2], ALU.mult, ALU.add
                                   ).then_inc(init_done, 1)
            dve.wait_ge(init_done, 6)
            dve.sem_inc(x1_stored, 1)
            dve.sem_inc(stat_stored, 1)
            dve.sem_inc(sig_evicted, 1)
            with dve.Fori(0, B) as b:
                ch = Chain(dve, chain_dve, b * CPER, CPER)
                for q in range(NQ):
                    dve.wait_ge(x_loaded[q], b * 32 + 32)
                    v.tensor_reduce(PB1[:, QR * q:QR * q + QR, :],
                                    X[:, QPX * q:QPX * q + QPX].rearrange("p (r q w) -> p r q w", r=QR, q=4), AX_X, ALU.add
                                    ).then_inc(block_sums, 1)
                dve.wait_ge(block_sums, b * NQ + NQ)
                ch(v.tensor_reduce(PB[:, :].rearrange("p (a q) -> p a q", a=2),
                                   PB1[:, :, :].rearrange("p (a r) q -> p a q r", a=2), AX_X, ALU.add))
                v.tensor_reduce(st[:, 0:1], PB[:, :], AX_X, ALU.add).then_inc(sum_ready, 1)
                dve.wait_ge(mean_ready, b + 1)
                v.tensor_scalar(st[:, 1:2], P[:, 2, 0:1], -1.0, None, ALU.mult).then_inc(negmean_ready, 1)
                dve.wait_ge(var_ready, b + 1)
                v.tensor_scalar(st[:, 3:4], P[:, 2, 0:1], GN_EPS, None, ALU.add).then_inc(vare_ready, 1)
                dve.wait_ge(std_ready, b + 1)
                ch(v.reciprocal(st[:, 5:6], st[:, 4:5]))
                v.tensor_scalar(st[:, 6:7], st[:, 1:2], st[:, 5:6], None, ALU.mult).then_inc(gnp_ready, 1)
                dve.wait_ge(gnp_ready, b + 1)
                ch(v.tensor_scalar(PBn[:, :], PB[:, :], 1.0 / 1024, None, ALU.mult))
                v.tensor_scalar(PBn[:, :], PBn[:, :], st[:, 5:6], st[:, 6:7], ALU.mult, ALU.add
                                ).then_inc(pooled_ready, 1)
                v.tensor_scalar(GN[:, GQ * QPX:NPX], X[:, GQ * QPX:NPX], st[:, 5:6], st[:, 6:7], ALU.mult, ALU.add).then_inc(gn_low, 1)
                dve.wait_ge(h1_ready, b + 1)
                v.tensor_scalar(h1b[:, :], ones32[:, :], h1[:, 0:1], None, ALU.mult).then_inc(h1b_ready, 1)
                dve.wait_ge(lin2_done, b + 1)
                ch(v.tensor_tensor(ang[:, 0, :], P[:, 2, 0:NA], lin2b[:, :], ALU.add))
                ch(v.scalar_tensor_tensor(ang[:, 0, :], ang[:, 0, :], 30.0, base[:, :], ALU.mult, ALU.add))
                ch(v.tensor_scalar(ang[:, 0, :], ang[:, 0, :], 0.0, 180.0, ALU.max, ALU.min))
                a, o = 0, 1
                for n in range(NA):
                    if n % 2 == 0:
                        lo, hi = slice(0, NA, 2), slice(1, NA, 2)
                    else:
                        lo, hi = slice(1, NA - 1, 2), slice(2, NA - 1, 2)
                        ch(v.tensor_copy(ang[:, o, 0:NA:NA - 1], ang[:, a, 0:NA:NA - 1]))
                    ch(v.tensor_tensor(ang[:, o, lo], ang[:, a, lo], ang[:, a, hi], ALU.min))
                    ch(v.tensor_tensor(ang[:, o, hi], ang[:, a, lo], ang[:, a, hi], ALU.max))
                    a, o = o, a
                ch(v.tensor_scalar(ang[:, 2, :], ang[:, a, :], float(np.float32(np.pi / 180)), None, ALU.mult))
                v.tensor_scalar(ang[:, 3, :], ang[:, 2, :], -1.0, float(np.pi / 2), ALU.mult, ALU.add
                                ).then_inc(theta_ready, 1)
                for n in range(0, 16, 2):
                    dve.wait_ge(tr_done, b * 16 + n + 1)
                    for h in range(2):
                        ins = v.tensor_copy(XT[:, HR * h + 4 * n:HR * h + 4 * n + 4, 0, :],
                                            P[:, 4 + n % 4, :].rearrange("p (r h c) -> p h r c", r=4, h=2)[:, h])
                    ins.then_inc(tr_ev0, 1)
                for n in range(0, 16, 2):
                    dve.wait_ge(rot_done, b * 16 + n + 1)
                    v.tensor_copy(XT[:, 127 - 8 * n:119 - 8 * n:-1, 1, :],
                                  P[:, 4 + n % 4, :].rearrange("p (r c) -> p r c", r=8)).then_inc(rot_ev0, 1)
                dve.wait_ge(trig_ready, b + 1)
                dve.wait_ge(chain_act, b + 1)
                ch(v.tensor_scalar(jt[:, 0, :], trig[:, 1, :], jc[:, 0:1], 63.5, ALU.mult, ALU.add))
                ch(v.tensor_scalar(jt[:, 1, :], trig[:, 0, :], jc[:, 1:2], 63.5, ALU.mult, ALU.add))
                icb = bc(ic[:, :].unsqueeze(1), [128, NA, HR])
                for m in range(2):
                    cm = COORD[:, m, :].rearrange("p (k i) -> p k i", k=NA)
                    ch(v.tensor_tensor(cm, icb, bc(trig[:, m, :].unsqueeze(2), [128, NA, HR]), ALU.mult))
                    ch(v.tensor_tensor(cm, cm, bc(jt[:, m, :].unsqueeze(2), [128, NA, HR]), ALU.add))

                dve.sem_inc(coords_ready, 1)

                def diff(p, q, u):
                    dve.wait_ge(rows_done, ((b * PAIRS + p) * NB + q) * UN + u + 1)
                    subtract(v.tensor_tensor, p, q, u).then_inc(diff_ready, 1)

                def tent(p, q, u):
                    dve.wait_ge(abs_ready, ((b * PAIRS + p) * NB + q) * UN + u + 1)
                    t = D[:, u].rearrange("p a r w -> p (a r w)")
                    v.tensor_scalar(t, t, 1.0, 1.0, ALU.min, ALU.subtract).then_inc(tents_ready, 1)

                def tents(p, q, first=False):
                    for u in range(UN):
                        if u >= 2:
                            tent(p, q, u - 2)
                        elif not first:
                            tent(p, q - 1, UN + u - 2)
                        if u not in POOLS:
                            diff(p, q, u)

                def sums(p):
                    dve.wait_ge(sig_ready, b * PAIRS + p + 2)
                    v.tensor_copy(SIG[:, p * 128:p * 128 + 128], P[:, 3, 0:128]).then_inc(sig_evicted, 1)

                for p in range(PAIRS):
                    tents(p, 0, first=True)
                    if p:
                        sums(p - 1)
                    with dve.Fori(1, NB) as q:
                        tents(p, q)
                    tent(p, NB - 1, UN - 2)
                    tent(p, NB - 1, UN - 1)
                def wavelets(p0, p1):
                    ks = slice(2 * p0, 2 * p1)
                    sig = SIG[:, :].rearrange("p (k i) -> p k i", k=NA)[:, ks]
                    sp, cur, f1, f2, u1, qt, cc = (t[:, ks] for t in (SP, CUR, F1, F2, U1, QT, CC))
                    ch(v.memset(sp[:, :, 0:W + 2:W + 1], 0.0))
                    ch(v.memset(cur, 0.0))
                    ch(v.tensor_copy(sp[:, :, 1:1 + HR], sig[0:64]))
                    ch(v.tensor_copy(sp[:, :, W:HR:-1], sig[64:128]))
                    ch(v.tensor_scalar(cc[:, :, :, 0], sp[:, :, 0:W], wf0[:, 0:1], None, ALU.mult))
                    for t in (1, 2):
                        ch(v.scalar_tensor_tensor(cc[:, :, :, 0], sp[:, :, t:t + W], wf0[:, t:t + 1], cc[:, :, :, 0], ALU.mult, ALU.add))
                    mid = cur[:, :, 2:2 + HR]
                    ch(v.tensor_tensor(mid, sp[:, :, 1:W:2], sp[:, :, 2:W + 1:2], ALU.add))
                    ch(v.tensor_scalar(mid, mid, 0.5, None, ALU.mult))
                    ch(v.tensor_scalar(f1, cur[:, :, 0:HR], wf1[:, 0:1], None, ALU.mult))
                    for t in range(1, 5):
                        ch(v.scalar_tensor_tensor(f1, cur[:, :, t:t + HR], wf1[:, t:t + 1], f1, ALU.mult, ALU.add))
                    L = HR // 2
                    ch(v.tensor_tensor(f2[:, :, 1:1 + L], f1[:, :, 0:HR:2], f1[:, :, 1:HR:2], ALU.add))
                    ch(v.tensor_scalar(f2[:, :, 1:1 + L], f2[:, :, 1:1 + L], 0.5, None, ALU.mult))
                    for src, dst, n in ((f2, u1[:, :, 1:1 + HR], L), (u1, cc[:, :, :, 1], HR)):
                        ch(v.tensor_copy(src[:, :, 0:1], src[:, :, 1:2]))
                        ch(v.tensor_copy(src[:, :, n + 1:n + 2], src[:, :, n:n + 1]))
                        ch(v.tensor_scalar(qt[:, :, 0:n + 2], src[:, :, 0:n + 2], 0.25, None, ALU.mult))
                        ch(v.scalar_tensor_tensor(dst[:, :, 0:2 * n:2], src[:, :, 1:n + 1], 0.75, qt[:, :, 0:n], ALU.mult, ALU.add))
                        ch(v.scalar_tensor_tensor(dst[:, :, 1:2 * n:2], src[:, :, 1:n + 1], 0.75, qt[:, :, 2:n + 2], ALU.mult, ALU.add))

                dve.wait_ge(rows_done, (b * PAIRS + PAIRS) * GPP + UN)
                dve.wait_ge(sig_evicted, b * PAIRS + PAIRS)
                wavelets(0, PAIRS - 1)
                sums(PAIRS - 1)
                dve.wait_ge(sig_evicted, b * PAIRS + PAIRS + 1)
                wavelets(PAIRS - 1, PAIRS)
                dve.sem_inc(coef_ready, 1)
                dve.wait_ge(fuse_done, b + 1)
                ch(v.tensor_copy(Z[:, :, :], P[:, 2, 0:NA * HR].rearrange("p (k i) -> p k i", k=NA)))
                v.tensor_tensor(DZ[:, :, :], Z[:, 1:NA, :], Z[:, 0:NA - 1, :], ALU.subtract).then_inc(steps_ready, 1)

                def blend(q):
                    dve.wait_ge(scaled_ready, b * NQ + q + 1)
                    for m, (w0, w1) in enumerate(segments()):
                        r0 = QR * q
                        ins = v.tensor_tensor(Vw[:, r0:r0 + QR, w0:w1], Vw[:, r0:r0 + QR, w0:w1],
                                              bc(Z[:, m, r0:r0 + QR].unsqueeze(2), [128, QR, w1 - w0]), ALU.add)
                    ins.then_inc(blend_ready, 1)

                def add_x(q):
                    dve.wait_ge(relu_ready, b * NQ + q + 1)
                    vq = V[:, QPX * q:QPX * q + QPX]
                    v.tensor_tensor(vq, vq, X[:, QPX * q:QPX * q + QPX], ALU.add).then_inc(out_ready, 1)

                blend(0)
                for q in range(1, NQ):
                    blend(q)
                    add_x(q - 1)
                add_x(NQ - 1)
                dve.wait_ge(ts_ready, b * NQ + NQ)
                v.tensor_reduce(ts[:, NQ:NQ + 1], ts[:, 0:NQ], AX_X, ALU.add).then_inc(tsum_ready, 1)
                dve.wait_ge(tmean_ready, b + 1)
                dve.wait_ge(stat_stored, b * 16 + 1)
                v.tensor_scalar(stat[:, 0:1], P[:, 2, 0:1], -1.0, None, ALU.mult).then_inc(tneg_ready, 1)
                ch.done()

        @block.gpsimd
        def _(pool):
            with pool.Fori(0, B) as b:
                gate(pool, coords_ready, b + 1, passed)
                with pool.Fori(0, PAIRS) as p:
                    with pool.Fori(0, NB) as q:
                        for u in POOLS:
                            gate(pool, rows_done, ((b * PAIRS + p) * NB + q) * UN + u + 1, passed)
                            subtract(nc.gpsimd.tensor_tensor, p, q, u).then_inc(diff_ready_pool, 1)
                gate(pool, steps_ready, b + 1, passed)
                for q in range(NQ):
                    r0 = QR * q
                    for m, (w0, w1) in enumerate(segments()):
                        ins = nc.gpsimd.tensor_tensor(Vw[:, r0:r0 + QR, w0:w1],
                                                      bc(DZ[:, m, r0:r0 + QR].unsqueeze(2), [128, QR, w1 - w0]),
                                                      bc(ftab[:, w0:w1].unsqueeze(1), [128, QR, w1 - w0]), ALU.mult)
                    ins.then_inc(scaled_ready, 1)


def segments():
    pos = np.arange(W, dtype=np.float32) * np.float32((NA - 1) / (W - 1))
    i0 = np.minimum(np.floor(pos).astype(int), NA - 2)
    return [(int(np.argmax(i0 == m)), int(W - np.argmax(i0[::-1] == m))) for m in range(NA - 1)]



TAPS = 9
TR = 4
NT = HR // TR
PR, PW = HR + 2, W + 2


class TapGroups:

    def __init__(self, sizes):
        assert sum(sizes) == TAPS
        self.n = len(sizes)
        self.adds = TAPS - self.n
        self.firsts = [sum(sizes[:g]) for g in range(self.n)]

    def group(self, t):
        return max(g for g in range(self.n) if self.firsts[g] <= t)

    def first(self, t):
        return self.firsts[self.group(t)]

    def is_last(self, t):
        return t == TAPS - 1 or t + 1 in self.firsts

    def adds_to(self, t):
        return t - self.group(t)


def layer1(nc, B, x1, stat1, x2, pool2, norm2, k):
    CPER = 2
    NS = 5
    SQ = 8
    QT = 4
    NQ = NT // QT
    QR = QT * TR
    CONV0 = [NT - 2, NT - 1] + list(range(NT - 2))
    DEPTH = [NT - 1] + list(range(NT - 1))
    LATE = 5
    BEHIND = 4
    ADDS = TAPS - 1
    DEPTH0 = NT * ADDS
    with phase(nc) as named, ExitStack() as ctx:
        def sb(name, shape, dt=F32):
            return ctx.enter_context(nc.sbuf_tensor("b_" + name, shape, dt))

        def sem(name):
            return named("b_" + name)

        X = sb("X", [128, HR, W])
        G = sb("G", [128, PR, PW], F32R)
        GL = sb("GL", [128, PR, PW], F32R)
        Y = sb("Y", [128, PR, PW])
        T = sb("T", [128, HR, W])
        W0P = sb("W0P", [128, 2, TAPS, 128], F32R)
        WFP = sb("WFP", [128, 2, TAPS, 128], F32R)
        W3 = sb("W3", [128, TAPS, 128])
        W0, WF = (T[:, TAPS * n:TAPS * n + TAPS, :] for n in range(2))
        gsum = sb("gsum", [128, 128])
        shift = sb("shift", [128, 3, 128])
        w1 = sb("w1", [128, TAPS])
        b3 = sb("b3", [128, TAPS])
        b3m = sb("b3m", [128, TAPS])
        w2 = sb("w2", [128, 3])
        bias = sb("bias", [128, 4])
        st = sb("st", [128, 2, 16])
        BS1 = sb("BS1", [128, 2, TR, W // 4])
        BS = sb("BS", [128, NT, W // 4])
        stat = sb("stat", [128, 5])
        ms = sb("ms", [128, NT])
        sqt = sb("sqt", [128, SQ])
        m3 = sb("m3", [128, 4])
        PROD = sb("PROD", [128, NS, TR, W])
        ACC = sb("ACC", [128, 2, TR, W])
        P = ctx.enter_context(nc.psum_tensor("b_P", [128, 8, 512], F32))
        const_loaded = sem("const_loaded")
        cleared = sem("cleared")
        weights_loaded = sem("weights_loaded")
        x_loaded = [sem("x_loaded%d" % q) for q in range(NQ)]
        x2_stored = sem("x2_stored")
        out_ready = sem("out_ready")
        passed = sem("passed")
        chain_dve = sem("chain_dve")
        chain_pads = sem("chain_pads")
        stat_loaded = sem("stat_loaded")
        sum_ready = sem("sum_ready")
        mean_ready = sem("mean_ready")
        negmean_ready = sem("negmean_ready")
        sq_ready = [sem("sq_ready" + s) for s in "xt"]
        var_ready = [sem("var_ready" + s) for s in "xt"]
        vare_ready = [sem("vare_ready" + s) for s in "xt"]
        std_ready = [sem("std_ready" + s) for s in "xt"]
        inv_ready = [sem("inv_ready" + s) for s in "xt"]
        gnp_ready = [sem("gnp_ready" + s) for s in "xt"]
        columns_ready = sem("columns_ready")
        blocks_ready = sem("blocks_ready")
        next_stored = sem("next_stored")
        residual_ready = sem("residual_ready")
        gn_ready = sem("gn_ready")
        exact_ready = sem("exact_ready")
        low_ready = sem("low_ready")
        low_ready_pool = sem("low_ready_pool")
        split_done = sem("split_done")
        leaked = sem("leaked")
        high_ready = sem("high_ready")
        gn_halo = sem("gn_halo")
        conv0_done = sem("conv0_done")
        conv0_ev = sem("conv0_ev")
        y_halo = sem("y_halo")
        ysum_ready = sem("ysum_ready")
        m3_done = sem("m3_done")
        dbias_ready = sem("dbias_ready")
        b3_done = sem("b3_done")
        b3_ready = sem("b3_ready")
        tap0_ready = sem("tap0_ready")
        depth_step = sem("depth_step")
        fil_done = sem("fil_done")
        prod_ready = sem("prod_ready")
        added = sem("added")
        filtered = sem("filtered")
        f_halo = sem("f_halo")
        convf_done = sem("convf_done")
        mix_ready = sem("mix_ready")
        consts = [(gsum, "gsum"), (shift, "shift"), (w1, "w1"), (b3, "b3"), (w2, "w2"), (bias, "bias1")]
        XX, TT = 0, 1
        block = ctx.enter_context(nc.Block())
        t9 = [(t // 3, t % 3) for t in range(TAPS)]
        PARTS = ((0, 0), (1, 0), (0, 1))
        POOLQ = 2

        def tile(t, n, dy=0, dx=0):
            return t[:, TR * n + dy:TR * n + dy + TR, dx:dx + W]

        def low(tensor_tensor, q):
            rows = slice(1 + QR * q, 1 + QR * q + QR)
            return tensor_tensor(GL[:, rows, 1:1 + W], Y[:, rows, 1:1 + W], G[:, rows, 1:1 + W], ALU.subtract)

        def bank(m):
            return P[:, m, :].rearrange("p (r w) -> p r w", r=TR)

        @block.sync
        def _(sp):
            for t, name in consts:
                sp.dma_start(t[:], k[name]).then_inc(const_loaded, 16)
            sp.wait_ge(cleared, 3)
            for t, name in ((W0, "w0"), (W3, "w3"), (WF, "wf")):
                for h in range(2):
                    sp.dma_start(t[64 * h:64 * h + 64, :, 64 * h:64 * h + 64], k[name]).then_inc(weights_loaded, 16)

            def load(b, q):
                for h in range(2):
                    sp.dma_start(X[64 * h:64 * h + 64, QR * q:QR * q + QR], x1[b, :, HR * h + QR * q:HR * h + QR * q + QR, :]
                                 ).then_inc(x_loaded[q], 16)

            def store(b, q):
                sp.wait_ge(out_ready, b * NT + QT * q + QT)
                for h in range(2):
                    sp.dma_start(x2[b, :, HR * h + QR * q:HR * h + QR * q + QR, :], T[64 * h:64 * h + 64, QR * q:QR * q + QR]
                                 ).then_inc(x2_stored, 16)

            def store_next(b):
                sp.wait_ge(gnp_ready[TT], b + 1)
                sp.dma_start(pool2[b], BS[:, :, :]).then_inc(next_stored, 16)
                sp.dma_start(norm2[b], st[:, TT, 5:7]).then_inc(next_stored, 16)

            def load_stat(b):
                sp.dma_start(stat[:, :], stat1[b]).then_inc(stat_loaded, 16)

            load_stat(0)
            for q in range(NQ):
                load(0, q)
            with sp.Fori(0, B - 1) as b:
                sp.wait_ge(gnp_ready[XX], b + 1)
                load_stat(b + 1)
                for q in range(NQ):
                    store(b, q)
                    load(b + 1, q)
                store_next(b)
            for q in range(NQ):
                store(B - 1, q)
            store_next(B - 1)
            sp.wait_ge(x2_stored, 32 * NQ * B + 1)
            sp.wait_ge(next_stored, 32 * B + 1)

        def inner(t):
            return t[:, 1:1 + HR, 1:1 + W]

        def halo(copy, t):
            copy(t[0:64, PR - 1, :], t[64:128, 1, :])
            return copy(t[64:128, 0, :], t[0:64, HR, :])

        @block.scalar
        def _(act):
            act.sem_inc(conv0_ev, 4)

            def deviation(z, b):
                act.wait_ge(vare_ready[z], b + 1)
                nc.scalar.activation(st[:, z, 4:5], st[:, z, 3:4], ACT.Sqrt).then_inc(std_ready[z], 1)

            def square(b):
                gate(act, negmean_ready, b + 1, passed)
                n = HR // SQ
                for m in range(SQ):
                    if m:
                        act.wait_ge(sq_ready[TT], b * SQ + m)
                    nc.scalar.activation(P[:, 4:6, :].rearrange("p m w -> p (m w)"), T[:, n * m:n * m + n, :].rearrange("p r w -> p (r w)"),
                                         ACT.Square, bias=st[:, TT, 1:2], accum_out=sqt[:, m:m + 1]).then_inc(sq_ready[TT], 1)

            def exact(b):
                gate(act, gnp_ready[XX], b + 1, passed)
                for q in range(NQ):
                    gate(act, x_loaded[q], b * 32 + 32, passed)
                    nc.scalar.activation(Y[:, 1 + QR * q:1 + QR * q + QR, 1:1 + W], X[:, QR * q:QR * q + QR, :], ACT.Identity,
                                         bias=st[:, XX, 6:7], scale=st[:, XX, 5:6]).then_inc(exact_ready, 1)

            def main(b):
                def tap0(j):
                    nc.scalar.activation(tile(T, DEPTH[j]), tile(Y, DEPTH[j]), ACT.Copy, scale=w1[:, 0:1]).then_inc(tap0_ready, 1)

                for m, n in enumerate(CONV0):
                    act.wait_ge(conv0_done, b * NT + m + 1)
                    nc.scalar.activation(Y[:, 1 + TR * n:1 + TR * n + TR, 1:1 + W], bank(m % 4),
                                         ACT.Identity, bias=bias[:, 0:1], accum_out=ms[:, n:n + 1]).then_inc(conv0_ev, 1)
                    if m == 3:
                        gate(act, y_halo, b + 1, passed)
                        gate(act, x2_stored, b * (32 * NQ) + 1, passed)
                        tap0(0)
                    if m >= 3:
                        act.wait_ge(conv0_ev, b * NT + m + 5)
                        tap0(m - 2)
                tap0(NT - 2)
                tap0(NT - 1)

                def high(m):
                    act.wait_ge(leaked, b * NT + m + 1)
                    n = DEPTH[m]
                    nc.scalar.activation(G[:, 1 + TR * n:1 + TR * n + TR, 1:1 + W], ACC[:, m % 2], ACT.Copy).then_inc(high_ready, 1)

                def output(n):
                    act.wait_ge(mix_ready, b * NT + n + 3)
                    nc.scalar.activation(tile(T, n), tile(T, n), ACT.Identity, bias=st[:, XX, 8:9]).then_inc(out_ready, 1)

                for m in range(NT):
                    high(m)
                    if m >= BEHIND:
                        output(m - BEHIND)
                for n in range(NT - BEHIND, NT):
                    output(n)

            deviation(XX, 0)
            exact(0)
            with act.Fori(0, B - 1) as b:
                main(b)
                deviation(XX, b + 1)
                exact(b + 1)
                square(b)
                deviation(TT, b)
            main(B - 1)
            square(B - 1)
            deviation(TT, B - 1)

        @block.tensor
        def _(pe):
            pe.wait_ge(const_loaded, 16 * len(consts))
            pe.wait_ge(weights_loaded, 96)
            pe.wait_ge(split_done, 4)

            def mean(b):
                gate(pe, sum_ready, b + 1, passed)
                nc.tensor.matmul(P[:, 7, 0:1], gsum[:, :], st[:, TT, 0:1], start=True, stop=True).then_inc(mean_ready, 1)

            def variance(z, b):
                gate(pe, sq_ready[z], b + 1 if z == XX else b * SQ + SQ, passed)
                pieces = [st[:, XX, 2:3]] if z == XX else [sqt[:, m:m + 1] for m in range(SQ)]
                for m, piece in enumerate(pieces):
                    mm = nc.tensor.matmul(P[:, 7, 2 + z:3 + z], gsum[:, :], piece, start=m == 0, stop=m == len(pieces) - 1)
                mm.then_inc(var_ready[z], 1)

            def main(b, before=None):
                gate(pe, gn_halo, b + 1, passed)
                for m, n in enumerate(CONV0):
                    pe.wait_ge(conv0_ev, b * NT + m + 1)
                    for t, (dy, dx) in enumerate(t9):
                        for i, (w, g) in enumerate(PARTS):
                            mm = nc.tensor.matmul(P[:, m % 4, :], W0P[:, w, t, :], tile((G, GL)[g], n, dy, dx),
                                                  start=t == i == 0, stop=t == TAPS - 1 and i == 2)
                    mm.then_inc(conv0_done, 1)
                    if m == 1 and before is not None:
                        variance(TT, before)
                gate(pe, ysum_ready, b + 1, passed)
                for m in range(3):
                    mm = nc.tensor.matmul(P[:, 7, m:m + 1], shift[:, m, :], st[:, XX, 7:8], start=True, stop=True)
                mm.then_inc(m3_done, 1)
                gate(pe, dbias_ready, b + 1, passed)
                for t in range(TAPS):
                    mm = nc.tensor.matmul(P[:, 7, t:t + 1], W3[:, t, :], m3[:, 3:4], start=True, stop=True)
                mm.then_inc(b3_done, 1)
                gate(pe, conv0_ev, b * NT + NT + 4, passed)

                def last_conv(c, t):
                    if t == 0:
                        pe.wait_ge(mix_ready, b * NT + c + 1)
                        gate(pe, filtered, b * NT + min(c + 3, NT) + 2, passed)
                        if c == 0:
                            gate(pe, f_halo, b + 1, passed)
                    for i, (w, g) in enumerate(PARTS):
                        mm = nc.tensor.matmul(P[:, 4 + c % 2, :], WFP[:, w, t, :], tile((G, GL)[g], c, *t9[t]),
                                              start=t == i == 0, stop=t == TAPS - 1 and i == 2)
                    if t == TAPS - 1:
                        mm.then_inc(convf_done, 1)

                for m, n in enumerate(DEPTH):
                    gate(pe, depth_step, b * (NT * ADDS) + DEPTH0 + (m + 1) * ADDS, passed)
                    for t in range(TAPS):
                        s = m * TAPS + t
                        if s >= 4:
                            pe.wait_ge(prod_ready, b * (NT * TAPS) + s - 3)
                        nc.tensor.matmul(P[:, s % 4, :], W3[:, t, :], tile(T, n), start=True, stop=True).then_inc(fil_done, 1)
                        if m >= BEHIND:
                            last_conv(m - BEHIND, t)
                for c in range(NT - BEHIND, NT):
                    for t in range(TAPS):
                        last_conv(c, t)

            variance(XX, 0)
            main(0)
            with pe.Fori(1, B) as b:
                variance(XX, b)
                mean(b - 1)
                main(b, b - 1)
            mean(B - 1)
            variance(TT, B - 1)

        @block.gpsimd
        def _(pool):
            pool.sem_inc(filtered, 2)
            with pool.Fori(0, B) as b:
                for q in range(POOLQ):
                    gate(pool, gn_ready, b * NQ + q + 1, passed)
                    gate(pool, exact_ready, b * NQ + q + 1, passed)
                    low(nc.gpsimd.tensor_tensor, q).then_inc(low_ready_pool, 1)
                for m in range(NT):
                    for t in range(1, TAPS):
                        gate(pool, prod_ready, b * (NT * TAPS) + m * TAPS + t + 1, passed)
                        if t == 1:
                            gate(pool, filtered, b * NT + m + 1, passed)
                        else:
                            gate(pool, added, b * (NT * ADDS) + m * ADDS + t - 1, passed)
                        first = PROD[:, (m * TAPS) % NS] if t == 1 else ACC[:, m % 2]
                        nc.gpsimd.tensor_tensor(ACC[:, m % 2], first, PROD[:, (m * TAPS + t) % NS], ALU.add).then_inc(added, 1)

        @block.vector
        def _(dve):
            v = nc.vector
            for n, t in enumerate((W0, W3, WF)):
                v.memset(t[:, :, :], 0.0).then_inc(cleared, 1)
            for t in (G, GL, Y):
                v.memset(t[:, 0:PR:PR - 1, :].bitcast(F32), 0.0).then_inc(chain_pads, 1)
                v.memset(t[:, 1:1 + HR, 0:PW:PW - 1].bitcast(F32), 0.0).then_inc(chain_pads, 1)
            dve.wait_ge(chain_pads, 6)
            dve.wait_ge(weights_loaded, 96)
            for n, (t, parts) in enumerate(((W0, W0P), (WF, WFP))):
                v.tensor_copy(parts[:, 0], t[:, :, :]).then_inc(split_done, 1)
                dve.wait_ge(split_done, 2 * n + 1)
                v.tensor_tensor(parts[:, 1], t[:, :, :], parts[:, 0], ALU.subtract).then_inc(split_done, 1)
            dve.wait_ge(const_loaded, 16 * len(consts))
            dve.sem_inc(x2_stored, 1)
            dve.sem_inc(mix_ready, 2)
            dve.sem_inc(depth_step, DEPTH0)
            dve.sem_inc(next_stored, 1)

            def negmean(b):
                dve.wait_ge(mean_ready, b + 1)
                v.tensor_scalar(st[:, TT, 1:2], P[:, 7, 0:1], -1.0, None, ALU.mult).then_inc(negmean_ready, 1)

            def scale_shift(z, b):
                if z == TT:
                    dve.wait_ge(next_stored, b * 32 + 1)
                dve.wait_ge(var_ready[z], b + 1)
                v.tensor_scalar(st[:, z, 3:4], P[:, 7, 2 + z:3 + z], GN_EPS, None, ALU.add).then_inc(vare_ready[z], 1)
                dve.wait_ge(std_ready[z], b + 1)
                v.reciprocal(st[:, z, 5:6], st[:, z, 4:5]).then_inc(inv_ready[z], 1)
                dve.wait_ge(inv_ready[z], b + 1)
                negative = stat[:, 0:1] if z == XX else st[:, TT, 1:2]
                v.tensor_scalar(st[:, z, 6:7], negative, st[:, z, 5:6], None, ALU.mult).then_inc(gnp_ready[z], 1)

            def squares_x(b):
                dve.wait_ge(stat_loaded, b * 16 + 16)
                v.tensor_reduce(st[:, XX, 2:3], stat[:, 1:5], AX_X, ALU.add).then_inc(sq_ready[XX], 1)

            def sum_t(b):
                dve.wait_ge(blocks_ready, b * NT + NT)
                v.tensor_reduce(st[:, TT, 0:1], BS[:, :, :].rearrange("p n q -> p (n q)"), AX_X, ALU.add).then_inc(sum_ready, 1)

            def normalise(b):
                dve.wait_ge(gnp_ready[XX], b + 1)
                for q in range(NQ):
                    dve.wait_ge(x_loaded[q], b * 32 + 32)
                    v.tensor_scalar(G[:, 1 + QR * q:1 + QR * q + QR, 1:1 + W], X[:, QR * q:QR * q + QR, :], st[:, XX, 5:6],
                                    st[:, XX, 6:7], ALU.mult, ALU.add).then_inc(gn_ready, 1)
                    if q >= POOLQ:
                        dve.wait_ge(gn_ready, b * NQ + q + 1)
                        dve.wait_ge(exact_ready, b * NQ + q + 1)
                        low(v.tensor_tensor, q).then_inc(low_ready, 1)
                v.tensor_tensor(st[:, XX, 8:9], st[:, XX, 6:7], bias[:, 3:4], ALU.add).then_inc(residual_ready, 1)
                v.tensor_scalar(st[:, XX, 9:10], st[:, XX, 5:6], 1.0, None, ALU.add).then_inc(residual_ready, 1)
                dve.wait_ge(low_ready, b * (NQ - POOLQ) + NQ - POOLQ)
                dve.wait_ge(low_ready_pool, b * POOLQ + POOLQ)
                halo(v.tensor_copy, G)
                halo(v.tensor_copy, GL).then_inc(gn_halo, 1)

            def main(b):
                ch = Chain(dve, chain_dve, b * CPER, CPER)
                dve.wait_ge(residual_ready, b * 2 + 2)
                gate(dve, conv0_ev, b * NT + 3 + 4, passed)
                halo(v.tensor_copy, Y).then_inc(y_halo, 1)

                def depth(j, t):
                    if t == 1:
                        dve.wait_ge(tap0_ready, b * NT + j + 1)
                    else:
                        dve.wait_ge(depth_step, b * (NT * ADDS) + DEPTH0 + j * ADDS + t - 1)
                    n = DEPTH[j]
                    v.scalar_tensor_tensor(tile(T, n), tile(Y, n, *t9[t]), w1[:, t:t + 1], tile(T, n), ALU.mult, ALU.add
                                           ).then_inc(depth_step, 1)

                for j in range(NT - LATE):
                    for t in range(1, TAPS):
                        depth(j, t)
                gate(dve, conv0_ev, b * NT + NT + 4, passed)
                v.tensor_reduce(st[:, XX, 7:8], ms[:, :], AX_X, ALU.add).then_inc(ysum_ready, 1)
                dve.wait_ge(m3_done, b + 1)
                ch(v.tensor_tensor(m3[:, 0:3], P[:, 7, 0:3], w2[:, :], ALU.mult))
                ch(v.tensor_reduce(m3[:, 3:4], m3[:, 0:3], AX_X, ALU.add))
                v.tensor_scalar(m3[:, 3:4], m3[:, 3:4], bias[:, 1:2], bias[:, 2:3], ALU.add, ALU.add).then_inc(dbias_ready, 1)
                dve.wait_ge(b3_done, b + 1)
                v.tensor_tensor(b3m[:, :], P[:, 7, 0:TAPS], b3[:, :], ALU.add).then_inc(b3_ready, 1)
                dve.wait_ge(b3_ready, b + 1)

                def leaky(m):
                    dve.wait_ge(added, b * (NT * ADDS) + m * ADDS + ADDS)
                    v.scalar_tensor_tensor(ACC[:, m % 2], ACC[:, m % 2], 0.2, ACC[:, m % 2], ALU.mult, ALU.max).then_inc(leaked, 1)

                def filtered_low(m):
                    dve.wait_ge(leaked, b * NT + m + 1)
                    dve.wait_ge(high_ready, b * NT + m + 1)
                    n = DEPTH[m]
                    rows = slice(1 + TR * n, 1 + TR * n + TR)
                    v.tensor_tensor(GL[:, rows, 1:1 + W], ACC[:, m % 2], G[:, rows, 1:1 + W], ALU.subtract).then_inc(filtered, 1)
                    if m == 1:
                        gate(dve, filtered, b * NT + 2 + 2, passed)
                        halo(v.tensor_copy, G)
                        halo(v.tensor_copy, GL).then_inc(f_halo, 1)

                def mix(c):
                    dve.wait_ge(convf_done, b * NT + c + 1)
                    v.scalar_tensor_tensor(tile(T, c), tile(X, c), st[:, XX, 9:10], bank(4 + c % 2), ALU.mult, ALU.add
                                           ).then_inc(mix_ready, 1)

                def columns(c):
                    dve.wait_ge(out_ready, b * NT + c + 1)
                    v.tensor_reduce(BS1[:, c % 2], tile(T, c).rearrange("p r (q w) -> p r q w", w=4), AX_X, ALU.add
                                    ).then_inc(columns_ready, 1)

                def blocks(c):
                    dve.wait_ge(columns_ready, b * NT + c + 1)
                    if c == 0:
                        dve.wait_ge(next_stored, b * 32 + 1)
                    v.tensor_reduce(BS[:, c, :], BS1[:, c % 2].rearrange("p r q -> p q r"), AX_X, ALU.add).then_inc(blocks_ready, 1)

                late = [(j, t) for j in range(NT - LATE, NT) for t in range(1, TAPS)]
                for s in range(NT * TAPS):
                    m, t = s // TAPS, s % TAPS
                    dve.wait_ge(fil_done, b * (NT * TAPS) + s + 1)
                    if s >= NS:
                        m8, t8 = (s - NS) // TAPS, (s - NS) % TAPS
                        dve.wait_ge(added, b * (NT * ADDS) + m8 * ADDS + max(t8, 1))
                    v.scalar_tensor_tensor(PROD[:, s % NS], bank(s % 4), b3m[:, t:t + 1], tile(Y, DEPTH[m], *t9[t]),
                                           ALU.add, ALU.mult).then_inc(prod_ready, 1)
                    if m >= 1 and t == 3:
                        leaky(m - 1)
                    if m >= 1 and t == 5:
                        filtered_low(m - 1)
                    c = m - BEHIND - 1
                    if c >= 0 and t == 4:
                        mix(c)
                    if c >= 1 and t == 2:
                        columns(c - 1)
                    if c >= 1 and t == 6:
                        blocks(c - 1)
                    if s >= TAPS and s % 2 and late:
                        depth(*late.pop(0))
                leaky(NT - 1)
                filtered_low(NT - 1)
                for c in range(NT - BEHIND - 1, NT):
                    mix(c)
                    columns(c - 1)
                    blocks(c - 1)
                columns(NT - 1)
                blocks(NT - 1)
                ch.done()

            squares_x(0)
            scale_shift(XX, 0)
            normalise(0)
            with dve.Fori(0, B - 1) as b:
                main(b)
                squares_x(b + 1)
                scale_shift(XX, b + 1)
                sum_t(b)
                negmean(b)
                normalise(b + 1)
                scale_shift(TT, b)
            main(B - 1)
            sum_t(B - 1)
            negmean(B - 1)
            scale_shift(TT, B - 1)



S1, S2 = 32, 16


def layer2_small(nc, B, pool2, norm2, y2, k):
    PRS = B // 2
    NWP = 6
    with phase(nc) as named, ExitStack() as ctx:
        def sb(name, shape, dt=F32):
            return ctx.enter_context(nc.sbuf_tensor("c_" + name, shape, dt))

        def sem(name):
            return named("c_" + name)

        BS = sb("BS", [128, PRS, 2, S1 // 2, S1])
        NORM = sb("NORM", [128, PRS, 2])
        SC16 = sb("SC16", [128, PRS])
        WTS = sb("WTS", [128, 12, TAPS, 128])
        bias = sb("bias", [128, 12])
        YP = sb("YP", [128, PRS, S1 + 2, S1 + 2])
        HP = sb("HP", [128, PRS, S1 + 2, S1 + 2])
        YQ = sb("YQ", [128, PRS, S2 + 2, S2 + 2])
        HQ = sb("HQ", [128, PRS, S2 + 2, S2 + 2])
        MX = sb("MX", [128, S1, S2])
        YE = sb("YE", [128, PRS, S2 + 2, S2])
        P = ctx.enter_context(nc.psum_tensor("c_P", [128, 8, 512], F32))
        const_loaded = sem("const_loaded")
        cleared = sem("cleared")
        weights_loaded = [sem("weights_loaded%d" % w) for w in range(NWP)]
        next_loaded = sem("next_loaded")
        chain_tail = sem("chain_tail")
        scale_ready = sem("scale_ready")
        pooled = sem("pooled")
        conv_done = sem("conv_done")
        hid_ev = sem("hid_ev")
        hid_ready = sem("hid_ready")
        res_ready = sem("res_ready")
        maxed = sem("maxed")
        y2_ready = sem("y2_ready")
        y2_stored = sem("y2_stored")
        block = ctx.enter_context(nc.Block())
        n_items = {1: PRS * 2, 2: (PRS + 1) // 2}
        steps = [(bl, la, cv, it) for bl in (1, 2) for la in range(3) for cv in (0, 1) for it in range(n_items[bl])]

        def src_dst(bl, cv, it):
            if bl == 1:
                pr, tile = it // 2, it % 2
                s = (YP, HP)[cv][:, pr]
                d = (HP, YP)[cv][:, pr, 1 + 16 * tile:17 + 16 * tile, 1:1 + S1]
                return (lambda dy, dx: s[:, 16 * tile + dy:16 * tile + dy + 16, dx:dx + S1]), d, 512
            p0, p1 = 2 * it, min(2 * it + 2, PRS)
            s, d = ((YQ, HQ) if cv == 0 else (HQ, YQ))
            return (lambda dy, dx: s[:, p0:p1, dy:dy + S2, dx:dx + S2]), d[:, p0:p1, 1:1 + S2, 1:1 + S2], 256 * (p1 - p0)

        def psum(s, n, bl):
            o = P[:, s % 8, 0:n]
            return o.rearrange("p (r w) -> p r w", w=S1) if bl == 1 else o.rearrange("p (a r w) -> p a r w", r=S2, w=S2)

        hid_before = [sum(1 for q in steps[:s] if q[2] == 0) for s in range(len(steps) + 1)]
        res_before = [sum(1 for q in steps[:s] if q[2] == 1) for s in range(len(steps) + 1)]

        @block.sync
        def _(sp):
            sp.dma_start(bias[:], k["bias2"]).then_inc(const_loaded, 16)
            for b in range(B):
                p = slice(64 * (b % 2), 64 * (b % 2) + 64)
                for h in range(2):
                    sp.dma_start(BS[p, b // 2, h].rearrange("p r q -> p (r q)"), pool2[b, 64 * h:64 * h + 64, :]).then_inc(next_loaded, 16)
                sp.dma_start(NORM[p, b // 2, :], norm2[b, 0:64, :]).then_inc(next_loaded, 16)
            sp.wait_ge(y2_ready, 1)
            for b in range(B):
                sp.dma_start(y2[b], YE[64 * (b % 2):64 * (b % 2) + 64, b // 2]).then_inc(y2_stored, 16)
            sp.wait_ge(y2_stored, 16 * B)

        @block.scalar
        def _(act):
            for w in range(NWP):
                act.wait_ge(cleared, w + 1)
                for h in range(2):
                    act.dma_start(WTS[64 * h:64 * h + 64, 2 * w:2 * w + 2, :, 64 * h:64 * h + 64].rearrange("p a t c -> p (a t) c"),
                                  k["blocks"][:, 2 * w * TAPS:(2 * w + 2) * TAPS]).then_inc(weights_loaded[w], 16)
            act.wait_ge(const_loaded, 16)
            for s, (bl, la, cv, it) in enumerate(steps):
                if cv == 0:
                    _, d, n = src_dst(bl, cv, it)
                    w = (bl - 1) * 6 + la * 2
                    act.wait_ge(conv_done, s + 1)
                    nc.scalar.activation(d, psum(s, n, bl), ACT.Identity, bias=bias[:, w:w + 1]).then_inc(hid_ev, 1)

        @block.tensor
        def _(pe):
            pe.wait_ge(pooled, PRS * 2)
            for s, (bl, la, cv, it) in enumerate(steps):
                f, _, n = src_dst(bl, cv, it)
                w = (bl - 1) * 6 + la * 2 + cv
                if s >= 8:
                    if steps[s - 8][2] == 0:
                        pe.wait_ge(hid_ev, hid_before[s - 7])
                    else:
                        pe.wait_ge(res_ready, res_before[s - 7])
                first = s - it
                if bl == 2 and la == 0 and cv == 0:
                    pe.wait_ge(maxed, 1)
                need = first - n_items[bl] + (it // 2 * 2 + 2 if bl == 1 else it + 1)
                if cv == 1:
                    pe.wait_ge(hid_ready, hid_before[need])
                elif la > 0:
                    pe.wait_ge(res_ready, res_before[need])
                if cv == it == 0:
                    pe.wait_ge(weights_loaded[w // 2], 32)
                for t in range(TAPS):
                    mm = nc.tensor.matmul(P[:, s % 8, 0:n], WTS[:, w, t, :], f(t // 3, t % 3), start=t == 0, stop=t == TAPS - 1)
                mm.then_inc(conv_done, 1)

        @block.vector
        def _(dve):
            v = nc.vector
            for w in range(NWP):
                v.memset(WTS[:, 2 * w:2 * w + 2, :, :], 0.0).then_inc(cleared, 1)
                if w == 0:
                    for t in (YP, HP, YQ, HQ):
                        v.memset(t[:, :, :, :], 0.0).then_inc(chain_tail, 1)
            dve.wait_ge(chain_tail, 4)
            dve.wait_ge(const_loaded, 16)
            dve.wait_ge(next_loaded, 48 * B)
            v.tensor_scalar(SC16[:, :], NORM[:, :, 0], 1.0 / 16, None, ALU.mult).then_inc(scale_ready, 1)
            dve.wait_ge(scale_ready, 1)
            for pr in range(PRS):
                for h in range(2):
                    v.tensor_scalar(YP[:, pr, 1 + 16 * h:17 + 16 * h, 1:1 + S1], BS[:, pr, h], SC16[:, pr:pr + 1], NORM[:, pr, 1:2],
                                    ALU.mult, ALU.add).then_inc(pooled, 1)
            for s, (bl, la, cv, it) in enumerate(steps):
                if bl == 2 and la == 0 and cv == 0 and it == 0:
                    dve.wait_ge(res_ready, res_before[s])
                    for pr in range(PRS):
                        yi = YP[:, pr, 1:1 + S1, 1:1 + S1]
                        v.tensor_tensor(MX[:, :, :], yi[:, :, 0:S1:2], yi[:, :, 1:S1:2], ALU.max).then_inc(chain_tail, 1)
                        dve.wait_ge(chain_tail, 4 + 2 * pr + 1)
                        v.tensor_tensor(YQ[:, pr, 1:1 + S2, 1:1 + S2], MX[:, 0:S1:2, :], MX[:, 1:S1:2, :], ALU.max
                                        ).then_inc(chain_tail, 1)
                        dve.wait_ge(chain_tail, 4 + 2 * pr + 2)
                    dve.sem_inc(maxed, 1)
                _, d, n = src_dst(bl, cv, it)
                if cv == 0:
                    dve.wait_ge(hid_ev, hid_before[s + 1])
                    items = [d] if bl == 1 else [d[:, q] for q in range(n // 256)]
                    for e in items:
                        ins = v.scalar_tensor_tensor(e, e, 0.1, e, ALU.mult, ALU.max)
                    ins.then_inc(hid_ready, 1)
                else:
                    w = (bl - 1) * 6 + la * 2 + 1
                    dve.wait_ge(conv_done, s + 1)
                    o = psum(s, n, bl)
                    items = [(d, o)] if bl == 1 else [(d[:, q], o[:, q]) for q in range(n // 256)]
                    for e, ps in items:
                        ins = v.scalar_tensor_tensor(e, ps, bias[:, w:w + 1], e, ALU.add, ALU.add)
                    ins.then_inc(res_ready, 1)
            dve.wait_ge(res_ready, res_before[-1])
            base = 4 + 2 * PRS
            v.tensor_copy(YE[:, :, 1:1 + S2, :], YQ[:, :, 1:1 + S2, 1:1 + S2]).then_inc(chain_tail, 1)
            v.tensor_copy(YE[:, :, 0, :], YQ[:, :, 1, 1:1 + S2]).then_inc(chain_tail, 1)
            v.tensor_copy(YE[:, :, S2 + 1, :], YQ[:, :, S2, 1:1 + S2]).then_inc(chain_tail, 1)
            dve.wait_ge(chain_tail, base + 3)
            dve.sem_inc(y2_ready, 1)


def layer2_apply(nc, B, x2, norm2, y2, x3, g3, k):
    NAP = S2 + 1
    BF16 = mybir.dt.bfloat16
    GROUPS = TapGroups((2, 2, 2, 2, 1))
    NS = 8
    NW = 4
    LAG = 5
    QT = 4
    NQ = NT // QT
    QR = QT * TR
    GACT = 16
    CUT = ((0, 5), (5, TAPS))
    with phase(nc) as named, ExitStack() as ctx:
        def sb(name, shape, dt=F32):
            return ctx.enter_context(nc.sbuf_tensor("d_" + name, shape, dt))

        def sem(name):
            return named("d_" + name)

        X = sb("X", [128, HR, W])
        G = sb("G", [128, PR, PW])
        T = sb("T", [128, HR, W])
        WT = sb("WT", [128, NAP // 2 + 1, TAPS, 2, C], BF16)
        U32 = sb("U32", [128, 2, 512])
        U = sb("U", [128, 2, 512], BF16)
        REST = sb("REST", [32, NW, TAPS, C])
        MID = sb("MID", [32, NW, TAPS, C], BF16)
        YE = sb("YE", [128, S2 + 2, S2])
        tok = sb("tok", [128, TAPS * C])
        ident = sb("ident", [128, 128])
        gsum = sb("gsum", [128, 128])
        st = sb("st", [128, 8])
        norm = sb("norm", [128, 2])
        ts = sb("ts", [128, NT])
        junk = sb("junk", [128, 2, TR, W])
        PROD = sb("PROD", [128, NS, TR, W])
        P = ctx.enter_context(nc.psum_tensor("d_P", [128, 8, 512], F32))
        const_loaded = sem("const_loaded")
        x_loaded = [sem("x_loaded%d" % q) for q in range(NQ)]
        y_loaded = sem("y_loaded")
        x3_stored = sem("x3_stored")
        g3_stored = sem("g3_stored")
        passed = sem("passed")
        norm_loaded = sem("norm_loaded")
        sum_ready = sem("sum_ready")
        mean_ready = sem("mean_ready")
        negmean_ready = sem("negmean_ready")
        sq_ready = sem("sq_ready")
        var_ready = sem("var_ready")
        vare_ready = sem("vare_ready")
        std_ready = sem("std_ready")
        inv_ready = sem("inv_ready")
        gnp_ready = sem("gnp_ready")
        gn_ready = sem("gn_ready")
        upper_ready = sem("upper_ready")
        lower_ready = sem("lower_ready")
        g_padded = sem("g_padded")
        wt_done = sem("wt_done")
        hi_ready = sem("hi_ready")
        rest_ready = sem("rest_ready")
        mid_ready = sem("mid_ready")
        mid_stacked = sem("mid_stacked")
        low_ready = sem("low_ready")
        init_done = sem("init_done")
        u_ready = sem("u_ready")
        fil_done = sem("fil_done")
        prod_ready = sem("prod_ready")
        prod_used = sem("prod_used")
        added = sem("added")
        acc_done = sem("acc_done")
        acc_ev = sem("acc_ev")
        ts_ready = sem("ts_ready")
        consts = [(ident[:], k["ident"]), (gsum[:], k["gsum"]), (tok[0:C], k["tok"]), (tok[C:C + 1], k["tokb"])]
        consts += [(U32[32 * part:32 * part + 32], k["U"]) for part in range(3)]
        block = ctx.enter_context(nc.Block())

        def inner(t):
            return t[:, 1:1 + HR, 1:1 + W]

        def tile(t, n, dy=0, dx=0):
            return t[:, TR * n + dy:TR * n + dy + TR, dx:dx + W]

        def bank(m):
            return P[:, m, :].rearrange("p (r w) -> p r w", r=TR)

        def halves(a):
            return [h for h in range(2) if h * 8 <= a <= h * 8 + 8]

        def filters(a, u):
            n0, n1 = CUT[u]
            return P[0:32, (2 * a + u) % 4, 0:(n1 - n0) * C].rearrange("p (t c) -> p t c", c=C)

        @block.sync
        def _(sp):
            sp.wait_ge(init_done, 5)
            for t, src in consts:
                sp.dma_start(t, src).then_inc(const_loaded, 16)

            def load_y(b):
                sp.dma_start(YE[0:C, :, :], y2[b]).then_inc(y_loaded, 16)

            def load(b, q):
                for h in range(2):
                    sp.dma_start(X[64 * h:64 * h + 64, QR * q:QR * q + QR], x2[b, :, HR * h + QR * q:HR * h + QR * q + QR, :]
                                 ).then_inc(x_loaded[q], 16)

            def store(b, q):
                sp.wait_ge(acc_ev, b * NT + QT * q + QT)
                for h in range(2):
                    sp.dma_start(x3[b, HR * h + QR * q:HR * h + QR * q + QR, :, :].rearrange("y c x -> c y x"),
                                 T[64 * h:64 * h + 64, QR * q:QR * q + QR]).then_inc(x3_stored, 16)

            def store_g(b):
                sp.wait_ge(upper_ready, b + 1)
                sp.wait_ge(lower_ready, b + 1)
                for h in range(2):
                    sp.dma_start(g3[b, HR * h:HR * h + HR, :, :].rearrange("y c x -> c y x"), T[64 * h:64 * h + 64]
                                 ).then_inc(g3_stored, 16)

            def load_norm(b):
                sp.dma_start(norm[:, :], norm2[b]).then_inc(norm_loaded, 16)

            load_norm(0)
            load_y(0)
            for q in range(NQ):
                load(0, q)
            with sp.Fori(0, B - 1) as b:
                sp.wait_ge(rest_ready, b * NAP + NAP)
                load_y(b + 1)
                sp.wait_ge(g_padded, b * 3 + 3)
                load_norm(b + 1)
                for q in range(NQ):
                    store(b, q)
                    load(b + 1, q)
                store_g(b)
            for q in range(NQ):
                store(B - 1, q)
            store_g(B - 1)
            sp.wait_ge(x3_stored, 32 * NQ * B)
            sp.wait_ge(g3_stored, 32 * B + 1)

        @block.scalar
        def _(act):
            def square(b):
                gate(act, negmean_ready, b + 1, passed)
                for m in range(2):
                    if m:
                        act.wait_ge(sq_ready, b * 2 + 1)
                    nc.scalar.activation(PROD[:, :, :, :].rearrange("p s r w -> p (s r) w"), T[:, HR // 2 * m:HR // 2 * (m + 1), :],
                                         ACT.Square, bias=st[:, 1:2], accum_out=st[:, 2 + 5 * m:3 + 5 * m]).then_inc(sq_ready, 1)
                act.wait_ge(vare_ready, b + 1)
                nc.scalar.activation(st[:, 4:5], st[:, 3:4], ACT.Sqrt).then_inc(std_ready, 1)

            def tail(b):
                square(b)
                gate(act, gnp_ready, b + 1, passed)
                gate(act, x3_stored, b * (32 * NQ) + 32 * NQ, passed)
                nc.scalar.activation(T[:, 0:GACT, :], T[:, 0:GACT, :], ACT.Identity, bias=st[:, 6:7], scale=st[:, 5:6]
                                     ).then_inc(upper_ready, 1)

            def head(b):
                def stack(a):
                    act.wait_ge(rest_ready, b * NAP + a + 1)
                    for h in halves(a):
                        ins = nc.scalar.activation(WT[32:64, a - 8 * h, :, h, :], REST[:, a % NW], ACT.Copy)
                    ins.then_inc(mid_stacked, 1)

                for a in range(NAP):
                    act.wait_ge(wt_done, b * NAP + a + 1)
                    for h in halves(a):
                        for u, (n0, n1) in enumerate(CUT):
                            ins = nc.scalar.activation(WT[0:32, a - 8 * h, n0:n1, h, :], filters(a, u), ACT.Copy)
                    ins.then_inc(hi_ready, 1)
                    if a >= 1:
                        stack(a - 1)
                stack(NAP - 1)

            def main(b):
                for n in range(NT):
                    act.wait_ge(acc_ev, b * NT + n + 1)
                    if n >= 2:
                        act.wait_ge(ts_ready, b * NT + n - 1)
                    nc.scalar.activation(junk[:, n % 2], tile(T, n), ACT.Copy, accum_out=ts[:, n:n + 1]).then_inc(ts_ready, 1)

            head(0)
            with act.Fori(0, B - 1) as b:
                main(b)
                tail(b)
                head(b + 1)
            main(B - 1)
            tail(B - 1)

        @block.tensor
        def _(pe):
            pe.wait_ge(const_loaded, 16 * len(consts))
            pe.wait_ge(u_ready, 1)

            def mean(b):
                gate(pe, sum_ready, b + 1, passed)
                nc.tensor.matmul(P[:, 7, 0:1], gsum[:, :], st[:, 0:1], start=True, stop=True).then_inc(mean_ready, 1)

            def variance(b):
                gate(pe, sq_ready, b * 2 + 2, passed)
                nc.tensor.matmul(P[:, 7, 1:2], gsum[:, :], st[:, 2:3], start=True, stop=False)
                nc.tensor.matmul(P[:, 7, 1:2], gsum[:, :], st[:, 7:8], start=False, stop=True).then_inc(var_ready, 1)

            def generate(b):
                gate(pe, y_loaded, b * 16 + 16, passed)
                for a in range(NAP):
                    if a >= 2:
                        gate(pe, rest_ready, b * NAP + a - 1, passed)
                    for u, (n0, n1) in enumerate(CUT):
                        mm = nc.tensor.matmul(P[0:32, (2 * a + u) % 4, 0:(n1 - n0) * C], YE[:, a:a + 2, :].rearrange("p a w -> p (a w)"),
                                              tok[:, n0 * C:n1 * C], start=True, stop=True)
                    mm.then_inc(wt_done, 1)

            def main(b):
                gate(pe, mid_stacked, b * NAP + NAP, passed)
                gate(pe, low_ready, b * NAP + NAP, passed)
                for s in range(NT * TAPS + LAG):
                    if s < NT * TAPS:
                        n, t = s // TAPS, s % TAPS
                        if s >= 4:
                            gate(pe, prod_ready, b * (NT * TAPS) + s - 3, passed)
                        nc.tensor.matmul(P[:, s % 4, :], WT[:, (n + 1) // 2, t].rearrange("p h c -> p (h c)"), U[:, n % 2, :],
                                         start=True, stop=True).then_inc(fil_done, 1)
                    n, t = (s - LAG) // TAPS, (s - LAG) % TAPS
                    if s < LAG or not GROUPS.is_last(t):
                        continue
                    g, f = GROUPS.group(t), GROUPS.first(t)
                    if f == t:
                        pe.wait_ge(prod_ready, b * (NT * TAPS) + s - LAG + 1)
                    else:
                        pe.wait_ge(added, b * (NT * GROUPS.adds) + n * GROUPS.adds + GROUPS.adds_to(t))
                    if g == 0 and n >= 2:
                        pe.wait_ge(acc_ev, b * NT + n - 1)
                    mm = nc.tensor.matmul(P[:, 4 + n % 2, :], ident[:, :], PROD[:, (n * TAPS + f) % NS],
                                          start=g == 0, stop=g == GROUPS.n - 1)
                    mm.then_inc(acc_done if g == GROUPS.n - 1 else prod_used, 1)

            generate(0)
            with pe.Fori(0, B - 1) as b:
                main(b)
                mean(b)
                variance(b)
                generate(b + 1)
            main(B - 1)
            mean(B - 1)
            variance(B - 1)

        @block.gpsimd
        def _(pool):
            def low(b):
                for a in range(NAP):
                    gate(pool, mid_ready, b * NAP + a + 1, passed)
                    for h in halves(a):
                        ins = nc.gpsimd.tensor_tensor(WT[64:96, a - 8 * h, :, h, :], REST[:, a % NW], MID[:, a % NW], ALU.subtract)
                    ins.then_inc(low_ready, 1)

            def main(b):
                for s in range(NT * TAPS):
                    n, t = s // TAPS, s % TAPS
                    f = n * TAPS + GROUPS.first(t)
                    if s == f:
                        continue
                    gate(pool, prod_ready, b * (NT * TAPS) + s + 1, passed)
                    nc.gpsimd.tensor_tensor(PROD[:, f % NS], PROD[:, f % NS], PROD[:, s % NS], ALU.add).then_inc(added, 1)

            low(0)
            with pool.Fori(0, B - 1) as b:
                main(b)
                low(b + 1)
            main(B - 1)

        @block.vector
        def _(dve):
            v = nc.vector
            v.memset(U32[:, :, :], 0.0).then_inc(init_done, 1)
            v.memset(WT[:, :, :, :, :], 0.0).then_inc(init_done, 1)
            v.memset(tok[:, :], 0.0).then_inc(init_done, 1)
            v.memset(YE[:, :, :], 0.0).then_inc(init_done, 1)
            dve.wait_ge(init_done, 4)
            v.memset(YE[C:C + 1, :, :], 1.0).then_inc(init_done, 1)
            dve.wait_ge(const_loaded, 16 * len(consts))
            v.tensor_copy(U[:, :, :], U32[:, :, :]).then_inc(u_ready, 1)
            dve.sem_inc(g3_stored, 1)

            def negmean(b):
                dve.wait_ge(mean_ready, b + 1)
                v.tensor_scalar(st[:, 1:2], P[:, 7, 0:1], -1.0, None, ALU.mult).then_inc(negmean_ready, 1)

            def scale_shift(b):
                dve.wait_ge(var_ready, b + 1)
                v.tensor_scalar(st[:, 3:4], P[:, 7, 1:2], GN_EPS, None, ALU.add).then_inc(vare_ready, 1)
                dve.wait_ge(std_ready, b + 1)
                v.reciprocal(st[:, 5:6], st[:, 4:5]).then_inc(inv_ready, 1)
                dve.wait_ge(inv_ready, b + 1)
                v.tensor_scalar(st[:, 6:7], st[:, 1:2], st[:, 5:6], None, ALU.mult).then_inc(gnp_ready, 1)

            def sum_t(b):
                dve.wait_ge(ts_ready, b * NT + NT)
                v.tensor_reduce(st[:, 0:1], ts[:, :], AX_X, ALU.add).then_inc(sum_ready, 1)

            def normalise_t(b):
                dve.wait_ge(gnp_ready, b + 1)
                dve.wait_ge(x3_stored, b * (32 * NQ) + 32 * NQ)
                v.tensor_scalar(T[:, GACT:HR, :], T[:, GACT:HR, :], st[:, 5:6], st[:, 6:7], ALU.mult, ALU.add
                                ).then_inc(lower_ready, 1)

            def normalise_x(b):
                dve.wait_ge(norm_loaded, b * 16 + 16)
                for q in range(NQ):
                    dve.wait_ge(x_loaded[q], b * 32 + 32)
                    v.tensor_scalar(G[:, 1 + QR * q:1 + QR * q + QR, 1:1 + W], X[:, QR * q:QR * q + QR, :], norm[:, 0:1],
                                    norm[:, 1:2], ALU.mult, ALU.add).then_inc(gn_ready, 1)

            def pad_x(b):
                dve.wait_ge(gn_ready, b * NQ + NQ)
                v.tensor_copy(G[:, 1:1 + HR, 0:1], G[:, 1:1 + HR, 1:2]).then_inc(g_padded, 1)
                v.tensor_copy(G[:, 1:1 + HR, PW - 1:PW], G[:, 1:1 + HR, PW - 2:PW - 1]).then_inc(g_padded, 1)
                dve.wait_ge(g_padded, b * 3 + 2)
                v.tensor_copy(G[0:64, 0, :], G[0:64, 1, :])
                v.tensor_copy(G[64:128, PR - 1, :], G[64:128, PR - 2, :])
                v.tensor_copy(G[0:64, PR - 1, :], G[64:128, 1, :])
                v.tensor_copy(G[64:128, 0, :], G[0:64, HR, :]).then_inc(g_padded, 1)

            def split(b):
                for a in range(NAP):
                    dve.wait_ge(hi_ready, b * NAP + a + 1)
                    if a >= NW:
                        dve.wait_ge(mid_stacked, b * NAP + a - NW + 1)
                        dve.wait_ge(low_ready, b * NAP + a - NW + 1)
                    h = halves(a)[0]
                    for u, (n0, n1) in enumerate(CUT):
                        ins = v.tensor_tensor(REST[:, a % NW, n0:n1], filters(a, u), WT[0:32, a - 8 * h, n0:n1, h, :], ALU.subtract)
                    ins.then_inc(rest_ready, 1)
                    dve.wait_ge(rest_ready, b * NAP + a + 1)
                    v.tensor_copy(MID[:, a % NW], REST[:, a % NW]).then_inc(mid_ready, 1)

            def main(b):
                dve.wait_ge(g_padded, b * 3 + 3)

                def total(n):
                    dve.wait_ge(acc_done, b * NT + n + 1)
                    if n == 0:
                        dve.wait_ge(g3_stored, b * 32 + 1)
                    v.tensor_tensor(tile(T, n), bank(4 + n % 2), tile(X, n), ALU.add).then_inc(acc_ev, 1)

                for s in range(NT * TAPS):
                    n, t = s // TAPS, s % TAPS
                    dve.wait_ge(fil_done, b * (NT * TAPS) + s + 1)
                    if s >= NS:
                        n8, t8 = (s - NS) // TAPS, (s - NS) % TAPS
                        if t8 != GROUPS.first(t8):
                            dve.wait_ge(added, b * (NT * GROUPS.adds) + n8 * GROUPS.adds + GROUPS.adds_to(t8))
                        elif GROUPS.group(t8) == GROUPS.n - 1:
                            dve.wait_ge(acc_done, b * NT + n8 + 1)
                        else:
                            dve.wait_ge(prod_used, b * (NT * (GROUPS.n - 1)) + n8 * (GROUPS.n - 1) + GROUPS.group(t8) + 1)
                    v.tensor_tensor(PROD[:, s % NS], bank(s % 4), tile(G, n, t // 3, t % 3), ALU.mult).then_inc(prod_ready, 1)
                    if t == 7 and n >= 1:
                        total(n - 1)
                total(NT - 1)

            normalise_x(0)
            pad_x(0)
            split(0)
            with dve.Fori(0, B - 1) as b:
                main(b)
                sum_t(b)
                negmean(b)
                normalise_x(b + 1)
                scale_shift(b)
                normalise_t(b)
                pad_x(b + 1)
                split(b + 1)
            main(B - 1)
            sum_t(B - 1)
            negmean(B - 1)
            scale_shift(B - 1)
            normalise_t(B - 1)



NM = 16
NF = 2 * NM
UP = 2.0 ** 30


def layer3_modes(nc, B, g3, modes, k):
    MB = 64
    NCH = NF * NM // MB
    H = NM // 2
    CG = C * W // 512
    COPIES = 5
    with phase(nc) as named, ExitStack() as ctx:
        def sb(name, shape, dt=F32):
            return ctx.enter_context(nc.sbuf_tensor("e_" + name, shape, dt))

        def sem(name):
            return named("e_" + name)

        GY = sb("GY", [128, 2, C, W])
        T1 = sb("T1", [128, 2, NF, C])
        XM = sb("XM", [128, NF * NM, B])
        WA = sb("WA", [128, 2, MB * C])
        WN = sb("WN", [128, 2, MB * C])
        OM = sb("OM", [C, NF, NM, B])
        OF = sb("OF", [NF, 2, C, NM])
        cas1 = sb("cas1", [128, W])
        ccol = sb("ccol", [128, 2, NM])
        sign = sb("sign", [128, 1])
        ident = sb("ident", [128, 128])
        P = ctx.enter_context(nc.psum_tensor("e_P", [128, 8, 512], F32))
        const_loaded = sem("const_loaded")
        g_loaded = [[sem("g_loaded%d%d" % (s, q)) for q in range(4)] for s in range(2)]
        w_loaded = [sem("w_loaded0"), sem("w_loaded1")]
        rows_done = sem("rows_done")
        rows_ev = sem("rows_ev")
        cols_done = sem("cols_done")
        cols_ev = sem("cols_ev")
        w_ready = sem("w_ready")
        mix_done = sem("mix_done")
        mix_ev = sem("mix_ev")
        turn_done = sem("turn_done")
        turn_ev = sem("turn_ev")
        modes_stored = [sem("modes_stored0"), sem("modes_stored1")]
        passed = sem("passed")
        consts = [(cas1, "cas1"), (ccol, "ccol"), (sign, "sign"), (ident, "ident")]
        block = ctx.enter_context(nc.Block())

        @block.sync
        def _(sp):
            for t, name in consts:
                sp.dma_start(t[:], k[name]).then_inc(const_loaded, 16)
            for b in range(B):
                for q in range(4):
                    if b >= 2:
                        sp.wait_ge(rows_done, (b - 2) * CG + (q + 1) * CG // 4)
                    sp.dma_start(GY[:, b % 2, 16 * q:16 * q + 16], g3[b, :, 16 * q:16 * q + 16]).then_inc(g_loaded[b % 2][q], 16)
            for b in range(B):
                sp.wait_ge(turn_ev, 2 * b + 2)
                sp.dma_start(modes[b], OF[:, b % 2].rearrange("p o g -> p (o g)")).then_inc(modes_stored[b % 2], 16)
            for n in range(2):
                sp.wait_ge(modes_stored[n], 16 * (B // 2))

        @block.gpsimd
        def _(pool):
            for n in range(NCH):
                if n >= 2:
                    pool.wait_ge(mix_done, n - 1)
                for t, name in ((WA, "w_at"), (WN, "w_neg")):
                    for h in range(2):
                        pool.dma_start(t[64 * h:64 * h + 64, n % 2, :], k[name][:, n * MB * C:(n + 1) * MB * C]
                                       ).then_inc(w_loaded[n % 2], 16)

        @block.tensor
        def _(pe):
            pe.wait_ge(const_loaded, 16 * len(consts))
            def rows(b):
                for q in range(CG):
                    n = b * CG + q
                    if q % (CG // 4) == 0:
                        pe.wait_ge(g_loaded[b % 2][q // (CG // 4)], 16 * (b // 2) + 16)
                    if n >= 4:
                        pe.wait_ge(rows_ev, n - 3)
                    for c in range(C // CG):
                        mm = nc.tensor.matmul(P[:, q % 4, W * c:W * c + W], GY[:, b % 2, q * (C // CG) + c, :], cas1[:, :],
                                              start=True, stop=True)
                    mm.then_inc(rows_done, 1)

            def columns(b):
                pe.wait_ge(rows_ev, CG * b + CG)
                if b >= 2:
                    pe.wait_ge(cols_ev, (b - 1) * COPIES)
                for j in range(NF // 2):
                    mm = nc.tensor.matmul(P[:, 4 + b % 2, 2 * NM * j:2 * NM * j + 2 * NM],
                                          T1[:, b % 2, 2 * j:2 * j + 2, :].rearrange("p f c -> p (f c)"),
                                          ccol[:, :, :].rearrange("p s g -> p (s g)"), start=True, stop=True)
                mm.then_inc(cols_done, 1)

            rows(0)
            for b in range(1, B):
                rows(b)
                columns(b - 1)
            columns(B - 1)
            pe.wait_ge(cols_ev, B * COPIES)
            for n in range(NCH):
                pe.wait_ge(w_ready, n + 1)
                if n >= 2:
                    pe.wait_ge(mix_ev, n - 1)
                for m in range(MB):
                    mm = nc.tensor.matmul(P[0:64, 6 + n % 2, B * m:B * m + B], WA[:, n % 2, C * m:C * m + C],
                                          XM[:, n * MB + m, :], start=True, stop=True)
                mm.then_inc(mix_done, 1)
            pe.wait_ge(mix_ev, NCH)
            for n in range(2 * B):
                if n >= 4:
                    pe.wait_ge(turn_ev, n - 3)
                for g in range(8):
                    mm = nc.tensor.transpose(P[0:NF, n % 4, C * g:C * g + C], OM[:, :, (n % 2) * 8 + g, n // 2], ident[0:C, 0:C])
                mm.then_inc(turn_done, 1)

        @block.scalar
        def _(act):
            for b in range(B):
                for q in range(CG):
                    act.wait_ge(rows_done, b * CG + q + 1)
                    if b >= 2:
                        act.wait_ge(cols_done, b - 1)
                    n = C // CG
                    nc.scalar.activation(T1[:, b % 2, :, n * q:n * q + n].rearrange("p (k f) c -> p c k f", k=2),
                                         P[:, q % 4, :].rearrange("p (c k f) -> p c k f", c=n, f=NM)[:, :, 0:W // NM:W // NM - 1],
                                         ACT.Copy).then_inc(rows_ev, 1)

        @block.vector
        def _(dve):
            v = nc.vector
            dve.wait_ge(const_loaded, 16 * len(consts))
            for b in range(B):
                dve.wait_ge(cols_done, b + 1)
                xm = XM[:, :, b].rearrange("p (k j e g) -> p k j e g", k=2, j=H, e=2)
                o = P[:, 4 + b % 2, :].rearrange("p (k j s g) -> p k j s g", k=2, j=H, s=2)
                for e in range(2):
                    v.tensor_copy(xm[0:64, :, :, e], o[64 * e:64 * e + 64, :, :, 0]).then_inc(cols_ev, 1)
                v.tensor_copy(xm[64:128, :, :, 1], o[64:128, :, ::-1, 1]).then_inc(cols_ev, 1)
                v.tensor_copy(xm[64:128, :, 0, 0], o[0:64, :, 0, 1]).then_inc(cols_ev, 1)
                v.tensor_copy(xm[64:128, :, 1:H, 0], o[0:64, :, H - 1:0:-1, 1]).then_inc(cols_ev, 1)
            for n in range(NCH):
                dve.wait_ge(w_loaded[n % 2], 64 * (n // 2) + 64)
                v.scalar_tensor_tensor(WA[:, n % 2], WN[:, n % 2], sign[:, 0:1], WA[:, n % 2], ALU.mult, ALU.add
                                       ).then_inc(w_ready, 1)
                if n >= 1:
                    dve.wait_ge(mix_done, n)
                    v.tensor_copy(OM[:, :, :, :].rearrange("p f g b -> p (f g b)")[:, MB * B * (n - 1):MB * B * n], P[0:64, 6 + (n - 1) % 2, 0:MB * B]
                                  ).then_inc(mix_ev, 1)
            dve.wait_ge(mix_done, NCH)
            v.tensor_copy(OM[:, :, :, :].rearrange("p f g b -> p (f g b)")[:, MB * B * (NCH - 1):], P[0:64, 6 + (NCH - 1) % 2, 0:MB * B]
                          ).then_inc(mix_ev, 1)
            for n in range(2 * B):
                dve.wait_ge(turn_done, n + 1)
                if n >= 4:
                    dve.wait_ge(modes_stored[n // 2 % 2], 16 * (n // 4))
                v.tensor_copy(OF[:, n // 2 % 2, :, (n % 2) * 8:(n % 2) * 8 + 8], P[0:NF, n % 4, :].rearrange("p (g o) -> p o g", o=C)
                              ).then_inc(turn_ev, 1)


def layer3_phase(nc, B, x3, g3, modes, out, k):
    CG = 4
    NG = C // CG
    NS = 4
    NQ = 4
    QG = NG // NQ
    QC = C // NQ
    with phase(nc) as named, ExitStack() as ctx:
        def sb(name, shape, dt=F32):
            return ctx.enter_context(nc.sbuf_tensor("f_" + name, shape, dt))

        def sem(name):
            return named("f_" + name)

        XY = sb("XY", [128, 2, C, W])
        GY = sb("GY", [128, 2, C, W])
        MO = sb("MO", [NF, 2, C * NM])
        T2 = sb("T2", [128, 2, CG, 2 * W])
        SC = sb("SC", [128, NS, CG * W])
        SS = sb("SS", [128, NS, CG * W])
        ZZ = sb("ZZ", [128, NS, CG * W])
        RT = sb("RT", [128, NS, CG * W])
        IV = sb("IV", [128, 2, 128])
        cas2 = sb("cas2", [128, 2 * W])
        casup = sb("casup", [128, 2 * W])
        cinv1 = sb("cinv1", [NF, W])
        cblk = sb("cblk", [128, 2, CG * W])
        P = ctx.enter_context(nc.psum_tensor("f_P", [128, 8, 512], F32))
        const_loaded = sem("const_loaded")
        g_loaded = [[sem("g_loaded%d%d" % (s, q)) for q in range(NQ)] for s in range(2)]
        x_loaded = [[sem("x_loaded%d%d" % (s, q)) for q in range(NQ)] for s in range(2)]
        m_loaded = [sem("m_loaded0"), sem("m_loaded1")]
        stored = [sem("stored%d" % q) for q in range(NQ)]
        passed = sem("passed")
        first_done = sem("first_done")
        first_ev = sem("first_ev")
        second_done = sem("second_done")
        inv1_done = sem("inv1_done")
        inv1_ev = sem("inv1_ev")
        inv2_done = sem("inv2_done")
        cos_sq = sem("cos_sq")
        sin_sq = sem("sin_sq")
        root_ready = sem("root_ready")
        squares_ready = sem("squares_ready")
        step = sem("step")
        cos_read = sem("cos_read")
        y_read = sem("y_read")
        slots_used = sem("slots_used")
        sums_ready = sem("sums_ready")
        inverse_ready = sem("inverse_ready")
        consts = [(cas2, "cas2"), (casup, "casup"), (cinv1, "cinv1"), (cblk, "cblk")]
        block = ctx.enter_context(nc.Block())
        PRS = B // 2

        @block.sync
        def _(sp):
            for t, name in consts:
                sp.dma_start(t[:], k[name]).then_inc(const_loaded, 16)

            def load(b, q):
                c = slice(QC * q, QC * q + QC)
                sp.dma_start(GY[:, b % 2, c], g3[b, :, c]).then_inc(g_loaded[b % 2][q], 16)
                sp.dma_start(XY[:, b % 2, c], x3[b, :, c]).then_inc(x_loaded[b % 2][q], 16)

            def load_modes(b):
                sp.dma_start(MO[:, b % 2], modes[b]).then_inc(m_loaded[b % 2], 16)

            for b in range(2):
                load(b, 0)
                load_modes(b)
                for q in range(1, NQ):
                    load(b, q)
            for b in range(B):
                for q in range(NQ):
                    sp.wait_ge(slots_used, b * NG + QG * q + QG + NS)
                    sp.dma_start(out[b, QC * q:QC * q + QC].rearrange("c y x -> y c x"), XY[:, b % 2, QC * q:QC * q + QC]
                                 ).then_inc(stored[q], 16)
                if b + 2 < B:
                    load_modes(b + 2)
                    for q in range(NQ):
                        sp.wait_ge(stored[q], 16 * b + 16)
                        load(b + 2, q)
            for q in range(NQ):
                sp.wait_ge(stored[q], 16 * B)

        @block.tensor
        def _(pe):
            pe.wait_ge(const_loaded, 16 * len(consts))
            with pe.Fori(0, PRS) as pr:
                for bb in range(2):
                    def first(i):
                        n = (pr * 2 + bb) * NG + i
                        if i % QG == 0:
                            gate(pe, g_loaded[bb][i // QG], pr * 16 + 16, passed)
                        gate(pe, first_ev, n + 1, passed)
                        for c in range(CG):
                            mm = nc.tensor.matmul(P[:, c // 2, (c % 2) * 256:(c % 2) * 256 + 256], GY[:, bb, i * CG + c, :],
                                                  cas2[:, :], start=True, stop=True)
                        mm.then_inc(first_done, 1)

                    def second(i):
                        n = (pr * 2 + bb) * NG + i
                        gate(pe, first_ev, n + 2, passed)
                        gate(pe, cos_read, n + 1, passed)
                        gate(pe, sin_sq, n + 1, passed)
                        for s in range(2):
                            for c in range(CG):
                                mm = nc.tensor.matmul(P[:, 2 + 2 * s + i % 2, c * W:c * W + W], T2[:, i % 2, c, s * W:s * W + W],
                                                      casup[:, s * W:s * W + W], start=True, stop=True)
                        mm.then_inc(second_done, 1)

                    def rows(i):
                        m = (pr * 2 + bb) * (NG // 2) + i // 2
                        gate(pe, inv1_ev, m + 1, passed)
                        nc.tensor.matmul(P[:, 7, 0:128], MO[:, bb, i // 2 * 128:i // 2 * 128 + 128], cinv1[:, :],
                                         start=True, stop=True).then_inc(inv1_done, 1)

                    def inverse(i):
                        n = (pr * 2 + bb) * NG + i
                        gate(pe, inv1_ev, (pr * 2 + bb) * (NG // 2) + i // 2 + 2, passed)
                        gate(pe, y_read, n + 1, passed)
                        nc.tensor.matmul(P[:, 6, :], IV[:, i // 2 % 2, :], cblk[:, i % 2, :], start=True, stop=True
                                         ).then_inc(inv2_done, 1)

                    gate(pe, m_loaded[bb], pr * 16 + 16, passed)
                    first(0)
                    for i in range(NG):
                        if i + 1 < NG:
                            first(i + 1)
                        second(i)
                        if i >= 1:
                            inverse(i - 1)
                        if i % 2 == 0:
                            rows(i)
                    inverse(NG - 1)

        @block.scalar
        def _(act):
            act.sem_inc(first_ev, 1)
            act.sem_inc(sin_sq, 2)
            with act.Fori(0, PRS) as pr:
                for bb in range(2):
                    def evict(i):
                        n = (pr * 2 + bb) * NG + i
                        act.wait_ge(first_done, n + 1)
                        nc.scalar.activation(T2[:, i % 2].rearrange("p c w -> p (c w)"), P[:, 0:2, :].rearrange("p a w -> p (a w)"),
                                             ACT.Copy).then_inc(first_ev, 1)

                    def root(i):
                        n = (pr * 2 + bb) * NG + i
                        act.wait_ge(squares_ready, n + 1)
                        nc.scalar.activation(RT[:, i % NS], SC[:, i % NS], ACT.Sqrt).then_inc(root_ready, 1)
                    evict(0)
                    for i in range(NG):
                        n = (pr * 2 + bb) * NG + i
                        if i + 1 < NG:
                            evict(i + 1)
                        act.wait_ge(second_done, n + 1)
                        act.wait_ge(slots_used, n + 1)
                        nc.scalar.activation(SC[:, i % NS], P[:, 2 + i % 2, :], ACT.Square).then_inc(cos_sq, 1)
                        nc.scalar.activation(SS[:, i % NS], P[:, 4 + i % 2, :], ACT.Square).then_inc(sin_sq, 1)
                        if i >= 1:
                            root(i - 1)
                    root(NG - 1)

        @block.vector
        def _(dve):
            v = nc.vector
            dve.sem_inc(inv1_ev, 1)
            dve.sem_inc(y_read, 1)
            dve.sem_inc(cos_read, 2)
            dve.sem_inc(slots_used, NS)
            with dve.Fori(0, PRS) as pr:
                for bb in range(2):
                    def squares(i):
                        n = (pr * 2 + bb) * NG + i
                        dve.wait_ge(sums_ready, n + 1)
                        v.scalar_tensor_tensor(SC[:, i % NS], SS[:, i % NS], 0.0, SS[:, i % NS], ALU.is_equal, ALU.add
                                               ).then_inc(squares_ready, 1)
                        v.scalar_tensor_tensor(ZZ[:, i % NS], SS[:, i % NS], 0.0, P[:, 2 + i % 2, :], ALU.is_equal, ALU.add
                                               ).then_inc(cos_read, 1)

                    def finish(i):
                        n = (pr * 2 + bb) * NG + i
                        dve.wait_ge(cos_read, n + 3)
                        dve.wait_ge(inv2_done, n + 1)
                        v.tensor_tensor(ZZ[:, i % NS], ZZ[:, i % NS], P[:, 6, :], ALU.mult).then_inc(y_read, 1)
                        dve.wait_ge(root_ready, n + 1)
                        v.reciprocal(RT[:, i % NS], RT[:, i % NS]).then_inc(inverse_ready, 1)

                    for i in range(NG):
                        squares(i)
                        if i % 2 == 0:
                            dve.wait_ge(inv1_done, (pr * 2 + bb) * (NG // 2) + i // 2 + 1)
                            v.tensor_copy(IV[:, i // 2 % 2, :], P[:, 7, 0:128]).then_inc(inv1_ev, 1)
                        if i >= 1:
                            finish(i - 1)
                    finish(NG - 1)

        @block.gpsimd
        def _(pool):
            with pool.Fori(0, PRS) as pr:
                for bb in range(2):
                    def add_squares(i):
                        n = (pr * 2 + bb) * NG + i
                        gate(pool, cos_sq, n + 1, passed)
                        gate(pool, sin_sq, n + 3, passed)
                        nc.gpsimd.tensor_tensor(SS[:, i % NS], SS[:, i % NS], SC[:, i % NS], ALU.add).then_inc(sums_ready, 1)

                    def add_to_x(i):
                        n = (pr * 2 + bb) * NG + i
                        x = XY[:, bb, CG * i:CG * i + CG, :].rearrange("p c w -> p (c w)")
                        if i % QG == 0:
                            gate(pool, x_loaded[bb][i // QG], pr * 16 + 16, passed)
                        gate(pool, y_read, n + 2, passed)
                        gate(pool, inverse_ready, n + 1, passed)
                        nc.gpsimd.tensor_tensor(ZZ[:, i % NS], ZZ[:, i % NS], RT[:, i % NS], ALU.mult).then_inc(step, 1)
                        gate(pool, step, n + 1, passed)
                        nc.gpsimd.tensor_tensor(x, x, ZZ[:, i % NS], ALU.add).then_inc(slots_used, 1)

                    for i in range(NG):
                        add_squares(i)
                        if i >= 2:
                            add_to_x(i - 2)
                    add_to_x(NG - 2)
                    add_to_x(NG - 1)


def cas(n):
    j = np.arange(n, dtype=np.float32)
    a = (np.float32(2.0 * np.pi) / np.float32(n) * (j[:, None] * j[None, :])).astype(np.float32)
    return (np.cos(a) + np.sin(a)).astype(np.float32)


def constants():
    f = np.float32
    k = {}
    part = np.arange(128)
    c = part % C
    k["iota"] = np.tile(np.arange(128, dtype=f), (128, 1))
    k["ident"] = np.eye(128, dtype=f)
    k["anti"] = np.eye(128, dtype=f)[::-1]
    k["gsum"] = (c[:, None] // 2 == c[None, :] // 2).astype(f) / f(2 * W * W)
    k["shift"] = np.stack([c[:, None] == c[None, :] + m - 1 for m in range(3)], 1).astype(f) / f(W * W)
    line = np.linspace(-1, 1, W, dtype=f) * f((W - 1) / 2)
    k["jc"] = np.stack([line, -line], 1)
    k["ic"] = np.tile(line[:HR], (128, 1))
    k["base"] = np.tile(np.linspace(0, 180, NA, dtype=f), (128, 1))
    pos = np.arange(W, dtype=f) * f((NA - 1) / (W - 1))
    k["ftab"] = np.tile((pos - np.minimum(np.floor(pos), NA - 2)).astype(f), (128, 1))
    src = (np.arange(W) + 0.5) / 8 - 0.5
    i0 = np.floor(src).astype(int)
    col = np.zeros((S2, W))
    for x in range(W):
        col[max(i0[x], 0), x] += 1 - (src[x] - i0[x])
        col[min(i0[x] + 1, S2 - 1), x] += src[x] - i0[x]
    u = np.zeros((2, S2, 2, TR, W))
    for odd in range(2):
        for r in range(TR):
            low = ((TR * odd + r + 0.5) / 8 - 0.5) % 1
            u[0, :, odd, r] = (1 - low) * col
            u[1, :, odd, r] = low * col
    k["U"] = u.reshape(32, 2, TR * W).astype(f)
    full = cas(W)
    kept = np.r_[0:NM, W - NM:W]
    g = np.arange(NM)
    k["cas1"] = full
    k["ccol"] = np.stack([full[:, g], full[:, (-g) % NM]], 1)
    k["sign"] = np.repeat(np.array([1, -1], f), C)[:, None]
    k["cas2"] = np.concatenate([full, full[::-1]], 1)
    k["casup"] = k["cas2"] * f(UP)
    k["cinv1"] = full[kept] * f(0.5 / (W * W))
    cb = np.zeros((8, NM, 2, 4, W), f)
    for o in range(8):
        cb[o, :, o // 4, o % 4, :] = full[:NM]
    k["cblk"] = cb.reshape(128, 2, 4 * W)
    return k


def layouts(a):
    k = {}
    twice = lambda v: np.tile(v, 2)
    k["lin1"] = a["L0_conv_lin1_w"].reshape(32, C, 2, 2, 4).transpose(2, 1, 3, 4, 0).reshape(128, 8, 32)
    k["lin2"] = a["L0_conv_lin2_w"].T
    k["lin1b"] = a["L0_conv_lin1_b"][:, None]
    k["lin2b"] = np.tile(a["L0_conv_lin2_b"], (128, 1))
    k["wf0"] = np.tile(a["L0_conv_wf0"].reshape(1, 3), (C, 1))
    k["wf1"] = np.tile(a["L0_conv_wf1"].reshape(1, 5), (C, 1))
    k["fuse"] = a["L0_conv_fuse_w"].reshape(C, C, 2).transpose(1, 2, 0)
    k["bn"] = np.stack([twice(a["L0_conv_" + n]) for n in ("bn_gamma", "bn_beta", "bn_mean", "bn_var", "fuse_b")], 1)
    k["w0"] = a["L1_conv_w0"].transpose(1, 2, 3, 0).reshape(C, TAPS, C)
    k["wf"] = a["L1_conv_wf"].transpose(1, 2, 3, 0).reshape(C, TAPS, C)
    k["w3"] = a["L1_conv_w3"].reshape(C, TAPS, C).transpose(2, 1, 0)
    k["w1"] = np.tile(a["L1_conv_w1"].reshape(C, TAPS), (2, 1))
    k["b3"] = np.tile(a["L1_conv_b3"].reshape(C, TAPS), (2, 1))
    k["w2"] = np.tile(a["L1_conv_w2"].reshape(1, 3), (128, 1))
    k["bias1"] = np.stack([twice(a["L1_conv_b0"]), twice(a["L1_conv_b1"]), np.tile(a["L1_conv_b2"], 128),
                           twice(a["L1_conv_bf"])], 1)
    convs = [(b, n, j) for b in ("blk1", "blk2") for n in range(3) for j in "12"]
    k["blocks"] = np.stack([a[f"L2_conv_{b}_w{j}"][n].transpose(1, 2, 3, 0).reshape(C, TAPS, C) for b, n, j in convs], 1
                           ).reshape(C, -1, C)
    k["bias2"] = np.stack([twice(a[f"L2_conv_{b}_b{j}"][n]) for b, n, j in convs], 1)
    k["tok"] = a["L2_conv_tok_w"].reshape(C, TAPS, C).transpose(2, 1, 0).reshape(C, TAPS * C)
    k["tokb"] = a["L2_conv_tok_b"].reshape(C, TAPS).T.reshape(1, TAPS * C)
    w = np.stack([a["L3_conv_weights1"], a["L3_conv_weights2"]])
    neg = (-np.arange(NM)) % NM
    k["w_at"] = w.transpose(1, 0, 3, 4, 2).reshape(C, -1)
    k["w_neg"] = w[:, :, :, neg][:, :, :, :, neg].transpose(1, 0, 3, 4, 2).reshape(C, -1)
    return k


def program(nc, x, out, k):
    B = x.shape[0]

    def scratch(name, shape):
        return nc.dram_tensor(name, shape, F32, kind="Internal").ap()

    x1 = scratch("x1_dram", (B, C, W, W))
    x2 = scratch("x2_dram", (B, C, W, W))
    stat1 = scratch("stat1_dram", (B, 128, 5))
    pool2 = scratch("pool2_dram", (B, 128, NT * W // 4))
    norm2 = scratch("norm2_dram", (B, 128, 2))
    y2 = scratch("y2_dram", (B, C, S2 + 2, S2))
    x3 = scratch("x3_dram", (B, W, C, W))
    g3 = scratch("g3_dram", (B, W, C, W))
    modes = scratch("modes_dram", (B, NF, C * NM))
    layer0(nc, B, x, x1, stat1, k)
    layer1(nc, B, x1, stat1, x2, pool2, norm2, k)
    layer2_small(nc, B, pool2, norm2, y2, k)
    layer2_apply(nc, B, x2, norm2, y2, x3, g3, k)
    layer3_modes(nc, B, g3, modes, k)
    layer3_phase(nc, B, x3, g3, modes, out, k)


def kernel(**inputs):
    import concourse.bacc as _bacc
    from concourse.bass_utils import run_bass_kernel_spmd as _run

    nc = _bacc.Bacc("TRN2", target_bir_lowering=False, num_devices=1)
    a = {name: np.ascontiguousarray(v) for name, v in inputs.items()}
    arrays = {"in_x_dram": a["x"]}
    for name, v in {**constants(), **layouts(a)}.items():
        arrays[f"in_{name}_dram"] = np.ascontiguousarray(v)
    aps = {name: nc.dram_tensor(name, v.shape, mybir.dt.from_np(v.dtype), kind="ExternalInput").ap()
           for name, v in arrays.items()}
    out = nc.dram_tensor("out_dram", a["x"].shape, F32, kind="ExternalOutput").ap()
    program(nc, aps["in_x_dram"], out, {name[3:-5]: ap for name, ap in aps.items() if name != "in_x_dram"})
    r = _run(nc, [arrays], core_ids=[0])
    return r.results[0]["out_dram"]
```
